# Optimizing a Trainium2 kernel written in Bass

```python
import numpy as np
import jax
import jax.numpy as jnp

def _softmax(x, axis=-1):
    return jax.nn.softmax(x, axis=axis)

def _gelu(x):
    return jax.nn.gelu(x, approximate=True)

def _silu(x):
    return jax.nn.silu(x)

def _sigmoid(x):
    return jax.nn.sigmoid(x)

def _layernorm(x, axis=-1, eps=1e-05):
    m = jnp.mean(x, axis=axis, keepdims=True)
    v = jnp.var(x, axis=axis, keepdims=True)
    return (x - m) / jnp.sqrt(v + eps)

def _scatter_add(tgt, idx, src, axis=0):
    return tgt.at[idx].add(src)

def _segment_sum(src, seg, n):
    return jax.ops.segment_sum(src, seg, n)
kernel_name = 'mk_gnn_preln_d2_gnn_r8_433759'

def setup_inputs(seed: int=0):
    np.random.seed(seed)
    _w = jnp.asarray

    def _rec_inputs():
        import jax
        import jax.numpy as jnp
        _gk = jax.random.key(seed)
        x = -0.000204 + 1 * jax.random.normal(jax.random.fold_in(_gk, 1), (6250, 128), jnp.float32)
        _s = jax.random.randint(jax.random.fold_in(_gk, 2), (50000,), 0, 6250, jnp.int32)
        _d = jax.random.randint(jax.random.fold_in(_gk, 3), (50000,), 0, 6250, jnp.int32)
        _loop = jnp.arange(6250, dtype=jnp.int32)
        src = jnp.concatenate([_s, _d, _loop])
        dst = jnp.concatenate([_d, _s, _loop])
        _o = jnp.argsort(dst, stable=True)
        src = src[_o]
        dst = dst[_o]
        edge_attr_64 = 0.000133148 + 1.00009 * jax.random.normal(jax.random.fold_in(_gk, 11), (106250, 64), jnp.float32)
        edge_weight = jax.random.uniform(jax.random.fold_in(_gk, 13), (106250,), jnp.float32, 0.0, 5)
        return (x, src, dst, edge_attr_64, edge_weight)
    x, src, dst, edge_attr_64, edge_weight = _rec_inputs()

    def _L0_gnn_setup():
        import jax, jax.numpy as jnp
        import numpy as np
        N_NODES = 6250

        def _gcn_conv(x, W, b, src, dst, n):
            x = x @ W
            loops = jnp.arange(n, dtype=src.dtype)
            src_f = jnp.concatenate([src, loops])
            dst_f = jnp.concatenate([dst, loops])
            deg = jax.ops.segment_sum(jnp.ones_like(dst_f, dtype=x.dtype), dst_f, num_segments=n)
            dinv = jnp.where(deg > 0, jax.lax.rsqrt(deg), 0.0)
            norm = dinv[src_f] * dinv[dst_f]
            msg = x[src_f] * norm[:, None]
            out = jax.ops.segment_sum(msg, dst_f, num_segments=n)
            return out + b
        key = jax.random.key(seed)
        k1, k2, k3, k4 = jax.random.split(key, 4)
        ninp = 128
        emb = jax.random.normal(k1, (N_NODES, ninp), dtype=jnp.float32)
        emb = emb.at[0].set(0.0)
        W1 = jax.random.normal(k2, (ninp, 2 * ninp), dtype=jnp.float32) * (1.0 / np.sqrt(ninp))
        b1 = jnp.zeros((2 * ninp,), dtype=jnp.float32)
        W2 = jax.random.normal(k3, (2 * ninp, ninp), dtype=jnp.float32) * (1.0 / np.sqrt(2 * ninp))
        b2 = jnp.zeros((ninp,), dtype=jnp.float32)
        edge_index = jax.random.randint(k4, (2, 100000), 0, N_NODES, dtype=jnp.int64)
        return {'emb': emb, 'W1': W1, 'b1': b1, 'W2': W2, 'b2': b2, 'edge_index': edge_index}
    _L0_gnn_all = _L0_gnn_setup()
    _L0_gnn_in = {k: v for k, v in _L0_gnn_all.items() if k in ('W1', 'b1', 'W2', 'b2')}
    del _L0_gnn_all

    def _L1_gnn_setup():
        import jax, jax.numpy as jnp
        import numpy as np
        N_NODES = 12500
        N_EDGES = 200000
        HIDDEN = 128
        NUM_RBF = 64
        NUM_FILTERS = 128
        CUTOFF_UPPER = 5.0

        def _xavier(key, fan_in, fan_out):
            limit = np.sqrt(6.0 / (fan_in + fan_out)).astype(np.float32)
            return jax.random.uniform(key, (fan_in, fan_out), jnp.float32, -limit, limit)
        key = jax.random.key(seed)
        ks = jax.random.split(key, 10)
        x = jax.random.normal(ks[0], (N_NODES, HIDDEN), jnp.float32)
        edge_index = jax.random.randint(ks[1], (2, N_EDGES), 0, N_NODES, jnp.int64)
        edge_weight = jax.random.uniform(ks[2], (N_EDGES,), jnp.float32) * CUTOFF_UPPER
        edge_attr = jax.random.normal(ks[3], (N_EDGES, NUM_RBF), jnp.float32)
        return {'x': x, 'edge_index': edge_index, 'edge_weight': edge_weight, 'edge_attr': edge_attr, 'mlp_w1': _xavier(ks[4], NUM_RBF, NUM_FILTERS), 'mlp_b1': jnp.zeros((NUM_FILTERS,), jnp.float32), 'mlp_w2': _xavier(ks[5], NUM_FILTERS, NUM_FILTERS), 'mlp_b2': jnp.zeros((NUM_FILTERS,), jnp.float32), 'lin1_w': _xavier(ks[6], HIDDEN, NUM_FILTERS), 'lin2_w': _xavier(ks[7], NUM_FILTERS, HIDDEN), 'lin2_b': jnp.zeros((HIDDEN,), jnp.float32), 'lin_w': _xavier(ks[8], HIDDEN, HIDDEN), 'lin_b': jnp.zeros((HIDDEN,), jnp.float32)}
    _L1_gnn_all = _L1_gnn_setup()
    _L1_gnn_in = {k: v for k, v in _L1_gnn_all.items() if k in ('mlp_w1', 'mlp_b1', 'mlp_w2', 'mlp_b2', 'lin1_w', 'lin2_w', 'lin2_b', 'lin_w', 'lin_b')}
    del _L1_gnn_all
    return {'x': x, 'src': src, 'dst': dst, 'edge_attr_64': edge_attr_64, 'edge_weight': edge_weight, 'L0_gnn_W1': _L0_gnn_in['W1'], 'L0_gnn_b1': _L0_gnn_in['b1'], 'L0_gnn_W2': _L0_gnn_in['W2'], 'L0_gnn_b2': _L0_gnn_in['b2'], 'L1_gnn_mlp_w1': _L1_gnn_in['mlp_w1'], 'L1_gnn_mlp_b1': _L1_gnn_in['mlp_b1'], 'L1_gnn_mlp_w2': _L1_gnn_in['mlp_w2'], 'L1_gnn_mlp_b2': _L1_gnn_in['mlp_b2'], 'L1_gnn_lin1_w': _L1_gnn_in['lin1_w'], 'L1_gnn_lin2_w': _L1_gnn_in['lin2_w'], 'L1_gnn_lin2_b': _L1_gnn_in['lin2_b'], 'L1_gnn_lin_w': _L1_gnn_in['lin_w'], 'L1_gnn_lin_b': _L1_gnn_in['lin_b']}

def reference(x, src, dst, edge_attr_64, edge_weight, L0_gnn_W1, L0_gnn_b1, L0_gnn_W2, L0_gnn_b2, L1_gnn_mlp_w1, L1_gnn_mlp_b1, L1_gnn_mlp_w2, L1_gnn_mlp_b2, L1_gnn_lin1_w, L1_gnn_lin2_w, L1_gnn_lin2_b, L1_gnn_lin_w, L1_gnn_lin_b):
    import jax
    import jax.numpy as jnp

    def _L0_gnn_ref(emb, W1, b1, W2, b2, edge_index):
        import jax, jax.numpy as jnp
        import numpy as np
        N_NODES = 6250

        def _gcn_conv(x, W, b, src, dst, n):
            x = x @ W
            loops = jnp.arange(n, dtype=src.dtype)
            src_f = jnp.concatenate([src, loops])
            dst_f = jnp.concatenate([dst, loops])
            deg = jax.ops.segment_sum(jnp.ones_like(dst_f, dtype=x.dtype), dst_f, num_segments=n)
            dinv = jnp.where(deg > 0, jax.lax.rsqrt(deg), 0.0)
            norm = dinv[src_f] * dinv[dst_f]
            msg = x[src_f] * norm[:, None]
            out = jax.ops.segment_sum(msg, dst_f, num_segments=n)
            return out + b
        src, dst = (edge_index[0], edge_index[1])
        h = _gcn_conv(emb, W1, b1, src, dst, N_NODES)
        out = _gcn_conv(h, W2, b2, src, dst, N_NODES)
        return out

    def _L1_gnn_ref(x, edge_index, edge_weight, edge_attr, mlp_w1, mlp_b1, mlp_w2, mlp_b2, lin1_w, lin2_w, lin2_b, lin_w, lin_b):
        import jax, jax.numpy as jnp
        import numpy as np
        N_NODES = 12500
        N_EDGES = 200000
        HIDDEN = 128
        NUM_RBF = 64
        NUM_FILTERS = 128
        CUTOFF_UPPER = 5.0

        def _xavier(key, fan_in, fan_out):
            limit = np.sqrt(6.0 / (fan_in + fan_out)).astype(np.float32)
            return jax.random.uniform(key, (fan_in, fan_out), jnp.float32, -limit, limit)
        n_nodes = x.shape[0]
        src, dst = (edge_index[0], edge_index[1])
        C = 0.5 * (jnp.cos(edge_weight * (jnp.pi / CUTOFF_UPPER)) + 1.0)
        C = C * (edge_weight < CUTOFF_UPPER).astype(x.dtype)
        h = jax.nn.silu(edge_attr @ mlp_w1 + mlp_b1)
        W = (h @ mlp_w2 + mlp_b2) * C[:, None]
        xf = x @ lin1_w
        msg = xf[src] * W
        agg_sum = jax.ops.segment_sum(msg, dst, num_segments=n_nodes)
        cnt = jax.ops.segment_sum(jnp.ones((msg.shape[0],), x.dtype), dst, num_segments=n_nodes)
        agg = agg_sum / jnp.maximum(cnt, 1.0)[:, None]
        out = agg @ lin2_w + lin2_b
        out = jax.nn.silu(out)
        out = out @ lin_w + lin_b
        return out
    edge_index = jnp.stack([src, dst])
    h = jnp.maximum(_layernorm(x, axis=-1), 0.0)
    x = x + _L0_gnn_ref(h, L0_gnn_W1, L0_gnn_b1, L0_gnn_W2, L0_gnn_b2, edge_index)
    h = jnp.maximum(_layernorm(x, axis=-1), 0.0)
    x = x + _L1_gnn_ref(h, edge_index, edge_weight, edge_attr_64, L1_gnn_mlp_w1, L1_gnn_mlp_b1, L1_gnn_mlp_w2, L1_gnn_mlp_b2, L1_gnn_lin1_w, L1_gnn_lin2_w, L1_gnn_lin2_b, L1_gnn_lin_w, L1_gnn_lin_b)
    return x

_drawn_inputs = setup_inputs


def setup_inputs(seed=0):
    import zlib

    import numpy as np

    out = dict(_drawn_inputs(seed))
    spreads = {'L0_gnn_b1': (0.0, 0.1),
     'L0_gnn_b2': (0.0, 0.1),
     'L1_gnn_mlp_b1': (0.0, 2.0),
     'L1_gnn_mlp_b2': (0.0, 2.0),
     'L1_gnn_lin2_b': (0.0, 0.1),
     'L1_gnn_lin_b': (0.0, 0.1)}
    factors = {'edge_weight': 4.024,
     'edge_attr_64': 4.923,
     'L1_gnn_mlp_w1': 4.963,
     'L1_gnn_mlp_w2': 2.843}
    for name, (base, spread) in spreads.items():
        noise = np.random.default_rng([zlib.crc32(name.encode()), seed]).standard_normal(out[name].shape)
        drawn = base * np.exp(spread * noise) if base else spread * noise
        out[name] = jnp.asarray(drawn.astype(out[name].dtype))
    for name, factor in factors.items():
        out[name] = (out[name] * factor).astype(out[name].dtype)
    return out
```

```python
from contextlib import ExitStack

import concourse.bass as bass
from concourse import mybir

F32 = mybir.dt.float32
BF16 = mybir.dt.bfloat16
I32 = mybir.dt.int32
ALU = mybir.AluOpType
ACT = mybir.ActivationFunctionType
AX_X = mybir.AxisListType.X

P = 128
CHUNKS = 4
GROUP = CHUNKS * P
WINDOW = 64
SLOTS = 4
LAG = 5
LN_EPS = 1e-5
CUTOFF = 5.0
NO_NODE = 20000
BATCH = SLOTS * CHUNKS
PARTS = 7
ROUND = 1.5 * 2.0 ** 23


def gnn_kernel(nc, x, src, dst, edge_attr, edge_weight, W1, b1, W2, b2,
               mlp_w1, mlp_b1, mlp_w2, mlp_b2, lin1_w, lin2_w, lin2_b, lin_w, lin_b, out):
    N, F = x.shape
    E, R = edge_attr.shape
    H = W1.shape[1]
    HM = H // P
    NG = -(-E // GROUP)
    HALF = NG // 2
    ITERS = NG // SLOTS
    NB = -(-N // P)
    LAST_ROWS = N - (NB - 1) * P
    NW = NB * P // WINDOW
    ACC = NB * P + WINDOW
    TAIL = E - (NG - 1) * GROUP
    assert F == P and NG == 2 * HALF == SLOTS * ITERS and NB % PARTS == 0 and ITERS % 2 == 0
    assert HALF <= P and H == HM * P and N < NO_NODE - ACC and N % P

    with ExitStack() as ctx:
        def sb(name, shape, dt=F32):
            return ctx.enter_context(nc.sbuf_tensor(name, shape, dt))

        def psum(name, shape):
            return ctx.enter_context(nc.psum_tensor(name, shape, F32))

        def sem(name):
            return ctx.enter_context(nc.semaphore(name))

        table = [None] + [nc.dram_tensor(f"node_table_{c}", [NB * P, F], F32, kind="Internal").ap()
                          for c in (1, 2, 3)]

        nodes = sb("nodes", [P, NB, F])
        z_nodes = sb("z_nodes", [P, NB, F])
        acc = sb("acc", [P, ACC])
        degree = sb("degree", [P, NB])
        dinv = sb("dinv", [P, NB])
        inv_count = sb("inv_count", [P, NB])
        dst_raw = sb("dst_raw", [HALF, 2, GROUP], I32)
        src_raw = sb("src_raw", [HALF, 2, GROUP], I32)
        src_f = sb("src_f", [HALF, 2, GROUP])
        dst_f = sb("dst_f", [HALF, 2, GROUP])
        rel_f = sb("rel_f", [HALF, 2, GROUP])
        weight_raw = sb("weight_raw", [HALF, 2, GROUP])
        dst_T = sb("dst_T", [P, NG * CHUNKS], I32)
        part_i = sb("part_i", [P, NG * CHUNKS], I32)
        dst_lo = sb("dst_lo", [P, NG * CHUNKS], BF16)
        dst_hi = sb("dst_hi", [P, NG * CHUNKS], BF16)
        iota_lo_i = sb("iota_lo_i", [P, P, BATCH], I32)
        iota_lo = sb("iota_lo", [P, P, BATCH], BF16)
        hist_lo = sb("hist_lo", [P, 2, P, BATCH], BF16)
        hist_hi = sb("hist_hi", [P, 2, NB, BATCH], BF16)
        base = sb("base", [HALF, 2])
        tests = sb("tests", [HALF, 4])
        group_id = sb("group_id", [HALF, 2], I32)
        earliest = sb("earliest", [HALF, 2])
        totals = sb("totals", [P, 4])
        fast = sb("fast", [P, 1])
        fast_i = sb("fast_i", [1, 1], I32)
        base_i = sb("base_i", [1, NG], I32)
        rel = sb("rel", [P, NG, CHUNKS])
        src_idx = sb("src_idx", [P, NG, CHUNKS], I32)
        cutoff = sb("cutoff", [P, NG, CHUNKS])
        angle = sb("angle", [P, NG, CHUNKS])
        turns = sb("turns", [P, NG, CHUNKS])
        idx_stage = sb("idx_stage", [P, SLOTS, CHUNKS], I32)
        ring = sb("ring", [P, SLOTS, CHUNKS, F])
        onehot = sb("onehot", [P, 2, CHUNKS, WINDOW])
        iota_i = sb("iota_i", [P, CHUNKS, WINDOW], I32)
        iota_f = sb("iota_f", [P, CHUNKS, WINDOW])
        iota_w = sb("iota_w", [P, CHUNKS, WINDOW])
        edge_in = sb("edge_in", [P, SLOTS, CHUNKS, R])
        edge_T = sb("edge_T", [R, 2, GROUP])
        hidden_T = sb("hidden_T", [P, 2, CHUNKS, P])
        z_T = sb("z_T", [P, P])
        h_T = sb("h_T", [P, HM, P])
        z_row = sb("z_row", [P, P])
        h2_T = sb("h2_T", [P, P])
        row_out = sb("row_out", [P, F])
        scale_diag = sb("scale_diag", [P, P])
        scale_all = sb("scale_all", [P, P])
        stats = sb("stats", [P, NB, 6])
        mean = sb("mean", [P, NB])
        var = sb("var", [P, NB])
        rstd = sb("rstd", [P, NB])
        tmp = sb("tmp", [P, NB])
        stats2 = sb("stats2", [P, 6])
        mv2 = sb("mv2", [P, 2])
        std2 = sb("std2", [P, 1])
        rstd2 = sb("rstd2", [P, 1])
        ident = sb("ident", [P, P])
        ones = sb("ones", [P, P])
        zeros = sb("zeros", [P, P])
        eps_col = sb("eps_col", [P, 1])
        half_pi = sb("half_pi", [P, 1])
        W1_sb = sb("W1_sb", [P, H])
        W2_sb = sb("W2_sb", [P, HM, F])
        b1_col = sb("b1_col", [P, HM])
        b2_all = sb("b2_all", [P, F])
        mlp_w1_sb = sb("mlp_w1_sb", [R, P])
        mlp_w2_sb = sb("mlp_w2_sb", [P, F])
        mlp_b1_col = sb("mlp_b1_col", [P, 1])
        mlp_b2_row = sb("mlp_b2_row", [1, CHUNKS, F])
        lin1_sb = sb("lin1_sb", [P, F])
        lin2_sb = sb("lin2_sb", [P, F])
        lin2_b_col = sb("lin2_b_col", [P, 1])
        lin_sb = sb("lin_sb", [P, F])
        lin_b_all = sb("lin_b_all", [P, F])

        ps_agg = psum("ps_agg", [P, 2, 512])
        ps_filter = psum("ps_filter", [P, 2, 512])
        ps_node = psum("ps_node", [P, 2, 512])
        ps_edge_T = psum("ps_edge_T", [P, 512])
        ps_hidden = psum("ps_hidden", [P, 512])

        padded = sem("padded")
        dst_loaded = sem("dst_loaded")
        src_loaded = sem("src_loaded")
        weight_loaded = sem("weight_loaded")
        x_loaded = sem("x_loaded")
        params_loaded = sem("params_loaded")
        pool_consts = sem("pool_consts")
        consts_ready = sem("consts_ready")
        tests_ready = sem("tests_ready")
        totals_ready = sem("totals_ready")
        rel_ready = sem("rel_ready")
        src_f_ready = sem("src_f_ready")
        flag_ready = sem("flag_ready")
        base_rows_ready = sem("base_rows_ready")
        rel_T_ready = sem("rel_T_ready")
        src_T_ready = sem("src_T_ready")
        weight_T_ready = sem("weight_T_ready")
        indices_ready = sem("indices_ready")
        angle_ready = sem("angle_ready")
        sin_ready = sem("sin_ready")
        var_ready = sem("var_ready")
        std_ready = sem("std_ready")
        norm_ready = sem("norm_ready")
        z_nodes_ready = sem("z_nodes_ready")
        dst_f_ready = sem("dst_f_ready")
        dst_T_ready = sem("dst_T_ready")
        dst_T_copied = sem("dst_T_copied")
        hist_iota = sem("hist_iota")
        hist_onehot = sem("hist_onehot")
        hist_summed = sem("hist_summed")
        degree_ready = sem("degree_ready")
        root_ready = sem("root_ready")
        table_ready = sem("table_ready")
        table_turned = sem("table_turned")
        start_ready = sem("start_ready")
        dve_chain = sem("dve_chain")
        act_chain = sem("act_chain")
        onehot_ready = [None] + [sem(f"onehot_ready_{c}") for c in (1, 2, 3)]
        summed = [None] + [sem(f"summed_{c}") for c in (1, 2, 3)]
        flushed = [None] + [sem(f"flushed_{c}") for c in (1, 2, 3)]
        staged = [None] + [sem(f"staged_{c}") for c in (1, 2, 3)]
        gathered = [None] + [[sem(f"gathered_{c}_{s}") for s in range(SLOTS)] for c in (1, 2, 3)]
        stored = [None] + [sem(f"stored_{c}") for c in (1, 2, 3)]
        edge_loaded = [sem(f"edge_loaded_{s}") for s in range(SLOTS)]
        edge_turned = sem("edge_turned")
        edge_T_ready = sem("edge_T_ready")
        hidden_done = sem("hidden_done")
        hidden_ready = sem("hidden_ready")
        filter_ready = sem("filter_ready")
        message_ready = sem("message_ready")
        z_ready = [None] + [sem(f"z_ready_{c}") for c in (1, 2, 3)]
        diag_ready = [None] + [sem(f"diag_ready_{c}") for c in (1, 2, 3)]
        scale_done = [None] + [sem(f"scale_done_{c}") for c in (1, 2, 3)]
        scale_ready = [None] + [sem(f"scale_ready_{c}") for c in (1, 2, 3)]
        h_done = sem("h_done")
        h_ready = sem("h_ready")
        y_done = sem("y_done")
        y_T_done = sem("y_T_done")
        acc_reset = [None] + [sem(f"acc_reset_{c}") for c in (1, 2)]
        row_ready = [None] + [sem(f"row_ready_{c}") for c in (1, 2, 3)]
        turned = sem("turned")
        var2_ready = sem("var2_ready")
        std2_ready = sem("std2_ready")
        rstd2_ready = sem("rstd2_ready")
        z_row_ready = sem("z_row_ready")
        z_turned = sem("z_turned")
        h2_ready = sem("h2_ready")
        xf_done = sem("xf_done")
        u_done = sem("u_done")
        u_ready = sem("u_ready")
        v_done = sem("v_done")
        v_added = sem("v_added")
        out_stored = sem("out_stored")
        z_summed = sem("z_summed")
        stats2_ready = sem("stats2_ready")
        held = sem("held")
        window_moved = [None] + [sem(f"window_moved_{c}") for c in (1, 2, 3)]

        def wait(eng, semaphore, count):
            if not (isinstance(count, int) and count <= 0):
                eng.wait_ge(semaphore, count)

        def hold(eng):
            eng.sem_inc(held, 1)

        def sweep(eng, body):
            body(0, None)
            with eng.Fori(1, LAG) as i:
                body(i, None)
            body(LAG, 0)
            with eng.Fori(LAG + 1, ITERS - 1) as i:
                body(i, i - LAG)
            body(ITERS - 1, ITERS - 1 - LAG)

        TAIL_BLOCKS = range(ITERS - LAG, NB)

        def all_blocks(eng, body):
            body(0)
            with eng.Fori(1, NB - 1) as j:
                body(j)
            body(NB - 1)

        def start_bank(q):
            return (ps_filter[:, 0, :], ps_filter[:, 1, :], ps_node[:, 0, :], ps_node[:, 1, :])[q % 4]

        def branch(eng, fast_path, general_path):
            eng.wait_ge(flag_ready, 1)
            flag = eng.value_load(fast_i[0:1, 0:1], min_val=0, max_val=1)
            with eng.If(flag > 0):
                fast_path()
            with eng.Else():
                general_path()

        block = ctx.enter_context(nc.Block())

        @block.sync
        def _(sp):
            def rows(v, lo, n):
                return v[lo * GROUP:(lo + n) * GROUP].rearrange("(g e) -> g e", e=GROUP)

            def one_row(v, lo, hi):
                return v[lo:hi].rearrange("(a e) -> a e", a=1)

            sp.dma_start(dst_raw[:, 0, :], rows(dst, 0, HALF)).then_inc(dst_loaded, 16)
            sp.wait_ge(padded, 1)
            sp.dma_start(dst_raw[0:HALF - 1, 1, :], rows(dst, HALF, HALF - 1)).then_inc(dst_loaded, 16)
            sp.dma_start(dst_raw[HALF - 1:HALF, 1, GROUP - TAIL:GROUP],
                         one_row(dst, E - TAIL, E)).then_inc(dst_loaded, 16)
            sp.dma_start(src_raw[:, 0, :], rows(src, 0, HALF)).then_inc(src_loaded, 16)
            sp.dma_start(src_raw[0:HALF - 1, 1, :], rows(src, HALF, HALF - 1)).then_inc(src_loaded, 16)
            sp.dma_start(src_raw[HALF - 1:HALF, 1, :], one_row(src, E - GROUP, E)).then_inc(src_loaded, 16)
            sp.dma_start(weight_raw[:, 0, :], rows(edge_weight, 0, HALF)).then_inc(weight_loaded, 16)
            sp.dma_start(weight_raw[0:HALF - 1, 1, :],
                         rows(edge_weight, HALF, HALF - 1)).then_inc(weight_loaded, 16)
            sp.dma_start(weight_raw[HALF - 1:HALF, 1, :],
                         one_row(edge_weight, E - GROUP, E)).then_inc(weight_loaded, 16)

            n = NB // PARTS
            for i in range(PARTS):
                sp.wait_ge(table_ready, i + 1)
                sp.dma_start(table[1][i * n * P:(i + 1) * n * P, :].rearrange("(b p) f -> p b f", p=P),
                             z_nodes[:, i * n:(i + 1) * n, :]).then_inc(stored[1], 16)

            def store_rows(c, j):
                wait(sp, row_ready[c], j + 1)
                sp.dma_start(table[c + 1][bass.ds(j * P, P), :], row_out[:]).then_inc(stored[c + 1], 16)

            def store_out(j):
                wait(sp, row_ready[3], j + 1)
                n = LAST_ROWS if isinstance(j, int) and j == NB - 1 else P
                sp.dma_start(out[bass.ds(j * P, n), :], row_out[0:n, :]).then_inc(out_stored, 16)

            def load_edges(i, s):
                g = SLOTS * i + s
                wait(sp, edge_turned, g - SLOTS + 1)
                first = min(g * GROUP, E - GROUP) if isinstance(g, int) else g * GROUP
                sp.dma_start(edge_in[:, s, :, :],
                             edge_attr[bass.ds(first, GROUP), :].rearrange("(p j) r -> p j r", j=CHUNKS)
                             ).then_inc(edge_loaded[s], 16)

            def fast_path():
                for c in (1, 2):
                    def body(i, j):
                        if j is not None:
                            store_rows(c, j)
                    sweep(sp, body)
                    for j in TAIL_BLOCKS:
                        store_rows(c, j)

                def body(i, j):
                    for s in range(SLOTS):
                        if s == 3 and j is not None and not (isinstance(j, int) and j == 0):
                            store_out(j - 1)
                        load_edges(i, s)
                sweep(sp, body)
                for j in range(ITERS - LAG - 1, NB):
                    store_out(j)

            def general_path():
                for c in (1, 2):
                    all_blocks(sp, lambda j: store_rows(c, j))

                def body(i, j):
                    for s in range(SLOTS):
                        load_edges(i, s)
                sweep(sp, body)
                all_blocks(sp, store_out)

            branch(sp, fast_path, general_path)
            sp.wait_ge(out_stored, 16 * NB)

        @block.gpsimd
        def _(pool):
            nc.gpsimd.iota(group_id[:], pattern=[[HALF, 2]], base=0, channel_multiplier=1)
            nc.gpsimd.iota(iota_i[:], pattern=[[0, CHUNKS], [1, WINDOW]], base=0,
                           channel_multiplier=0).then_inc(pool_consts, 1)
            nc.gpsimd.memset(ident[:], 0.0).then_inc(pool_consts, 1)
            pool.wait_ge(pool_consts, 2)
            nc.gpsimd.affine_select(out=ident[:], in_=ident[:], compare_op=ALU.not_equal, fill=1.0,
                                    base=0, pattern=[[-1, P]], channel_multiplier=1).then_inc(pool_consts, 1)

            nc.gpsimd.iota(iota_lo_i[:], pattern=[[1, P], [0, BATCH]], base=0,
                           channel_multiplier=0).then_inc(hist_iota, 1)
            pool.wait_ge(norm_ready, 1)
            nc.gpsimd.tensor_tensor(z_nodes[:], nodes[:], mean[:].unsqueeze(2).to_broadcast([P, NB, F]),
                                    ALU.subtract).then_inc(z_nodes_ready, 1)
            pool.wait_ge(z_nodes_ready, 1)
            nc.gpsimd.tensor_tensor(z_nodes[:], z_nodes[:], rstd[:].unsqueeze(2).to_broadcast([P, NB, F]),
                                    ALU.mult).then_inc(z_nodes_ready, 1)

            bound = pool.to_reg(NB * P - 1)

            def gather(c, i, s):
                wait(pool, staged[c], SLOTS * i + s + 1)
                hold(pool)
                for k in range(CHUNKS):
                    nc.gpsimd.indirect_dma_start(
                        ring[:, s, k, :], None, table[c],
                        bass.IndirectOffsetOnAxis(idx_stage[:, s, k:k + 1], 0),
                        bounds_check=bound, oob_is_err=False).then_inc(gathered[c][s], 16)

            def sweeps():
                for c in (1, 2, 3):
                    if c == 1:
                        pool.wait_ge(flag_ready, 1)
                    pool.wait_ge(stored[c], 16 * (PARTS if c == 1 else NB))

                    def body(i, j):
                        for s in range(SLOTS):
                            gather(c, i, s)
                    sweep(pool, body)

            sweeps()

        @block.scalar
        def _(act):
            def params(o, i, **kw):
                act.dma_start(o, i, **kw).then_inc(params_loaded, 16)

            def column(v, cols=1):
                return v.rearrange("(m p) -> p m", p=P)

            def row(v):
                return v.rearrange("(a f) -> a f", a=1)

            act.dma_start(nodes[:, 0:NB - 1, :],
                          x[0:(NB - 1) * P, :].rearrange("(b p) f -> p b f", p=P)).then_inc(x_loaded, 16)
            act.wait_ge(consts_ready, 1)
            act.dma_start(nodes[0:LAST_ROWS, NB - 1, :], x[(NB - 1) * P:N, :]).then_inc(x_loaded, 16)
            params(W1_sb[:], W1)
            params(W2_sb[:], W2.rearrange("(m p) f -> p m f", p=P))
            params(b1_col[:], column(b1), allow_slow_non_contiguous=True)
            params(b2_all[:], b2.partition_broadcast(P))
            params(mlp_w1_sb[:], mlp_w1)
            params(mlp_w2_sb[:], mlp_w2)
            params(mlp_b1_col[:], column(mlp_b1), allow_slow_non_contiguous=True)
            for k in range(CHUNKS):
                params(mlp_b2_row[:, k, :], row(mlp_b2))
            params(lin1_sb[:], lin1_w)
            params(lin2_sb[:], lin2_w)
            params(lin2_b_col[:], column(lin2_b), allow_slow_non_contiguous=True)
            params(lin_sb[:], lin_w)
            params(lin_b_all[:], lin_b.partition_broadcast(P))

            def halves(semaphore, ps, to):
                for t in range(2):
                    act.wait_ge(semaphore, t + 1)
                    last = nc.scalar.copy(
                        to[:, t * HALF:(t + 1) * HALF, :].rearrange("p g k -> p k g"),
                        ps[:, t, 0:CHUNKS * HALF].rearrange("p (k g) -> p k g", k=CHUNKS))
                return last

            halves(dst_T_ready, ps_agg, dst_T[:].rearrange("p (g k) -> p g k", k=CHUNKS)
                   ).then_inc(dst_T_copied, 1)
            act.wait_ge(hist_iota, 1)
            nc.scalar.copy(iota_lo[:], iota_lo_i[:]).then_inc(hist_iota, 1)
            halves(rel_T_ready, ps_filter, rel).then_inc(indices_ready, 1)
            halves(src_T_ready, ps_node, src_idx).then_inc(indices_ready, 1)
            halves(weight_T_ready, ps_agg, angle).then_inc(angle_ready, 1)
            act.wait_ge(var_ready, 1)
            nc.scalar.activation(rstd[:], var[:], ACT.Sqrt, bias=eps_col[:, 0:1]).then_inc(std_ready, 1)

            def scales(c, j):
                wait(act, scale_done[c], j + 1)
                nc.scalar.copy(scale_all[:], ps_node[:, 1, P:2 * P]).then_inc(scale_ready[c], 1)

            def node_1(j):
                scales(1, j)
                wait(act, y_done, j + 1)
                wait(act, stored[2], 16 * j)
                nc.scalar.copy(row_out[:], ps_node[:, 1, 0:F]).then_inc(row_ready[1], 1)

            def node_2(j, part):
                if part == 0:
                    wait(act, var2_ready, j + 1)
                    nc.scalar.activation(std2[:], mv2[:, 1:2], ACT.Sqrt, bias=eps_col[:, 0:1]
                                         ).then_inc(std2_ready, 1)
                if part == 1:
                    wait(act, z_turned, j + 1)
                    nc.scalar.activation(h2_T[:], ps_node[:, 1, 0:P], ACT.Relu).then_inc(h2_ready, 1)
                if part == 2:
                    wait(act, xf_done, j + 1)
                    wait(act, stored[3], 16 * j)
                    nc.scalar.copy(row_out[:], ps_node[:, 0, 0:F]).then_inc(row_ready[2], 1)

            def node_3(j):
                scales(3, j)
                wait(act, u_done, j + 1)
                nc.scalar.activation(z_row[:], ps_node[:, 0, 0:P], ACT.Silu, bias=lin2_b_col[:, 0:1]
                                     ).then_inc(u_ready, 1)

            def edge_copy(g, slot):
                wait(act, edge_turned, g + 1)
                nc.scalar.copy(edge_T[:, slot, :], ps_edge_T[0:R, :]).then_inc(edge_T_ready, 1)

            def edge_silu(g, slot):
                wait(act, filter_ready, g - 1)
                wait(act, hidden_done, g + 1)
                nc.scalar.activation(hidden_T[:, slot, :, :],
                                     ps_hidden[:, :].rearrange("p (k e) -> p k e", k=CHUNKS),
                                     ACT.Silu, bias=mlp_b1_col[:, 0:1]).then_inc(hidden_ready, 1)

            act.wait_ge(degree_ready, 1)
            nc.scalar.activation(dinv[:], degree[:], ACT.Sqrt).then_inc(root_ready, 1)
            for q in range(-(-NB // 4)):
                act.wait_ge(table_turned, q + 1)
                n = min(4, NB - 4 * q) * P
                nc.scalar.copy(acc[:, 4 * q * P:4 * q * P + n], start_bank(q)[:, 0:n]
                               ).then_inc(start_ready, 1)

            act.wait_ge(angle_ready, 2)
            nc.scalar.activation(angle[:], angle[:], ACT.Sin, bias=half_pi[:, 0:1],
                                 scale=-6.283185307179586).then_inc(sin_ready, 1)
            act.wait_ge(params_loaded, 16 * 16)

            def fast_path():
                def body(i, j):
                    if j is not None:
                        node_1(j)
                sweep(act, body)
                for j in TAIL_BLOCKS:
                    node_1(j)

                def body(i, j):
                    if j is not None:
                        for part in range(3):
                            node_2(j, part)
                sweep(act, body)
                for j in TAIL_BLOCKS:
                    for part in range(3):
                        node_2(j, part)

                edge_copy(0, 0)
                edge_copy(1, 1)
                edge_silu(0, 0)

                def body(i, j):
                    for s in range(SLOTS):
                        g = SLOTS * i + s
                        if not (isinstance(g, int) and g + 2 >= NG):
                            edge_copy(g + 2, s % 2)
                        if not (isinstance(g, int) and g + 1 >= NG):
                            edge_silu(g + 1, (s + 1) % 2)
                        if s == 1 and j is not None:
                            node_3(j)
                sweep(act, body)
                for j in TAIL_BLOCKS:
                    node_3(j)

            def general_path():
                all_blocks(act, node_1)

                def body(j):
                    for part in range(3):
                        node_2(j, part)
                all_blocks(act, body)

                def body(i, j):
                    for s in range(SLOTS):
                        g = SLOTS * i + s
                        edge_copy(g, s % 2)
                        edge_silu(g, s % 2)
                sweep(act, body)
                all_blocks(act, node_3)

            branch(act, fast_path, general_path)

        @block.vector
        def _(dve):
            chain = [0]

            def link(ins):
                chain[0] += 1
                ins.then_inc(dve_chain, 1)
                dve.wait_ge(dve_chain, chain[0])

            vec = nc.vector
            vec.memset(dst_raw[:, 1, :], NO_NODE).then_inc(padded, 1)
            vec.memset(nodes[:, NB - 1, :], 0.0).then_inc(consts_ready, 1)
            vec.memset(ones[:], 1.0)
            vec.memset(zeros[:], 0.0)
            vec.memset(eps_col[:], LN_EPS)
            vec.memset(half_pi[:], 1.5707963267948966)
            vec.memset(acc[:, NB * P:], 0.0)
            dve.wait_ge(pool_consts, 1)
            vec.tensor_copy(iota_f[:], iota_i[:]).then_inc(consts_ready, 1)
            link(vec.tensor_scalar(group_id[:], group_id[:], SLOTS.bit_length() - 1, P.bit_length() - 1,
                                   ALU.arith_shift_right, ALU.logical_shift_left))
            link(vec.tensor_scalar(earliest[:], group_id[:], float(-P * (LAG - 1)), None, ALU.add))

            dve.wait_ge(dst_loaded, 48)
            vec.tensor_copy(dst_f[:], dst_raw[:]).then_inc(dst_f_ready, 1)
            dve.wait_ge(dst_f_ready, 1)
            link(vec.tensor_reduce(base[:], dst_f[:], AX_X, ALU.min))
            for t in range(2):
                link(vec.tensor_scalar(rel_f[:, t, :], dst_f[:, t, :], base[:, t:t + 1], None, ALU.subtract))
                vec.tensor_scalar(rel_f[:, t, :], rel_f[:, t, :], float(WINDOW), 0.0, ALU.is_lt, ALU.add,
                                  accum_out=tests[:, t:t + 1])
            vec.tensor_tensor(tests[:, 2:4], base[:], earliest[:], ALU.is_ge).then_inc(tests_ready, 1)
            dve.wait_ge(src_loaded, 48)
            vec.tensor_copy(src_f[:], src_raw[:]).then_inc(src_f_ready, 1)
            dve.wait_ge(totals_ready, 1)
            link(vec.tensor_copy(totals[:], ps_edge_T[:, 0:4]))
            link(vec.tensor_tensor(totals[:, 0:1], totals[:, 0:1], totals[:, 1:2], ALU.add))
            link(vec.tensor_tensor(totals[:, 2:3], totals[:, 2:3], totals[:, 3:4], ALU.add))
            link(vec.tensor_scalar(totals[:, 1:2], totals[:, 0:1], float(E), None, ALU.is_equal))
            link(vec.tensor_scalar(fast[:], totals[:, 2:3], float(NG), totals[:, 1:2], ALU.is_equal, ALU.mult))
            vec.tensor_copy(fast_i[:], fast[0:1, :])
            link(vec.tensor_scalar(base[:], base[:], fast[0:HALF, 0:1], None, ALU.mult))
            for t in range(2):
                last = vec.tensor_scalar(rel_f[:, t, :], dst_f[:, t, :], base[:, t:t + 1], None, ALU.subtract)
            last.then_inc(rel_ready, 1)
            dve.wait_ge(base_rows_ready, 1)
            vec.tensor_copy(base_i[:], ps_hidden[0:1, 0:NG]).then_inc(flag_ready, 1)

            dve.wait_ge(dst_T_copied, 1)
            link(vec.tensor_scalar(part_i[:], dst_T[:], P - 1, None, ALU.bitwise_and))
            link(vec.tensor_copy(dst_lo[:], part_i[:]))
            link(vec.tensor_scalar(part_i[:], dst_T[:], P.bit_length() - 1, None, ALU.arith_shift_right))
            link(vec.tensor_copy(dst_hi[:], part_i[:]))

            dve.wait_ge(x_loaded, 32)
            for b in range(NB):
                last = vec.bn_stats(stats[:, b, :], nodes[:, b, :])
            link(last)
            me, mo, ve, vo = (stats[:, :, k] for k in (1, 4, 2, 5))
            link(vec.tensor_tensor(tmp[:], me, mo, ALU.subtract))
            link(vec.tensor_tensor(tmp[:], tmp[:], tmp[:], ALU.mult))
            link(vec.tensor_tensor(var[:], ve, vo, ALU.add))
            link(vec.tensor_scalar(tmp[:], tmp[:], 0.25, None, ALU.mult))
            link(vec.scalar_tensor_tensor(out=var[:], in0=var[:], scalar=1.0 / F, in1=tmp[:],
                                          op0=ALU.mult, op1=ALU.add))
            link(vec.tensor_tensor(mean[:], me, mo, ALU.add))
            vec.tensor_scalar(mean[:], mean[:], 0.5, None, ALU.mult).then_inc(var_ready, 1)
            dve.wait_ge(std_ready, 1)
            vec.reciprocal(rstd[:], rstd[:]).then_inc(norm_ready, 1)

            dve.wait_ge(hist_iota, 2)

            def hist_batch(b, slot):
                wait(dve, hist_summed, b - 1)
                for to, of, rows in ((hist_lo, dst_lo, P), (hist_hi, dst_hi, NB)):
                    last = vec.tensor_tensor(
                        to[:, slot, :, :], iota_lo[:, 0:rows, :],
                        of[:, bass.ds(b * BATCH, BATCH)].unsqueeze(1).to_broadcast([P, rows, BATCH]),
                        ALU.is_equal)
                last.then_inc(hist_onehot, 1)

            for slot in range(2):
                hist_batch(slot, slot)
            with dve.Fori(1, ITERS // 2) as i:
                for slot in range(2):
                    hist_batch(2 * i + slot, slot)

            dve.wait_ge(hist_summed, ITERS)
            link(vec.tensor_copy(inv_count[:], ps_hidden[:, 0:NB]))
            vec.tensor_scalar(degree[:], inv_count[:], 1.0, None, ALU.add).then_inc(degree_ready, 1)
            dve.wait_ge(root_ready, 1)
            link(vec.reciprocal(dinv[:], dinv[:]))
            dve.wait_ge(z_nodes_ready, 2)
            n = NB // PARTS
            for i in range(PARTS):
                zi = z_nodes[:, i * n:(i + 1) * n, :]
                vec.scalar_tensor_tensor(
                    out=zi, in0=zi, scalar=0.0,
                    in1=dinv[:, i * n:(i + 1) * n].unsqueeze(2).to_broadcast([P, n, F]),
                    op0=ALU.max, op1=ALU.mult).then_inc(table_ready, 1)
            link(vec.tensor_scalar(inv_count[:], inv_count[:], 1.0, None, ALU.max))
            link(vec.reciprocal(inv_count[:], inv_count[:]))
            dve.wait_ge(indices_ready, 2)

            def make_onehot(c, g, slot, iota):
                vec.tensor_tensor(onehot[:, slot, :, :], iota[:],
                                  rel[:, bass.ds(g, 1), :].rearrange("p a k -> p (a k)").unsqueeze(2)
                                  .to_broadcast([P, CHUNKS, WINDOW]),
                                  ALU.is_equal).then_inc(onehot_ready[c], 1)

            def flush(c, g, slot, at, before):
                wait(dve, flushed[c], before)
                wait(dve, summed[c], before + 1)
                to = acc[:, bass.ds(at, WINDOW)]
                vec.tensor_tensor(to, to, ps_agg[:, slot, 0:WINDOW], ALU.add).then_inc(flushed[c], 1)

            def stage(c, g, s):
                vec.tensor_copy(idx_stage[:, s, :].unsqueeze(1), src_idx[:, bass.ds(g, 1), :]
                                ).then_inc(staged[c], 1)

            def message(i, s):
                g = SLOTS * i + s
                wait(dve, gathered[3][s], 16 * CHUNKS * (i + 1))
                wait(dve, filter_ready, g + 1)
                for k in range(CHUNKS):
                    last = vec.scalar_tensor_tensor(
                        out=ring[:, s, k, :], in0=ps_filter[:, s % 2, k * P:(k + 1) * P],
                        scalar=cutoff[:].rearrange("p g k -> p (g k)")[:, bass.ds(g * CHUNKS + k, 1)],
                        in1=ring[:, s, k, :], op0=ALU.mult, op1=ALU.mult)
                last.then_inc(message_ready, 1)

            def fast_flush(c, g, s):
                at = dve.value_load(base_i[0:1, bass.ds(g, 1)], min_val=0, max_val=N - 1)
                flush(c, g, s % 2, at, g)

            def general_windows(c, g, s):
                wait(dve, window_moved[c], g * (NW + 1))
                vec.tensor_copy(iota_w[:], iota_f[:]).then_inc(window_moved[c], 1)
                with dve.Fori(0, NW) as w:
                    n = g * NW + w
                    dve.wait_ge(window_moved[c], n + g + 1)
                    make_onehot(c, g, s % 2, iota_w)
                    dve.wait_ge(summed[c], n + 1)
                    to = acc[:, bass.ds(w * WINDOW, WINDOW)]
                    vec.tensor_tensor(to, to, ps_agg[:, s % 2, 0:WINDOW], ALU.add).then_inc(flushed[c], 1)
                    vec.tensor_scalar(iota_w[:], iota_w[:], float(WINDOW), None, ALU.add
                                      ).then_inc(window_moved[c], 1)

            def columns(tile, j):
                return tile[:, bass.ds(j * P, P)]

            def diagonal(c, j):
                scale = inv_count if c == 3 else dinv
                vec.tensor_scalar(scale_diag[:], ident[:], scale[:, bass.ds(j, 1)], None, ALU.mult
                                  ).then_inc(diag_ready[c], 1)

            def node_1(j, part):
                if part == 0:
                    wait(dve, scale_ready[1], j + 1)
                    vec.tensor_tensor(z_T[:], columns(acc, j), scale_all[:], ALU.mult
                                      ).then_inc(z_ready[1], 1)
                if part == 1:
                    wait(dve, h_done, j + 1)
                    for m in range(HM):
                        last = vec.scalar_tensor_tensor(
                            out=h_T[:, m, :], in0=ps_node[:, 0, m * P:(m + 1) * P],
                            scalar=b1_col[:, m:m + 1], in1=scale_all[:], op0=ALU.add, op1=ALU.mult)
                    last.then_inc(h_ready, 1)
                if part == 2:
                    wait(dve, y_T_done, j + 1)
                    vec.tensor_scalar(columns(acc, j), ps_node[:, 0, 0:P], 1.0, None, ALU.mult
                                      ).then_inc(acc_reset[1], 1)

            def node_2(j, part):
                if part == 0:
                    vec.tensor_scalar(z_T[:], columns(acc, j), 1.0, None, ALU.mult
                                      ).then_inc(z_ready[2], 1)
                    wait(dve, z_ready[2], j + 1)
                    vec.tensor_scalar(columns(acc, j), zeros[:], 1.0, None, ALU.mult).then_inc(acc_reset[2], 1)
                if part == 1:
                    wait(dve, turned, j + 1)
                    xj = nodes[:, bass.ds(j, 1), :].rearrange("p a f -> p (a f)")
                    vec.scalar_tensor_tensor(out=z_row[:], in0=ps_node[:, 0, 0:F],
                                             scalar=dinv[:, bass.ds(j, 1)], in1=b2_all[:],
                                             op0=ALU.mult, op1=ALU.add).then_inc(z_summed, 1)
                    wait(dve, z_summed, 2 * j + 1)
                    vec.tensor_tensor(z_row[:], z_row[:], xj, ALU.add).then_inc(z_summed, 1)
                    wait(dve, z_summed, 2 * j + 2)
                    vec.tensor_scalar(xj, z_row[:], 1.0, None, ALU.mult)
                    vec.bn_stats(stats2[:], z_row[:]).then_inc(stats2_ready, 1)
                    wait(dve, stats2_ready, j + 1)
                    hold(dve)
                    vec.bn_aggr(mv2[:], stats2[:]).then_inc(var2_ready, 1)
                if part == 2:
                    wait(dve, std2_ready, j + 1)
                    vec.reciprocal(rstd2[:], std2[:]).then_inc(rstd2_ready, 1)
                    wait(dve, rstd2_ready, j + 1)
                    vec.tensor_scalar(z_row[:], z_row[:], mv2[:, 0:1], rstd2[:, 0:1],
                                      ALU.subtract, ALU.mult).then_inc(z_row_ready, 1)

            def node_3(j, part):
                if part == 0:
                    wait(dve, scale_ready[3], j + 1)
                    vec.tensor_tensor(z_T[:], columns(acc, j), scale_all[:], ALU.mult
                                      ).then_inc(z_ready[3], 1)
                if part == 1:
                    wait(dve, v_done, j + 1)
                    wait(dve, out_stored, 16 * j)
                    xj = nodes[:, bass.ds(j, 1), :].rearrange("p a f -> p (a f)")
                    vec.tensor_tensor(row_out[:], ps_node[:, 1, 0:F], lin_b_all[:], ALU.add
                                      ).then_inc(v_added, 1)
                    wait(dve, v_added, j + 1)
                    vec.tensor_tensor(row_out[:], row_out[:], xj, ALU.add).then_inc(row_ready[3], 1)

            def fast_path():
                for c in (1, 2):
                    if c == 2:
                        for s in range(SLOTS):
                            stage(c, s, s)
                    node = (node_1, node_2)[c - 1]

                    def body(i, j):
                        for s in range(SLOTS):
                            g = SLOTS * i + s
                            if j is not None and s == 0 and c == 1:
                                diagonal(c, j)
                            if j is not None and s == 2:
                                node(j, 1)
                            if j is not None and s == 3 and c == 2:
                                node(j, 2)
                            make_onehot(c, g, s % 2, iota_f)
                            fast_flush(c, g, s)
                            if not (isinstance(i, int) and i == ITERS - 1):
                                stage(c, g + SLOTS, s)
                            if j is not None and s == 0:
                                wait(dve, flushed[c], g + 1)
                                node(j, 0)
                            if j is not None and s == 3 and c == 1:
                                node(j, 2)
                    sweep(dve, body)
                    for j in TAIL_BLOCKS:
                        wait(dve, flushed[c], NG)
                        if c == 1:
                            diagonal(c, j)
                        for part in range(3):
                            node(j, part)
                    dve.wait_ge(acc_reset[c], NB)

                for s in range(SLOTS - 1):
                    stage(3, s, s)

                def body(i, j):
                    for s in range(SLOTS):
                        g = SLOTS * i + s
                        if j is not None and s == 0:
                            diagonal(3, j)
                        if j is not None and s == 3:
                            node_3(j, 1)
                        make_onehot(3, g, s % 2, iota_f)
                        message(i, s)
                        if not (isinstance(g, int) and g == 0):
                            fast_flush(3, g - 1, s - 1)
                        if not (isinstance(g, int) and g + SLOTS - 1 >= NG):
                            stage(3, g + SLOTS - 1, (s + SLOTS - 1) % SLOTS)
                        if j is not None and s == 0:
                            wait(dve, flushed[3], g)
                            node_3(j, 0)
                sweep(dve, body)
                fast_flush(3, NG - 1, SLOTS - 1)
                for j in TAIL_BLOCKS:
                    wait(dve, flushed[3], NG)
                    diagonal(3, j)
                    node_3(j, 0)
                    node_3(j, 1)

            def general_path():
                for c in (1, 2, 3):
                    if c != 1:
                        for s in range(SLOTS):
                            stage(c, s, s)

                    def body(i, j):
                        for s in range(SLOTS):
                            g = SLOTS * i + s
                            if c == 3:
                                message(i, s)
                            general_windows(c, g, s)
                            if not (isinstance(i, int) and i == ITERS - 1):
                                stage(c, g + SLOTS, s)
                    sweep(dve, body)
                    dve.wait_ge(flushed[c], NG * NW)

                    def body(j):
                        if c != 2:
                            diagonal(c, j)
                        for part in range(2 if c == 3 else 3):
                            (node_1, node_2, node_3)[c - 1](j, part)
                    all_blocks(dve, body)
                    if c < 3:
                        dve.wait_ge(acc_reset[c], NB)

            for s in range(SLOTS):
                stage(1, s, s)
            dve.wait_ge(angle_ready, 1)
            vec.tensor_scalar(cutoff[:], angle[:], CUTOFF, 0.5, ALU.is_lt, ALU.mult)
            link(vec.tensor_scalar(angle[:], angle[:], 0.5 / CUTOFF, None, ALU.mult))
            link(vec.tensor_scalar(turns[:], angle[:], ROUND, ROUND, ALU.add, ALU.subtract))
            link(vec.tensor_tensor(angle[:], angle[:], turns[:], ALU.subtract))
            vec.scalar_tensor_tensor(out=angle[:], in0=angle[:], scalar=-1.0, in1=angle[:],
                                     op0=ALU.mult, op1=ALU.max).then_inc(angle_ready, 1)
            dve.wait_ge(sin_ready, 1)
            link(vec.scalar_tensor_tensor(out=cutoff[:], in0=angle[:], scalar=1.0, in1=cutoff[:],
                                          op0=ALU.add, op1=ALU.mult))
            dve.wait_ge(params_loaded, 16 * 16)
            dve.wait_ge(start_ready, -(-NB // 4))
            branch(dve, fast_path, general_path)

        @block.tensor
        def _(pe):
            mm, turn = nc.tensor.matmul, nc.tensor.transpose

            pe.wait_ge(consts_ready, 2)
            pe.wait_ge(pool_consts, 3)

            def turn_indices(tile, ps, semaphore):
                for t in range(2):
                    for k in range(CHUNKS):
                        last = turn(ps[:, t, k * HALF:(k + 1) * HALF],
                                    tile[:, t, :].rearrange("g (p k) -> g k p", k=CHUNKS)[:, k, :],
                                    ident[0:HALF, 0:HALF])
                    last.then_inc(semaphore, 1)

            pe.wait_ge(dst_f_ready, 1)
            turn_indices(dst_f, ps_agg, dst_T_ready)
            pe.wait_ge(tests_ready, 1)
            mm(ps_edge_T[:, 0:4], ones[0:HALF, :], tests[:], start=True, stop=True).then_inc(totals_ready, 1)
            pe.wait_ge(rel_ready, 1)
            for t in range(2):
                last = mm(ps_hidden[0:1, t * HALF:(t + 1) * HALF], base[:, t:t + 1],
                          ident[0:HALF, 0:HALF], start=True, stop=True)
            last.then_inc(base_rows_ready, 1)
            turn_indices(rel_f, ps_filter, rel_T_ready)
            pe.wait_ge(src_f_ready, 1)
            turn_indices(src_f, ps_node, src_T_ready)
            pe.wait_ge(weight_loaded, 48)
            pe.wait_ge(dst_T_copied, 1)
            turn_indices(weight_raw, ps_agg, weight_T_ready)

            pe.wait_ge(flag_ready, 1)

            def hist_batch(b, slot, first, final):
                wait(pe, hist_onehot, b + 1)
                for k in range(BATCH):
                    last = mm(ps_hidden[:, 0:NB], hist_lo[:, slot, :, k], hist_hi[:, slot, :, k],
                              start=(first and k == 0), stop=(final and k == BATCH - 1),
                              skip_group_check=True)
                last.then_inc(hist_summed, 1)

            for slot in range(2):
                hist_batch(slot, slot, slot == 0, False)
            with pe.Fori(1, ITERS // 2 - 1) as i:
                for slot in range(2):
                    hist_batch(2 * i + slot, slot, False, False)
            for slot in range(2):
                hist_batch(ITERS - 2 + slot, slot, False, slot == 1)

            pe.wait_ge(indices_ready, 2)
            n = NB // PARTS
            for b in range(NB):
                if b % n == 0:
                    pe.wait_ge(table_ready, b // n + 1)
                q = b // 4
                if b % 4 == 0 and q >= 4:
                    pe.wait_ge(start_ready, q - 3)
                last = turn(start_bank(q)[:, b % 4 * P:(b % 4 + 1) * P], z_nodes[:, b, :], ident[:])
                if b % 4 == 3 or b == NB - 1:
                    last.then_inc(table_turned, 1)
            pe.wait_ge(start_ready, -(-NB // 4))
            pe.wait_ge(angle_ready, 1)
            pe.wait_ge(params_loaded, 16 * 16)

            def sum_window(c, n, s):
                wait(pe, onehot_ready[c], n + 1)
                for k in range(CHUNKS):
                    last = mm(ps_agg[:, s % 2, 0:WINDOW], ring[:, s, k, :],
                              onehot[:, s % 2, k, :], start=(k == 0), stop=(k == CHUNKS - 1))
                last.then_inc(summed[c], 1)

            def edge_turn(g, s, i):
                wait(pe, edge_loaded[s], 16 * (i + 1))
                wait(pe, edge_T_ready, g)
                hold(pe)
                for k in range(CHUNKS):
                    last = turn(ps_edge_T[0:R, k * P:(k + 1) * P], edge_in[:, s, k, :], ident[:])
                last.then_inc(edge_turned, 1)

            def edge_hidden(g, slot):
                wait(pe, hidden_ready, g)
                wait(pe, edge_T_ready, g + 1)
                mm(ps_hidden[:, :], mlp_w1_sb[:], edge_T[:, slot, :], start=True, stop=True
                   ).then_inc(hidden_done, 1)

            def edge_filter(g, slot):
                wait(pe, message_ready, g - 1)
                mm(ps_filter[:, slot, :], ones[0:1, :], mlp_b2_row[:].rearrange("a k f -> a (k f)"),
                   start=True, stop=False)
                wait(pe, hidden_ready, g + 1)
                for k in range(CHUNKS):
                    last = mm(ps_filter[:, slot, k * P:(k + 1) * P], hidden_T[:, slot, k, :],
                              mlp_w2_sb[:], start=False, stop=(k == CHUNKS - 1))
                last.then_inc(filter_ready, 1)

            def scales(c, j):
                wait(pe, diag_ready[c], j + 1)
                wait(pe, row_ready[c], j)
                mm(ps_node[:, 1, P:2 * P], ones[:], scale_diag[:], start=True, stop=True
                   ).then_inc(scale_done[c], 1)

            def node_1(j, part):
                if part == 0:
                    wait(pe, z_ready[1], j + 1)
                    for m in range(HM):
                        last = mm(ps_node[:, 0, m * P:(m + 1) * P], W1_sb[:, m * P:(m + 1) * P], z_T[:],
                                  start=True, stop=True)
                    last.then_inc(h_done, 1)
                if part == 1:
                    wait(pe, h_ready, j + 1)
                    wait(pe, row_ready[1], j)
                    for m in range(HM):
                        last = mm(ps_node[:, 1, 0:F], h_T[:, m, :], W2_sb[:, m, :],
                                  start=(m == 0), stop=(m == HM - 1))
                    last.then_inc(y_done, 1)
                    for m in range(HM):
                        last = mm(ps_node[:, 0, 0:P], W2_sb[:, m, :], h_T[:, m, :],
                                  start=(m == 0), stop=(m == HM - 1))
                    last.then_inc(y_T_done, 1)

            def node_2(j, part):
                if part == 0:
                    wait(pe, z_ready[2], j + 1)
                    wait(pe, row_ready[2], j)
                    turn(ps_node[:, 0, 0:P], z_T[:], ident[:]).then_inc(turned, 1)
                if part == 1:
                    wait(pe, z_row_ready, j + 1)
                    turn(ps_node[:, 1, 0:P], z_row[:], ident[:]).then_inc(z_turned, 1)
                if part == 2:
                    wait(pe, h2_ready, j + 1)
                    mm(ps_node[:, 0, 0:F], h2_T[:], lin1_sb[:], start=True, stop=True).then_inc(xf_done, 1)

            def node_3(j, part):
                if part == 0:
                    wait(pe, z_ready[3], j + 1)
                    mm(ps_node[:, 0, 0:P], lin2_sb[:], z_T[:], start=True, stop=True).then_inc(u_done, 1)
                if part == 1:
                    wait(pe, u_ready, j + 1)
                    wait(pe, row_ready[3], j)
                    mm(ps_node[:, 1, 0:F], z_row[:], lin_sb[:], start=True, stop=True).then_inc(v_done, 1)

            def fast_path():
                for c in (1, 2):
                    def body(i, j):
                        for s in range(SLOTS):
                            g = SLOTS * i + s
                            if j is not None and s == 3 and c == 1:
                                node_1(j, 1)
                            wait(pe, gathered[c][s], 16 * CHUNKS * (i + 1))
                            wait(pe, flushed[c], g - 1)
                            sum_window(c, g, s)
                            if j is not None and s == 0 and c == 1:
                                scales(c, j)
                            if j is not None and s == 1:
                                (node_1, node_2)[c - 1](j, 0)
                            if j is not None and s == 3 and c == 2:
                                node_2(j, 1)
                                node_2(j, 2)
                    sweep(pe, body)
                    for j in TAIL_BLOCKS:
                        if c == 1:
                            scales(c, j)
                        for part in range(c + 1):
                            (node_1, node_2)[c - 1](j, part)

                edge_turn(0, 0, 0)
                edge_turn(1, 1, 0)
                edge_hidden(0, 0)

                def body(i, j):
                    for s in range(SLOTS):
                        g = SLOTS * i + s
                        if not (isinstance(g, int) and g + 2 >= NG):
                            edge_turn(g + 2, (s + 2) % SLOTS, i + (s + 2) // SLOTS)
                        if not (isinstance(g, int) and g + 1 >= NG):
                            edge_hidden(g + 1, (s + 1) % 2)
                        edge_filter(g, s % 2)
                        if not (isinstance(g, int) and g == 0):
                            wait(pe, message_ready, g)
                            wait(pe, flushed[3], g - 2)
                            sum_window(3, g - 1, (s - 1) % SLOTS)
                        if j is not None and s == 0:
                            scales(3, j)
                        if j is not None and s in (1, 2):
                            node_3(j, s - 1)
                sweep(pe, body)
                wait(pe, message_ready, NG)
                wait(pe, flushed[3], NG - 2)
                sum_window(3, NG - 1, SLOTS - 1)
                for j in TAIL_BLOCKS:
                    scales(3, j)
                    node_3(j, 0)
                    node_3(j, 1)

            def general_windows(c, g, s):
                with pe.Fori(0, NW) as w:
                    sum_window(c, g * NW + w, s)

            def general_path():
                for c in (1, 2, 3):
                    def body(i, j):
                        for s in range(SLOTS):
                            g = SLOTS * i + s
                            if c == 3:
                                edge_turn(g, s, i)
                                edge_hidden(g, s % 2)
                                edge_filter(g, s % 2)
                                wait(pe, message_ready, g + 1)
                            else:
                                wait(pe, gathered[c][s], 16 * CHUNKS * (i + 1))
                            hold(pe)
                            general_windows(c, g, s)
                    sweep(pe, body)

                    def body(j):
                        if c != 2:
                            scales(c, j)
                        for part in range((2, 3, 2)[c - 1]):
                            (node_1, node_2, node_3)[c - 1](j, part)
                    all_blocks(pe, body)

            branch(pe, fast_path, general_path)


_INS = ['x', 'src', 'dst', 'edge_attr_64', 'edge_weight', 'L0_gnn_W1', 'L0_gnn_b1', 'L0_gnn_W2', 'L0_gnn_b2',
        'L1_gnn_mlp_w1', 'L1_gnn_mlp_b1', 'L1_gnn_mlp_w2', 'L1_gnn_mlp_b2', 'L1_gnn_lin1_w', 'L1_gnn_lin2_w',
        'L1_gnn_lin2_b', 'L1_gnn_lin_w', 'L1_gnn_lin_b']


def kernel(**inputs):
    import numpy as _np
    import concourse.bacc as _bacc
    from concourse import mybir as _mybir
    from concourse.bass_utils import run_bass_kernel_spmd as _run

    nc = _bacc.Bacc("TRN2", target_bir_lowering=False, num_devices=1)
    arrays, args = {}, []
    for name in _INS:
        a = _np.ascontiguousarray(inputs[name])
        arrays[f"in_{name}_dram"] = a
        args.append(nc.dram_tensor(f"in_{name}_dram", a.shape, _mybir.dt.from_np(a.dtype), kind="ExternalInput").ap())
    shape = tuple(inputs['x'].shape)
    args.append(nc.dram_tensor("out_dram", shape, _mybir.dt.float32, kind="ExternalOutput").ap())
    gnn_kernel(nc, *args)
    r = _run(nc, [arrays], core_ids=[0])
    return r.results[0]["out_dram"]
```

```python
from contextlib import ExitStack

import concourse.bass as bass
from concourse import mybir

F32 = mybir.dt.float32
BF16 = mybir.dt.bfloat16
I32 = mybir.dt.int32
ALU = mybir.AluOpType
ACT = mybir.ActivationFunctionType
AX_X = mybir.AxisListType.X

P = 128
CHUNKS = 4
GROUP = CHUNKS * P
WINDOW = 64
SLOTS = 4
LAG = 5
LN_EPS = 1e-5
CUTOFF = 5.0
NO_NODE = 20000
BATCH = SLOTS * CHUNKS
PARTS = 7
DENSE_ITERS = 6
EXTRA = 5
SPAN = 16
PRODUCTS = 3
CODE_ONE = 0x3F80
ROUND = 1.5 * 2.0 ** 23


def gnn_kernel(nc, x, src, dst, edge_attr, edge_weight, W1, b1, W2, b2,
               mlp_w1, mlp_b1, mlp_w2, mlp_b2, lin1_w, lin2_w, lin2_b, lin_w, lin_b, out):
    N, F = x.shape
    E, R = edge_attr.shape
    H = W1.shape[1]
    HM = H // P
    NG = -(-E // GROUP)
    HALF = NG // 2
    ITERS = NG // SLOTS
    NB = -(-N // P)
    LAST_ROWS = N - (NB - 1) * P
    NW = NB * P // WINDOW
    ACC = NB * P + WINDOW
    GCN_ITERS = ITERS - DENSE_ITERS
    DENSE = DENSE_ITERS * BATCH
    BUILD_ITERS = DENSE // SLOTS
    DENSE_EDGES = E - GCN_ITERS * SLOTS * GROUP
    DENSE_FULL = DENSE_EDGES // P
    DENSE_REST = DENSE_EDGES - DENSE_FULL * P
    COLS = (EXTRA + 1) * P
    ORIGIN = NB * P - COLS
    HI_SPLIT = -(-NB // 2)
    TAIL = E - (NG - 1) * GROUP
    assert F == P and NG == 2 * HALF == SLOTS * ITERS and NB % PARTS == 0 and ITERS % 2 == 0
    FIRST_PRODUCT = BUILD_ITERS + 1
    FIRST_EXTRA = GCN_ITERS - EXTRA
    assert DENSE_REST and DENSE_FULL + 1 <= DENSE <= HALF and N - 1 + SPAN <= NB * P
    assert LAG < BUILD_ITERS and FIRST_PRODUCT + NB // PRODUCTS == FIRST_EXTRA
    assert NB % PRODUCTS == 1
    assert HALF <= P and H == HM * P and N < NO_NODE - ACC and N % P

    with ExitStack() as ctx:
        def sb(name, shape, dt=F32):
            return ctx.enter_context(nc.sbuf_tensor(name, shape, dt))

        def psum(name, shape):
            return ctx.enter_context(nc.psum_tensor(name, shape, F32))

        def sem(name):
            return ctx.enter_context(nc.semaphore(name))

        table = [None] + [nc.dram_tensor(f"node_table_{c}", [NB * P, F], F32, kind="Internal").ap()
                          for c in (1, 2, 3)]

        early = ExitStack()

        def sb_early(name, shape, dt=F32):
            return early.enter_context(nc.sbuf_tensor(name, shape, dt))

        z_nodes = sb_early("z_nodes", [P, NB, F])
        turns = sb_early("turns", [P, NG, CHUNKS])
        code_iota_i = sb_early("code_iota_i", [P, NB * SPAN], I32)
        hist_lo = sb_early("hist_lo", [P, 2, P, BATCH], BF16)
        hist_hi = sb_early("hist_hi", [P, 2, NB, BATCH], BF16)
        iota_lo = sb_early("iota_lo", [P, P, BATCH], BF16)
        iota_lo_i = sb_early("iota_lo_i", [P, P, BATCH], I32)
        dst_lo = sb_early("dst_lo", [P, NG * CHUNKS], BF16)
        dst_hi = sb_early("dst_hi", [P, NG * CHUNKS], BF16)
        dst_T = sb_early("dst_T", [P, NG * CHUNKS], I32)
        part_i = sb_early("part_i", [P, NG * CHUNKS], I32)
        stats = sb_early("stats", [P, NB, 6])
        mean = sb_early("mean", [P, NB])
        var = sb_early("var", [P, NB])
        rstd = sb_early("rstd", [P, NB])
        tmp = sb_early("tmp", [P, NB])
        weight_raw = sb_early("weight_raw", [HALF, 2, GROUP])
        rel_f = sb_early("rel_f", [HALF, 2, GROUP])
        src_f = sb_early("src_f", [HALF, 2, GROUP])
        dst_f = sb_early("dst_f", [HALF, 2, GROUP])
        src_raw = sb_early("src_raw", [HALF, 2, GROUP], I32)
        dst_raw = sb_early("dst_raw", [HALF, 2, GROUP], I32)
        dense_dst = sb_early("dense_dst", [DENSE, P], I32)
        dense_src = sb_early("dense_src", [DENSE, P], I32)
        dense_part = sb_early("dense_part", [DENSE, P], I32)
        dense_dst_f = sb_early("dense_dst_f", [DENSE, P])
        dense_rel = sb_early("dense_rel", [DENSE, P])
        dense_lo = sb_early("dense_lo", [DENSE, P])
        dense_hi = sb_early("dense_hi", [DENSE, P])
        dense_code = sb_early("dense_code", [DENSE, P])
        early.close()
        adjacency = sb("adjacency", [P, NB, COLS], BF16)
        edge_in = sb("edge_in", [P, SLOTS, CHUNKS, R])
        edge_T = sb("edge_T", [R, 2, GROUP])
        hidden_T = sb("hidden_T", [P, 2, CHUNKS, P])
        h_T = sb("h_T", [P, HM, P])
        table_in = sb("table_in", [P, PRODUCTS, F])
        table_rest = sb("table_rest", [P, F])
        table_parts = sb("table_parts", [P, PRODUCTS, 3, F], BF16)
        lo_onehot = sb("lo_onehot", [P, 2, P], BF16)
        code_onehot = sb("code_onehot", [P, 2, NB * SPAN], BF16)
        nodes = sb("nodes", [P, NB, F])
        acc = sb("acc", [P, ACC])
        degree = sb("degree", [P, NB])
        dinv = sb("dinv", [P, NB])
        inv_count = sb("inv_count", [P, NB])
        base = sb("base", [HALF, 2])
        tests = sb("tests", [HALF, 8])
        group_id = sb("group_id", [HALF, 2], I32)
        earliest = sb("earliest", [HALF, 2])
        totals = sb("totals", [P, 1])
        fast = sb("fast", [P, 1])
        fast_i = sb("fast_i", [1, 1], I32)
        base_i = sb("base_i", [1, NG], I32)
        rel = sb("rel", [P, NG, CHUNKS])
        src_idx = sb("src_idx", [P, NG, CHUNKS], I32)
        cutoff = sb("cutoff", [P, NG, CHUNKS])
        angle = sb("angle", [P, NG, CHUNKS])
        chunk_base = sb("chunk_base", [DENSE, 1])
        chunk_at = sb("chunk_at", [1, DENSE], I32)
        lo_T = sb("lo_T", [P, DENSE])
        code_T = sb("code_T", [P, DENSE], I32)
        lo_iota = sb("lo_iota", [P, P], BF16)
        code_iota = sb("code_iota", [P, NB * SPAN], BF16)
        idx_stage = sb("idx_stage", [P, SLOTS, CHUNKS], I32)
        ring = sb("ring", [P, SLOTS, CHUNKS, F])
        onehot = sb("onehot", [P, 2, CHUNKS, WINDOW])
        iota_i = sb("iota_i", [P, CHUNKS, WINDOW], I32)
        iota_f = sb("iota_f", [P, CHUNKS, WINDOW])
        iota_w = sb("iota_w", [P, CHUNKS, WINDOW])
        z_T = sb("z_T", [P, P])
        z_row = sb("z_row", [P, P])
        h2_T = sb("h2_T", [P, P])
        row_out = sb("row_out", [P, F])
        scale_diag = sb("scale_diag", [P, P])
        scale_all = sb("scale_all", [P, P])
        stats2 = sb("stats2", [P, 6])
        mv2 = sb("mv2", [P, 2])
        std2 = sb("std2", [P, 1])
        rstd2 = sb("rstd2", [P, 1])
        ident = sb("ident", [P, P])
        ones = sb("ones", [P, P])
        zeros = sb("zeros", [P, P])
        eps_col = sb("eps_col", [P, 1])
        half_pi = sb("half_pi", [P, 1])
        W1_sb = sb("W1_sb", [P, H])
        W2_sb = sb("W2_sb", [P, HM, F])
        b1_col = sb("b1_col", [P, HM])
        b2_all = sb("b2_all", [P, F])
        mlp_w1_sb = sb("mlp_w1_sb", [R, P])
        mlp_w2_sb = sb("mlp_w2_sb", [P, F])
        mlp_b1_col = sb("mlp_b1_col", [P, 1])
        mlp_b2_row = sb("mlp_b2_row", [1, CHUNKS, F])
        lin1_sb = sb("lin1_sb", [P, F])
        lin2_sb = sb("lin2_sb", [P, F])
        lin2_b_col = sb("lin2_b_col", [P, 1])
        lin_sb = sb("lin_sb", [P, F])
        lin_b_all = sb("lin_b_all", [P, F])

        ps_agg = psum("ps_agg", [P, 2, 512])
        ps_filter = psum("ps_filter", [P, 2, 512])
        ps_node = psum("ps_node", [P, 2, 512])
        ps_edge_T = psum("ps_edge_T", [P, 512])
        ps_hidden = psum("ps_hidden", [P, 512])

        padded = sem("padded")
        dst_loaded = sem("dst_loaded")
        dense_loaded = sem("dense_loaded")
        dense_ready = sem("dense_ready")
        dense_T_ready = sem("dense_T_ready")
        src_loaded = sem("src_loaded")
        weight_loaded = sem("weight_loaded")
        x_loaded = sem("x_loaded")
        params_loaded = sem("params_loaded")
        pool_consts = sem("pool_consts")
        consts_ready = sem("consts_ready")
        tests_ready = sem("tests_ready")
        totals_ready = sem("totals_ready")
        rel_ready = sem("rel_ready")
        src_f_ready = sem("src_f_ready")
        flag_ready = sem("flag_ready")
        base_rows_ready = sem("base_rows_ready")
        rel_T_ready = sem("rel_T_ready")
        src_T_ready = sem("src_T_ready")
        weight_T_ready = sem("weight_T_ready")
        indices_ready = sem("indices_ready")
        angle_ready = sem("angle_ready")
        sin_ready = sem("sin_ready")
        var_ready = sem("var_ready")
        std_ready = sem("std_ready")
        norm_ready = sem("norm_ready")
        z_nodes_ready = sem("z_nodes_ready")
        dst_f_ready = sem("dst_f_ready")
        dst_T_ready = sem("dst_T_ready")
        dst_T_copied = sem("dst_T_copied")
        hist_iota = sem("hist_iota")
        hist_onehot = sem("hist_onehot")
        hist_summed = sem("hist_summed")
        degree_ready = sem("degree_ready")
        root_ready = sem("root_ready")
        table_ready = sem("table_ready")
        table_turned = sem("table_turned")
        start_ready = sem("start_ready")
        dve_chain = sem("dve_chain")
        act_chain = sem("act_chain")
        chunk_onehot = sem("chunk_onehot")
        chunk_summed = sem("chunk_summed")
        chunk_added = sem("chunk_added")
        block_loaded = [None] + [[sem(f"block_loaded_{c}_{s}") for s in range(PRODUCTS)] for c in (1, 2)]
        parts_ready = [None] + [sem(f"parts_ready_{c}") for c in (1, 2)]
        block_used = [None] + [sem(f"block_used_{c}") for c in (1, 2)]
        dense_added = [None] + [sem(f"dense_added_{c}") for c in (1, 2)]
        onehot_ready = [None] + [sem(f"onehot_ready_{c}") for c in (1, 2, 3)]
        summed = [None] + [sem(f"summed_{c}") for c in (1, 2, 3)]
        flushed = [None] + [sem(f"flushed_{c}") for c in (1, 2, 3)]
        staged = [None] + [sem(f"staged_{c}") for c in (1, 2, 3)]
        gathered = [None] + [[sem(f"gathered_{c}_{s}") for s in range(SLOTS)] for c in (1, 2, 3)]
        stored = [None] + [sem(f"stored_{c}") for c in (1, 2, 3)]
        edge_loaded = [sem(f"edge_loaded_{s}") for s in range(SLOTS)]
        edge_turned = sem("edge_turned")
        edge_T_ready = sem("edge_T_ready")
        hidden_done = sem("hidden_done")
        hidden_ready = sem("hidden_ready")
        filter_ready = sem("filter_ready")
        message_ready = sem("message_ready")
        z_ready = [None] + [sem(f"z_ready_{c}") for c in (1, 2, 3)]
        diag_ready = [None] + [sem(f"diag_ready_{c}") for c in (1, 2, 3)]
        scale_done = [None] + [sem(f"scale_done_{c}") for c in (1, 2, 3)]
        scale_ready = [None] + [sem(f"scale_ready_{c}") for c in (1, 2, 3)]
        h_done = sem("h_done")
        h_ready = sem("h_ready")
        y_done = sem("y_done")
        y_T_done = sem("y_T_done")
        acc_reset = [None] + [sem(f"acc_reset_{c}") for c in (1, 2)]
        row_ready = [None] + [sem(f"row_ready_{c}") for c in (1, 2, 3)]
        turned = sem("turned")
        var2_ready = sem("var2_ready")
        std2_ready = sem("std2_ready")
        rstd2_ready = sem("rstd2_ready")
        z_row_ready = sem("z_row_ready")
        z_turned = sem("z_turned")
        h2_ready = sem("h2_ready")
        xf_done = sem("xf_done")
        u_done = sem("u_done")
        u_ready = sem("u_ready")
        v_done = sem("v_done")
        v_added = sem("v_added")
        out_stored = sem("out_stored")
        z_summed = sem("z_summed")
        stats2_ready = sem("stats2_ready")
        held = sem("held")
        window_moved = [None] + [sem(f"window_moved_{c}") for c in (1, 2, 3)]

        def wait(eng, semaphore, count):
            if not (isinstance(count, int) and count <= 0):
                eng.wait_ge(semaphore, count)

        def hold(eng):
            eng.sem_inc(held, 1)

        def sweep(eng, body):
            body(0, None)
            with eng.Fori(1, LAG) as i:
                body(i, None)
            body(LAG, 0)
            with eng.Fori(LAG + 1, ITERS - 1) as i:
                body(i, i - LAG)
            body(ITERS - 1, ITERS - 1 - LAG)

        TAIL_BLOCKS = range(ITERS - LAG, NB)

        def gcn_sweep(eng, body):
            body(0, None, "build")
            with eng.Fori(1, LAG) as i:
                body(i, None, "build")
            body(LAG, 0, "build")
            with eng.Fori(LAG + 1, BUILD_ITERS) as i:
                body(i, i - LAG, "build")
            body(BUILD_ITERS, BUILD_ITERS - LAG, "built")
            body(FIRST_PRODUCT, FIRST_PRODUCT - LAG, "product")
            with eng.Fori(FIRST_PRODUCT + 1, FIRST_EXTRA) as i:
                body(i, i - LAG, "product")
            body(FIRST_EXTRA, FIRST_EXTRA - LAG, "last product")
            with eng.Fori(FIRST_EXTRA + 1, GCN_ITERS - 1) as i:
                body(i, 2 * i - FIRST_EXTRA - LAG, "extra")
            body(GCN_ITERS - 1, GCN_ITERS + EXTRA - 2 - LAG, "extra")

        def has_extra(stage):
            return stage in ("last product", "extra")

        def products_at(i, stage):
            slots = {"product": PRODUCTS, "last product": 1}.get(stage, 0)
            return [(s, PRODUCTS * (i - FIRST_PRODUCT) + s) for s in range(slots)]

        def counts_chunk(c, g, stage):
            return c == 1 and (stage == "build" and not (isinstance(g, int) and g == 0)
                               or isinstance(g, int) and g == DENSE)

        def adds_chunk(c, g, stage):
            return c == 1 and (stage == "build" and not (isinstance(g, int) and g < 2)
                               or isinstance(g, int) and DENSE <= g < DENSE + 2)

        def extra_block(i):
            return i + NB - GCN_ITERS

        GCN_TAIL = [(GCN_ITERS + EXTRA - LAG + k, GCN_ITERS - LAG + k) for k in range(NB - EXTRA - GCN_ITERS + LAG)]

        def all_blocks(eng, body):
            body(0)
            with eng.Fori(1, NB - 1) as j:
                body(j)
            body(NB - 1)

        def start_bank(q):
            return (ps_filter[:, 0, :], ps_filter[:, 1, :], ps_node[:, 0, :], ps_node[:, 1, :])[q % 4]

        def branch(eng, fast_path, general_path):
            eng.wait_ge(flag_ready, 1)
            flag = eng.value_load(fast_i[0:1, 0:1], min_val=0, max_val=1)
            with eng.If(flag > 0):
                fast_path()
            with eng.Else():
                general_path()

        block = ctx.enter_context(nc.Block())

        @block.sync
        def _(sp):
            def rows(v, lo, n):
                return v[lo * GROUP:(lo + n) * GROUP].rearrange("(g e) -> g e", e=GROUP)

            def one_row(v, lo, hi):
                return v[lo:hi].rearrange("(a e) -> a e", a=1)

            sp.dma_start(dst_raw[:, 0, :], rows(dst, 0, HALF)).then_inc(dst_loaded, 16)
            sp.wait_ge(padded, 1)
            sp.dma_start(dst_raw[0:HALF - 1, 1, :], rows(dst, HALF, HALF - 1)).then_inc(dst_loaded, 16)
            sp.dma_start(dst_raw[HALF - 1:HALF, 1, GROUP - TAIL:GROUP],
                         one_row(dst, E - TAIL, E)).then_inc(dst_loaded, 16)
            def chunks(v):
                return v[E - DENSE_EDGES:E - DENSE_REST].rearrange("(c e) -> c e", e=P)

            sp.wait_ge(padded, 3)
            sp.dma_start(dense_dst[0:DENSE_FULL, :], chunks(dst)).then_inc(dense_loaded, 16)
            sp.dma_start(dense_dst[DENSE_FULL:DENSE_FULL + 1, P - DENSE_REST:P],
                         one_row(dst, E - DENSE_REST, E)).then_inc(dense_loaded, 16)
            sp.dma_start(dense_src[0:DENSE_FULL, :], chunks(src)).then_inc(dense_loaded, 16)
            sp.dma_start(dense_src[DENSE_FULL:DENSE_FULL + 1, :],
                         one_row(src, E - P, E)).then_inc(dense_loaded, 16)
            sp.dma_start(src_raw[:, 0, :], rows(src, 0, HALF)).then_inc(src_loaded, 16)
            sp.dma_start(src_raw[0:HALF - 1, 1, :], rows(src, HALF, HALF - 1)).then_inc(src_loaded, 16)
            sp.dma_start(src_raw[HALF - 1:HALF, 1, :], one_row(src, E - GROUP, E)).then_inc(src_loaded, 16)
            sp.dma_start(weight_raw[:, 0, :], rows(edge_weight, 0, HALF)).then_inc(weight_loaded, 16)
            sp.dma_start(weight_raw[0:HALF - 1, 1, :],
                         rows(edge_weight, HALF, HALF - 1)).then_inc(weight_loaded, 16)
            sp.dma_start(weight_raw[HALF - 1:HALF, 1, :],
                         one_row(edge_weight, E - GROUP, E)).then_inc(weight_loaded, 16)

            n = NB // PARTS
            for i in range(PARTS):
                sp.wait_ge(table_ready, i + 1)
                sp.dma_start(table[1][i * n * P:(i + 1) * n * P, :].rearrange("(b p) f -> p b f", p=P),
                             z_nodes[:, i * n:(i + 1) * n, :]).then_inc(stored[1], 16)

            def store_rows(c, n, j):
                wait(sp, row_ready[c], n + 1)
                sp.dma_start(table[c + 1][bass.ds(j * P, P), :], row_out[:]).then_inc(stored[c + 1], 16)

            def store_out(j):
                wait(sp, row_ready[3], j + 1)
                n = LAST_ROWS if isinstance(j, int) and j == NB - 1 else P
                sp.dma_start(out[bass.ds(j * P, n), :], row_out[0:n, :]).then_inc(out_stored, 16)

            def load_edges(i, s):
                g = SLOTS * i + s
                wait(sp, edge_turned, g - SLOTS + 1)
                first = min(g * GROUP, E - GROUP) if isinstance(g, int) else g * GROUP
                sp.dma_start(edge_in[:, s, :, :],
                             edge_attr[bass.ds(first, GROUP), :].rearrange("(p j) r -> p j r", j=CHUNKS)
                             ).then_inc(edge_loaded[s], 16)

            def fast_path():
                for c in (1, 2):
                    sp.wait_ge(stored[c], 16 * (PARTS if c == 1 else NB))

                    def body(i, n, stage):
                        for s, k in products_at(i, stage):
                            wait(sp, parts_ready[c], 4 * (k - PRODUCTS + 1))
                            sp.dma_start(table_in[:, s, :], table[c][bass.ds(k * P, P), :]
                                         ).then_inc(block_loaded[c][s], 16)
                        if n is not None:
                            store_rows(c, n, i - LAG)
                        if has_extra(stage):
                            store_rows(c, n + 1, extra_block(i))
                    gcn_sweep(sp, body)
                    for n, j in GCN_TAIL:
                        store_rows(c, n, j)

                def body(i, j):
                    for s in range(SLOTS):
                        if s == 3 and j is not None and not (isinstance(j, int) and j == 0):
                            store_out(j - 1)
                        load_edges(i, s)
                sweep(sp, body)
                for j in range(ITERS - LAG - 1, NB):
                    store_out(j)

            def general_path():
                for c in (1, 2):
                    all_blocks(sp, lambda j: store_rows(c, j, j))

                def body(i, j):
                    for s in range(SLOTS):
                        load_edges(i, s)
                sweep(sp, body)
                all_blocks(sp, store_out)

            branch(sp, fast_path, general_path)
            sp.wait_ge(out_stored, 16 * NB)

        @block.gpsimd
        def _(pool):
            nc.gpsimd.iota(group_id[:], pattern=[[HALF, 2]], base=0, channel_multiplier=1)
            nc.gpsimd.iota(iota_i[:], pattern=[[0, CHUNKS], [1, WINDOW]], base=0,
                           channel_multiplier=0).then_inc(pool_consts, 1)
            nc.gpsimd.memset(ident[:], 0.0).then_inc(pool_consts, 1)
            pool.wait_ge(pool_consts, 2)
            nc.gpsimd.affine_select(out=ident[:], in_=ident[:], compare_op=ALU.not_equal, fill=1.0,
                                    base=0, pattern=[[-1, P]], channel_multiplier=1).then_inc(pool_consts, 1)

            nc.gpsimd.iota(iota_lo_i[:], pattern=[[1, P], [0, BATCH]], base=0,
                           channel_multiplier=0).then_inc(hist_iota, 1)
            nc.gpsimd.iota(code_iota_i[:], pattern=[[1, NB * SPAN]], base=CODE_ONE,
                           channel_multiplier=0).then_inc(hist_iota, 1)
            pool.wait_ge(norm_ready, 1)
            nc.gpsimd.tensor_tensor(z_nodes[:], nodes[:], mean[:].unsqueeze(2).to_broadcast([P, NB, F]),
                                    ALU.subtract).then_inc(z_nodes_ready, 1)
            pool.wait_ge(z_nodes_ready, 1)
            nc.gpsimd.tensor_tensor(z_nodes[:], z_nodes[:], rstd[:].unsqueeze(2).to_broadcast([P, NB, F]),
                                    ALU.mult).then_inc(z_nodes_ready, 1)

            bound = pool.to_reg(NB * P - 1)

            def gather(c, i, s):
                wait(pool, staged[c], SLOTS * i + s + 1)
                hold(pool)
                for k in range(CHUNKS):
                    nc.gpsimd.indirect_dma_start(
                        ring[:, s, k, :], None, table[c],
                        bass.IndirectOffsetOnAxis(idx_stage[:, s, k:k + 1], 0),
                        bounds_check=bound, oob_is_err=False).then_inc(gathered[c][s], 16)

            def gathers(c, iterations):
                pool.wait_ge(stored[c], 16 * (PARTS if c == 1 else NB))
                with pool.Fori(0, iterations) as i:
                    for s in range(SLOTS):
                        gather(c, i, s)

            def fast_path():
                for c, iterations in ((1, GCN_ITERS), (2, GCN_ITERS), (3, ITERS)):
                    gathers(c, iterations)

            def general_path():
                for c in (1, 2, 3):
                    gathers(c, ITERS)

            branch(pool, fast_path, general_path)

        @block.scalar
        def _(act):
            def params(o, i, **kw):
                act.dma_start(o, i, **kw).then_inc(params_loaded, 16)

            def column(v, cols=1):
                return v.rearrange("(m p) -> p m", p=P)

            def row(v):
                return v.rearrange("(a f) -> a f", a=1)

            act.dma_start(nodes[:, 0:NB - 1, :],
                          x[0:(NB - 1) * P, :].rearrange("(b p) f -> p b f", p=P)).then_inc(x_loaded, 16)
            act.wait_ge(consts_ready, 1)
            act.dma_start(nodes[0:LAST_ROWS, NB - 1, :], x[(NB - 1) * P:N, :]).then_inc(x_loaded, 16)
            params(W1_sb[:], W1)
            params(W2_sb[:], W2.rearrange("(m p) f -> p m f", p=P))
            params(b1_col[:], column(b1), allow_slow_non_contiguous=True)
            params(b2_all[:], b2.partition_broadcast(P))
            params(mlp_w1_sb[:], mlp_w1)
            params(mlp_w2_sb[:], mlp_w2)
            params(mlp_b1_col[:], column(mlp_b1), allow_slow_non_contiguous=True)
            for k in range(CHUNKS):
                params(mlp_b2_row[:, k, :], row(mlp_b2))
            params(lin1_sb[:], lin1_w)
            params(lin2_sb[:], lin2_w)
            params(lin2_b_col[:], column(lin2_b), allow_slow_non_contiguous=True)
            params(lin_sb[:], lin_w)
            params(lin_b_all[:], lin_b.partition_broadcast(P))

            def halves(semaphore, ps, to):
                for t in range(2):
                    act.wait_ge(semaphore, t + 1)
                    last = nc.scalar.copy(
                        to[:, t * HALF:(t + 1) * HALF, :].rearrange("p g k -> p k g"),
                        ps[:, t, 0:CHUNKS * HALF].rearrange("p (k g) -> p k g", k=CHUNKS))
                return last

            halves(dst_T_ready, ps_agg, dst_T[:].rearrange("p (g k) -> p g k", k=CHUNKS)
                   ).then_inc(dst_T_copied, 1)
            act.wait_ge(hist_iota, 2)
            nc.scalar.copy(iota_lo[:], iota_lo_i[:]).then_inc(hist_iota, 1)
            halves(rel_T_ready, ps_filter, rel).then_inc(indices_ready, 1)
            halves(src_T_ready, ps_node, src_idx).then_inc(indices_ready, 1)
            halves(weight_T_ready, ps_agg, angle).then_inc(angle_ready, 1)
            act.wait_ge(var_ready, 1)
            nc.scalar.activation(rstd[:], var[:], ACT.Sqrt, bias=eps_col[:, 0:1]).then_inc(std_ready, 1)

            def scales(c, j):
                wait(act, scale_done[c], j + 1)
                nc.scalar.copy(scale_all[:], ps_node[:, 1, P:2 * P]).then_inc(scale_ready[c], 1)

            def node_1(j):
                scales(1, j)
                wait(act, y_done, j + 1)
                wait(act, stored[2], 16 * j)
                nc.scalar.copy(row_out[:], ps_node[:, 1, 0:F]).then_inc(row_ready[1], 1)

            def node_2(j, part):
                if part == 0:
                    wait(act, var2_ready, j + 1)
                    nc.scalar.activation(std2[:], mv2[:, 1:2], ACT.Sqrt, bias=eps_col[:, 0:1]
                                         ).then_inc(std2_ready, 1)
                if part == 1:
                    wait(act, z_turned, j + 1)
                    nc.scalar.activation(h2_T[:], ps_node[:, 1, 0:P], ACT.Relu).then_inc(h2_ready, 1)
                if part == 2:
                    wait(act, xf_done, j + 1)
                    wait(act, stored[3], 16 * j)
                    nc.scalar.copy(row_out[:], ps_node[:, 0, 0:F]).then_inc(row_ready[2], 1)

            def node_3(j):
                scales(3, j)
                wait(act, u_done, j + 1)
                nc.scalar.activation(z_row[:], ps_node[:, 0, 0:P], ACT.Silu, bias=lin2_b_col[:, 0:1]
                                     ).then_inc(u_ready, 1)

            def edge_copy(g, slot):
                wait(act, edge_turned, g + 1)
                nc.scalar.copy(edge_T[:, slot, :], ps_edge_T[0:R, :]).then_inc(edge_T_ready, 1)

            def edge_silu(g, slot):
                wait(act, filter_ready, g - 1)
                wait(act, hidden_done, g + 1)
                nc.scalar.activation(hidden_T[:, slot, :, :],
                                     ps_hidden[:, :].rearrange("p (k e) -> p k e", k=CHUNKS),
                                     ACT.Silu, bias=mlp_b1_col[:, 0:1]).then_inc(hidden_ready, 1)

            act.wait_ge(degree_ready, 1)
            nc.scalar.activation(dinv[:], degree[:], ACT.Sqrt).then_inc(root_ready, 1)
            for q in range(-(-NB // 4)):
                act.wait_ge(table_turned, q + 1)
                n = min(4, NB - 4 * q) * P
                nc.scalar.copy(acc[:, 4 * q * P:4 * q * P + n], start_bank(q)[:, 0:n]
                               ).then_inc(start_ready, 1)

            act.wait_ge(angle_ready, 2)
            nc.scalar.activation(angle[:], angle[:], ACT.Sin, bias=half_pi[:, 0:1],
                                 scale=-6.283185307179586).then_inc(sin_ready, 1)
            act.wait_ge(params_loaded, 16 * 16)

            def fast_path():
                for c in (1, 2):
                    def update(n):
                        if c == 1:
                            node_1(n)
                        else:
                            for part in range(3):
                                node_2(n, part)

                    def body(i, n, stage):
                        if n is not None:
                            update(n)
                        if has_extra(stage):
                            update(n + 1)
                    gcn_sweep(act, body)
                    for n, j in GCN_TAIL:
                        update(n)

                edge_copy(0, 0)
                edge_copy(1, 1)
                edge_silu(0, 0)

                def body(i, j):
                    for s in range(SLOTS):
                        g = SLOTS * i + s
                        if not (isinstance(g, int) and g + 2 >= NG):
                            edge_copy(g + 2, s % 2)
                        if not (isinstance(g, int) and g + 1 >= NG):
                            edge_silu(g + 1, (s + 1) % 2)
                        if s == 1 and j is not None:
                            node_3(j)
                sweep(act, body)
                for j in TAIL_BLOCKS:
                    node_3(j)

            def general_path():
                all_blocks(act, node_1)

                def body(j):
                    for part in range(3):
                        node_2(j, part)
                all_blocks(act, body)

                def body(i, j):
                    for s in range(SLOTS):
                        g = SLOTS * i + s
                        edge_copy(g, s % 2)
                        edge_silu(g, s % 2)
                sweep(act, body)
                all_blocks(act, node_3)

            branch(act, fast_path, general_path)

        @block.vector
        def _(dve):
            chain = [0]

            def link(ins):
                chain[0] += 1
                ins.then_inc(dve_chain, 1)
                dve.wait_ge(dve_chain, chain[0])

            vec = nc.vector
            vec.memset(dst_raw[:, 1, :], NO_NODE).then_inc(padded, 1)
            vec.memset(dense_dst[:], NO_NODE).then_inc(padded, 1)
            vec.memset(dense_src[:], 0).then_inc(padded, 1)
            vec.memset(nodes[:, NB - 1, :], 0.0).then_inc(consts_ready, 1)
            vec.memset(tests[:], 0.0)
            vec.memset(ones[:], 1.0)
            vec.memset(zeros[:], 0.0)
            vec.memset(eps_col[:], LN_EPS)
            vec.memset(half_pi[:], 1.5707963267948966)
            vec.memset(acc[:, NB * P:], 0.0)
            dve.wait_ge(pool_consts, 1)
            vec.tensor_copy(iota_f[:], iota_i[:]).then_inc(consts_ready, 1)
            link(vec.tensor_scalar(group_id[:], group_id[:], SLOTS.bit_length() - 1, P.bit_length() - 1,
                                   ALU.arith_shift_right, ALU.logical_shift_left))
            link(vec.tensor_scalar(earliest[:], group_id[:], float(-P * (LAG - 1)), None, ALU.add))

            dve.wait_ge(dst_loaded, 48)
            vec.tensor_copy(dst_f[:], dst_raw[:]).then_inc(dst_f_ready, 1)
            dve.wait_ge(dst_f_ready, 1)
            link(vec.tensor_reduce(base[:], dst_f[:], AX_X, ALU.min))
            for t in range(2):
                link(vec.tensor_scalar(rel_f[:, t, :], dst_f[:, t, :], base[:, t:t + 1], None, ALU.subtract))
                vec.tensor_scalar(rel_f[:, t, :], rel_f[:, t, :], float(WINDOW), 0.0, ALU.is_lt, ALU.add,
                                  accum_out=tests[:, t:t + 1])
            vec.tensor_tensor(tests[:, 2:4], base[:], earliest[:], ALU.is_ge)
            dve.wait_ge(dense_loaded, 64)
            link(vec.tensor_copy(dense_dst_f[:], dense_dst[:]))
            link(vec.tensor_reduce(chunk_base[:], dense_dst_f[:], AX_X, ALU.min))
            link(vec.tensor_scalar(chunk_base[:], chunk_base[:], float(N - 1), None, ALU.min))
            link(vec.tensor_scalar(dense_rel[:], dense_dst_f[:], chunk_base[:], None, ALU.subtract))
            vec.tensor_scalar(dense_code[:], dense_rel[:], float(SPAN), 0.0, ALU.is_lt, ALU.add,
                              accum_out=tests[0:DENSE, 4:5])
            vec.tensor_scalar(tests[0:DENSE, 5:6], chunk_base[:], float(ORIGIN), None, ALU.is_ge)
            for t, n in ((0, HALF), (1, GCN_ITERS * SLOTS - HALF)):
                last = vec.tensor_scalar(tests[0:n, 6 + t:7 + t], base[0:n, t:t + 1],
                                         float(ORIGIN + P - WINDOW), None, ALU.is_le)
            last.then_inc(tests_ready, 1)
            link(vec.tensor_scalar(dense_part[:], dense_src[:], P - 1, None, ALU.bitwise_and))
            link(vec.tensor_copy(dense_lo[:], dense_part[:]))
            link(vec.tensor_scalar(dense_part[:], dense_src[:], P.bit_length() - 1, None, ALU.arith_shift_right))
            link(vec.tensor_copy(dense_hi[:], dense_part[:]))
            vec.scalar_tensor_tensor(out=dense_code[:], in0=dense_hi[:], scalar=float(SPAN), in1=dense_rel[:],
                                     op0=ALU.mult, op1=ALU.add).then_inc(dense_ready, 1)
            dve.wait_ge(src_loaded, 48)
            vec.tensor_copy(src_f[:], src_raw[:]).then_inc(src_f_ready, 1)
            dve.wait_ge(totals_ready, 1)
            link(vec.tensor_reduce(totals[:], ps_edge_T[:, 0:8], AX_X, ALU.add))
            link(vec.tensor_scalar(fast[:], totals[:], float(E + NG + DENSE_EDGES + DENSE + GCN_ITERS * SLOTS),
                                   None, ALU.is_equal))
            vec.tensor_copy(fast_i[:], fast[0:1, :])
            link(vec.tensor_scalar(base[:], base[:], fast[0:HALF, 0:1], None, ALU.mult))
            for t in range(2):
                last = vec.tensor_scalar(rel_f[:, t, :], dst_f[:, t, :], base[:, t:t + 1], None, ALU.subtract)
            last.then_inc(rel_ready, 1)
            dve.wait_ge(base_rows_ready, 1)
            vec.tensor_copy(base_i[:], ps_hidden[0:1, 0:NG]).then_inc(flag_ready, 1)

            dve.wait_ge(dense_T_ready, 1)
            vec.tensor_copy(lo_T[:], ps_edge_T[:, P:P + DENSE])
            vec.tensor_scalar(code_T[:], ps_edge_T[:, 2 * P:2 * P + DENSE], float(CODE_ONE), None, ALU.add)
            link(vec.tensor_scalar(chunk_at[:], ps_edge_T[0:1, 3 * P:3 * P + DENSE], float(ORIGIN), None,
                                   ALU.subtract))
            link(vec.tensor_scalar(code_T[:], code_T[:], 16, None, ALU.logical_shift_left))

            dve.wait_ge(dst_T_copied, 1)
            link(vec.tensor_scalar(part_i[:], dst_T[:], P - 1, None, ALU.bitwise_and))
            link(vec.tensor_copy(dst_lo[:], part_i[:]))
            link(vec.tensor_scalar(part_i[:], dst_T[:], P.bit_length() - 1, None, ALU.arith_shift_right))
            link(vec.tensor_copy(dst_hi[:], part_i[:]))

            dve.wait_ge(x_loaded, 32)
            for b in range(NB):
                last = vec.bn_stats(stats[:, b, :], nodes[:, b, :])
            link(last)
            me, mo, ve, vo = (stats[:, :, k] for k in (1, 4, 2, 5))
            link(vec.tensor_tensor(tmp[:], me, mo, ALU.subtract))
            link(vec.tensor_tensor(tmp[:], tmp[:], tmp[:], ALU.mult))
            link(vec.tensor_tensor(var[:], ve, vo, ALU.add))
            link(vec.tensor_scalar(tmp[:], tmp[:], 0.25, None, ALU.mult))
            link(vec.scalar_tensor_tensor(out=var[:], in0=var[:], scalar=1.0 / F, in1=tmp[:],
                                          op0=ALU.mult, op1=ALU.add))
            link(vec.tensor_tensor(mean[:], me, mo, ALU.add))
            vec.tensor_scalar(mean[:], mean[:], 0.5, None, ALU.mult).then_inc(var_ready, 1)
            dve.wait_ge(std_ready, 1)
            vec.reciprocal(rstd[:], rstd[:]).then_inc(norm_ready, 1)

            dve.wait_ge(hist_iota, 3)

            vec.tensor_copy(lo_iota[:], iota_lo[:, :, 0])
            link(vec.tensor_scalar(code_iota_i[:], code_iota_i[:], 16, None, ALU.logical_shift_left))
            link(vec.tensor_copy(code_iota[:], code_iota_i[:].bitcast(F32)))

            def hist_batch(b, slot):
                wait(dve, hist_summed, b - 1)
                for to, of, rows in ((hist_lo, dst_lo, P), (hist_hi, dst_hi, NB)):
                    last = vec.tensor_tensor(
                        to[:, slot, :, :], iota_lo[:, 0:rows, :],
                        of[:, bass.ds(b * BATCH, BATCH)].unsqueeze(1).to_broadcast([P, rows, BATCH]),
                        ALU.is_equal)
                last.then_inc(hist_onehot, 1)

            for slot in range(2):
                hist_batch(slot, slot)
            with dve.Fori(1, ITERS // 2) as i:
                for slot in range(2):
                    hist_batch(2 * i + slot, slot)

            dve.wait_ge(hist_summed, ITERS)
            link(vec.tensor_copy(inv_count[:], ps_hidden[:, 0:NB]))
            vec.tensor_scalar(degree[:], inv_count[:], 1.0, None, ALU.add).then_inc(degree_ready, 1)
            dve.wait_ge(root_ready, 1)
            link(vec.reciprocal(dinv[:], dinv[:]))
            dve.wait_ge(z_nodes_ready, 2)
            n = NB // PARTS
            for i in range(PARTS):
                zi = z_nodes[:, i * n:(i + 1) * n, :]
                vec.scalar_tensor_tensor(
                    out=zi, in0=zi, scalar=0.0,
                    in1=dinv[:, i * n:(i + 1) * n].unsqueeze(2).to_broadcast([P, n, F]),
                    op0=ALU.max, op1=ALU.mult).then_inc(table_ready, 1)
            link(vec.tensor_scalar(inv_count[:], inv_count[:], 1.0, None, ALU.max))
            link(vec.reciprocal(inv_count[:], inv_count[:]))
            dve.wait_ge(indices_ready, 2)

            def make_onehot(c, g, slot, iota):
                vec.tensor_tensor(onehot[:, slot, :, :], iota[:],
                                  rel[:, bass.ds(g, 1), :].rearrange("p a k -> p (a k)").unsqueeze(2)
                                  .to_broadcast([P, CHUNKS, WINDOW]),
                                  ALU.is_equal).then_inc(onehot_ready[c], 1)

            def flush(c, g, slot, at, before):
                wait(dve, flushed[c], before)
                wait(dve, summed[c], before + 1)
                to = acc[:, bass.ds(at, WINDOW)]
                vec.tensor_tensor(to, to, ps_agg[:, slot, 0:WINDOW], ALU.add).then_inc(flushed[c], 1)

            def stage_indices(c, g, s):
                vec.tensor_copy(idx_stage[:, s, :].unsqueeze(1), src_idx[:, bass.ds(g, 1), :]
                                ).then_inc(staged[c], 1)

            def message(i, s):
                g = SLOTS * i + s
                wait(dve, gathered[3][s], 16 * CHUNKS * (i + 1))
                wait(dve, filter_ready, g + 1)
                for k in range(CHUNKS):
                    last = vec.scalar_tensor_tensor(
                        out=ring[:, s, k, :], in0=ps_filter[:, s % 2, k * P:(k + 1) * P],
                        scalar=cutoff[:].rearrange("p g k -> p (g k)")[:, bass.ds(g * CHUNKS + k, 1)],
                        in1=ring[:, s, k, :], op0=ALU.mult, op1=ALU.mult)
                last.then_inc(message_ready, 1)

            def fast_flush(c, g, s):
                at = dve.value_load(base_i[0:1, bass.ds(g, 1)], min_val=0, max_val=N - 1)
                flush(c, g, s % 2, at, g)

            def general_windows(c, g, s):
                wait(dve, window_moved[c], g * (NW + 1))
                vec.tensor_copy(iota_w[:], iota_f[:]).then_inc(window_moved[c], 1)
                with dve.Fori(0, NW) as w:
                    n = g * NW + w
                    dve.wait_ge(window_moved[c], n + g + 1)
                    make_onehot(c, g, s % 2, iota_w)
                    dve.wait_ge(summed[c], n + 1)
                    to = acc[:, bass.ds(w * WINDOW, WINDOW)]
                    vec.tensor_tensor(to, to, ps_agg[:, s % 2, 0:WINDOW], ALU.add).then_inc(flushed[c], 1)
                    vec.tensor_scalar(iota_w[:], iota_w[:], float(WINDOW), None, ALU.add
                                      ).then_inc(window_moved[c], 1)

            def chunk_matrices(q, slot):
                wait(dve, chunk_summed, q - 1)
                hold(dve)
                vec.tensor_scalar(lo_onehot[:, slot, :], lo_iota[:], lo_T[:, bass.ds(q, 1)], None, ALU.is_equal)
                vec.tensor_scalar(code_onehot[:, slot, :], code_iota[:],
                                  code_T[:].bitcast(F32)[:, bass.ds(q, 1)], None, ALU.is_equal
                                  ).then_inc(chunk_onehot, 1)

            def add_chunk(q):
                at = dve.value_load(chunk_at[0:1, bass.ds(q, 1)], min_val=0, max_val=COLS - SPAN)
                wait(dve, chunk_summed, q + 1)
                wait(dve, chunk_added, 2 * q)
                hold(dve)
                for h, (lo, hi) in enumerate(((0, HI_SPLIT), (HI_SPLIT, NB))):
                    to = adjacency[:, lo:hi, bass.ds(at, SPAN)]
                    vec.tensor_tensor(to, to, ps_filter[:, h, 0:(hi - lo) * SPAN]
                                      .rearrange("p (b n) -> p b n", n=SPAN), ALU.add).then_inc(chunk_added, 1)

            def split_block(c, i, k, s):
                high, middle, low = (table_parts[:, s, part, :] for part in range(3))
                wait(dve, block_loaded[c][s], 16 * (i - FIRST_PRODUCT + 1))
                wait(dve, block_used[c], k - PRODUCTS + 1)
                vec.tensor_copy(high, table_in[:, s, :]).then_inc(parts_ready[c], 1)
                wait(dve, parts_ready[c], 4 * k + 1)
                vec.tensor_tensor(table_rest[:], table_in[:, s, :], high, ALU.subtract
                                  ).then_inc(parts_ready[c], 1)
                wait(dve, parts_ready[c], 4 * k + 2)
                vec.tensor_copy(middle, table_rest[:]).then_inc(parts_ready[c], 1)
                wait(dve, parts_ready[c], 4 * k + 3)
                vec.tensor_tensor(low, table_rest[:], middle, ALU.subtract).then_inc(parts_ready[c], 1)

            def add_dense(c):
                dve.wait_ge(block_used[c], NB)
                for h, ps in ((0, ps_edge_T), (1, ps_hidden)):
                    to = acc[:, ORIGIN + h * COLS // 2:ORIGIN + (h + 1) * COLS // 2]
                    vec.tensor_tensor(to, to, ps[:, 0:COLS // 2], ALU.add).then_inc(dense_added[c], 1)
                dve.wait_ge(dense_added[c], 2)

            def columns(tile, j):
                return tile[:, bass.ds(j * P, P)]

            def diagonal(c, j):
                scale = inv_count if c == 3 else dinv
                vec.tensor_scalar(scale_diag[:], ident[:], scale[:, bass.ds(j, 1)], None, ALU.mult
                                  ).then_inc(diag_ready[c], 1)

            def node_1(n, j, part):
                if part == 0:
                    wait(dve, scale_ready[1], n + 1)
                    vec.tensor_tensor(z_T[:], columns(acc, j), scale_all[:], ALU.mult
                                      ).then_inc(z_ready[1], 1)
                if part == 1:
                    wait(dve, h_done, n + 1)
                    for m in range(HM):
                        last = vec.scalar_tensor_tensor(
                            out=h_T[:, m, :], in0=ps_node[:, 0, m * P:(m + 1) * P],
                            scalar=b1_col[:, m:m + 1], in1=scale_all[:], op0=ALU.add, op1=ALU.mult)
                    last.then_inc(h_ready, 1)
                if part == 2:
                    wait(dve, y_T_done, n + 1)
                    vec.tensor_scalar(columns(acc, j), ps_node[:, 0, 0:P], 1.0, None, ALU.mult
                                      ).then_inc(acc_reset[1], 1)

            def node_2(n, j, part):
                if part == 0:
                    vec.tensor_scalar(z_T[:], columns(acc, j), 1.0, None, ALU.mult
                                      ).then_inc(z_ready[2], 1)
                    wait(dve, z_ready[2], n + 1)
                    vec.tensor_scalar(columns(acc, j), zeros[:], 1.0, None, ALU.mult).then_inc(acc_reset[2], 1)
                if part == 1:
                    wait(dve, turned, n + 1)
                    xj = nodes[:, bass.ds(j, 1), :].rearrange("p a f -> p (a f)")
                    vec.scalar_tensor_tensor(out=z_row[:], in0=ps_node[:, 0, 0:F],
                                             scalar=dinv[:, bass.ds(j, 1)], in1=b2_all[:],
                                             op0=ALU.mult, op1=ALU.add).then_inc(z_summed, 1)
                    wait(dve, z_summed, 2 * n + 1)
                    vec.tensor_tensor(z_row[:], z_row[:], xj, ALU.add).then_inc(z_summed, 1)
                    wait(dve, z_summed, 2 * n + 2)
                    vec.tensor_scalar(xj, z_row[:], 1.0, None, ALU.mult)
                    vec.bn_stats(stats2[:], z_row[:]).then_inc(stats2_ready, 1)
                    wait(dve, stats2_ready, n + 1)
                    hold(dve)
                    vec.bn_aggr(mv2[:], stats2[:]).then_inc(var2_ready, 1)
                if part == 2:
                    wait(dve, std2_ready, n + 1)
                    vec.reciprocal(rstd2[:], std2[:]).then_inc(rstd2_ready, 1)
                    wait(dve, rstd2_ready, n + 1)
                    vec.tensor_scalar(z_row[:], z_row[:], mv2[:, 0:1], rstd2[:, 0:1],
                                      ALU.subtract, ALU.mult).then_inc(z_row_ready, 1)

            def node_3(j, part):
                if part == 0:
                    wait(dve, scale_ready[3], j + 1)
                    vec.tensor_tensor(z_T[:], columns(acc, j), scale_all[:], ALU.mult
                                      ).then_inc(z_ready[3], 1)
                if part == 1:
                    wait(dve, v_done, j + 1)
                    wait(dve, out_stored, 16 * j)
                    xj = nodes[:, bass.ds(j, 1), :].rearrange("p a f -> p (a f)")
                    vec.tensor_tensor(row_out[:], ps_node[:, 1, 0:F], lin_b_all[:], ALU.add
                                      ).then_inc(v_added, 1)
                    wait(dve, v_added, j + 1)
                    vec.tensor_tensor(row_out[:], row_out[:], xj, ALU.add).then_inc(row_ready[3], 1)

            def fast_path():
                dve.wait_ge(stored[1], 16 * PARTS)
                link(vec.memset(adjacency[:], 0.0))
                for c in (1, 2):
                    if c == 2:
                        for s in range(SLOTS):
                            stage_indices(c, s, s)
                    node = (node_1, node_2)[c - 1]

                    def update(n, j):
                        if c == 1:
                            diagonal(c, j)
                        for part in range(3):
                            node(n, j, part)

                    def body(i, n, stage):
                        j = None if n is None else i - LAG
                        for s in range(SLOTS):
                            g = SLOTS * i + s
                            if j is not None and s == 0 and c == 1:
                                diagonal(c, j)
                            if j is not None and s == 2:
                                node(n, j, 1)
                            if j is not None and s == 3 and c == 2:
                                node(n, j, 2)
                            make_onehot(c, g, s % 2, iota_f)
                            if adds_chunk(c, g, stage):
                                add_chunk(g - 2)
                            for slot, k in products_at(i, stage):
                                if slot == s:
                                    split_block(c, i, k, s)
                            fast_flush(c, g, s)
                            if not (isinstance(i, int) and i == GCN_ITERS - 1):
                                stage_indices(c, g + SLOTS, s)
                            if j is not None and s == 0:
                                wait(dve, flushed[c], g + 1)
                                node(n, j, 0)
                            if j is not None and s == 3 and c == 1:
                                node(n, j, 2)
                            if c == 1 and stage == "build":
                                chunk_matrices(g, s % 2)
                        if stage == "last product":
                            add_dense(c)
                        if has_extra(stage):
                            update(n + 1, extra_block(i))
                    gcn_sweep(dve, body)
                    dve.wait_ge(flushed[c], GCN_ITERS * SLOTS)
                    for n, j in GCN_TAIL:
                        update(n, j)
                    dve.wait_ge(acc_reset[c], NB)

                for s in range(SLOTS - 1):
                    stage_indices(3, s, s)

                def body(i, j):
                    for s in range(SLOTS):
                        g = SLOTS * i + s
                        if j is not None and s == 0:
                            diagonal(3, j)
                        if j is not None and s == 3:
                            node_3(j, 1)
                        make_onehot(3, g, s % 2, iota_f)
                        message(i, s)
                        if not (isinstance(g, int) and g == 0):
                            fast_flush(3, g - 1, s - 1)
                        if not (isinstance(g, int) and g + SLOTS - 1 >= NG):
                            stage_indices(3, g + SLOTS - 1, (s + SLOTS - 1) % SLOTS)
                        if j is not None and s == 0:
                            wait(dve, flushed[3], g)
                            node_3(j, 0)
                sweep(dve, body)
                fast_flush(3, NG - 1, SLOTS - 1)
                for j in TAIL_BLOCKS:
                    wait(dve, flushed[3], NG)
                    diagonal(3, j)
                    node_3(j, 0)
                    node_3(j, 1)

            def general_path():
                for c in (1, 2, 3):
                    if c != 1:
                        for s in range(SLOTS):
                            stage_indices(c, s, s)

                    def body(i, j):
                        for s in range(SLOTS):
                            g = SLOTS * i + s
                            if c == 3:
                                message(i, s)
                            general_windows(c, g, s)
                            if not (isinstance(i, int) and i == ITERS - 1):
                                stage_indices(c, g + SLOTS, s)
                    sweep(dve, body)
                    dve.wait_ge(flushed[c], NG * NW)

                    def body(j):
                        if c != 2:
                            diagonal(c, j)
                        for part in range(2 if c == 3 else 3):
                            if c == 3:
                                node_3(j, part)
                            else:
                                (node_1, node_2)[c - 1](j, j, part)
                    all_blocks(dve, body)
                    if c < 3:
                        dve.wait_ge(acc_reset[c], NB)

            for s in range(SLOTS):
                stage_indices(1, s, s)
            dve.wait_ge(angle_ready, 1)
            vec.tensor_scalar(cutoff[:], angle[:], CUTOFF, 0.5, ALU.is_lt, ALU.mult)
            link(vec.tensor_scalar(angle[:], angle[:], 0.5 / CUTOFF, None, ALU.mult))
            link(vec.tensor_scalar(turns[:], angle[:], ROUND, ROUND, ALU.add, ALU.subtract))
            link(vec.tensor_tensor(angle[:], angle[:], turns[:], ALU.subtract))
            vec.scalar_tensor_tensor(out=angle[:], in0=angle[:], scalar=-1.0, in1=angle[:],
                                     op0=ALU.mult, op1=ALU.max).then_inc(angle_ready, 1)
            dve.wait_ge(sin_ready, 1)
            link(vec.scalar_tensor_tensor(out=cutoff[:], in0=angle[:], scalar=1.0, in1=cutoff[:],
                                          op0=ALU.add, op1=ALU.mult))
            dve.wait_ge(params_loaded, 16 * 16)
            dve.wait_ge(start_ready, -(-NB // 4))
            branch(dve, fast_path, general_path)

        @block.tensor
        def _(pe):
            mm, turn = nc.tensor.matmul, nc.tensor.transpose

            pe.wait_ge(consts_ready, 2)
            pe.wait_ge(pool_consts, 3)

            def turn_indices(tile, ps, semaphore):
                for t in range(2):
                    for k in range(CHUNKS):
                        last = turn(ps[:, t, k * HALF:(k + 1) * HALF],
                                    tile[:, t, :].rearrange("g (p k) -> g k p", k=CHUNKS)[:, k, :],
                                    ident[0:HALF, 0:HALF])
                    last.then_inc(semaphore, 1)

            pe.wait_ge(dst_f_ready, 1)
            turn_indices(dst_f, ps_agg, dst_T_ready)
            pe.wait_ge(tests_ready, 1)
            mm(ps_edge_T[:, 0:8], ones[0:HALF, :], tests[:], start=True, stop=True).then_inc(totals_ready, 1)
            pe.wait_ge(rel_ready, 1)
            for t in range(2):
                last = mm(ps_hidden[0:1, t * HALF:(t + 1) * HALF], base[:, t:t + 1],
                          ident[0:HALF, 0:HALF], start=True, stop=True)
            last.then_inc(base_rows_ready, 1)
            pe.wait_ge(dense_ready, 1)
            turn(ps_edge_T[:, P:P + DENSE], dense_lo[:], ident[0:DENSE, 0:DENSE])
            turn(ps_edge_T[:, 2 * P:2 * P + DENSE], dense_code[:], ident[0:DENSE, 0:DENSE])
            mm(ps_edge_T[0:1, 3 * P:3 * P + DENSE], chunk_base[:], ident[0:DENSE, 0:DENSE],
               start=True, stop=True).then_inc(dense_T_ready, 1)
            turn_indices(rel_f, ps_filter, rel_T_ready)
            pe.wait_ge(src_f_ready, 1)
            turn_indices(src_f, ps_node, src_T_ready)
            pe.wait_ge(weight_loaded, 48)
            pe.wait_ge(dst_T_copied, 1)
            turn_indices(weight_raw, ps_agg, weight_T_ready)

            pe.wait_ge(flag_ready, 1)

            def hist_batch(b, slot, first, final):
                wait(pe, hist_onehot, b + 1)
                for k in range(BATCH):
                    last = mm(ps_hidden[:, 0:NB], hist_lo[:, slot, :, k], hist_hi[:, slot, :, k],
                              start=(first and k == 0), stop=(final and k == BATCH - 1),
                              skip_group_check=True)
                last.then_inc(hist_summed, 1)

            for slot in range(2):
                hist_batch(slot, slot, slot == 0, False)
            with pe.Fori(1, ITERS // 2 - 1) as i:
                for slot in range(2):
                    hist_batch(2 * i + slot, slot, False, False)
            for slot in range(2):
                hist_batch(ITERS - 2 + slot, slot, False, slot == 1)

            pe.wait_ge(indices_ready, 2)
            n = NB // PARTS
            for b in range(NB):
                if b % n == 0:
                    pe.wait_ge(table_ready, b // n + 1)
                q = b // 4
                if b % 4 == 0 and q >= 4:
                    pe.wait_ge(start_ready, q - 3)
                last = turn(start_bank(q)[:, b % 4 * P:(b % 4 + 1) * P], z_nodes[:, b, :], ident[:])
                if b % 4 == 3 or b == NB - 1:
                    last.then_inc(table_turned, 1)
            pe.wait_ge(start_ready, -(-NB // 4))
            pe.wait_ge(angle_ready, 1)
            pe.wait_ge(params_loaded, 16 * 16)

            def sum_window(c, n, s):
                wait(pe, onehot_ready[c], n + 1)
                for k in range(CHUNKS):
                    last = mm(ps_agg[:, s % 2, 0:WINDOW], ring[:, s, k, :],
                              onehot[:, s % 2, k, :], start=(k == 0), stop=(k == CHUNKS - 1))
                last.then_inc(summed[c], 1)

            def edge_turn(g, s, i):
                wait(pe, edge_loaded[s], 16 * (i + 1))
                wait(pe, edge_T_ready, g)
                hold(pe)
                for k in range(CHUNKS):
                    last = turn(ps_edge_T[0:R, k * P:(k + 1) * P], edge_in[:, s, k, :], ident[:])
                last.then_inc(edge_turned, 1)

            def edge_hidden(g, slot):
                wait(pe, hidden_ready, g)
                wait(pe, edge_T_ready, g + 1)
                mm(ps_hidden[:, :], mlp_w1_sb[:], edge_T[:, slot, :], start=True, stop=True
                   ).then_inc(hidden_done, 1)

            def edge_filter(g, slot):
                wait(pe, message_ready, g - 1)
                mm(ps_filter[:, slot, :], ones[0:1, :], mlp_b2_row[:].rearrange("a k f -> a (k f)"),
                   start=True, stop=False)
                wait(pe, hidden_ready, g + 1)
                for k in range(CHUNKS):
                    last = mm(ps_filter[:, slot, k * P:(k + 1) * P], hidden_T[:, slot, k, :],
                              mlp_w2_sb[:], start=False, stop=(k == CHUNKS - 1))
                last.then_inc(filter_ready, 1)

            def scales(c, j):
                wait(pe, diag_ready[c], j + 1)
                wait(pe, row_ready[c], j)
                mm(ps_node[:, 1, P:2 * P], ones[:], scale_diag[:], start=True, stop=True
                   ).then_inc(scale_done[c], 1)

            def node_1(j, part):
                if part == 0:
                    wait(pe, z_ready[1], j + 1)
                    for m in range(HM):
                        last = mm(ps_node[:, 0, m * P:(m + 1) * P], W1_sb[:, m * P:(m + 1) * P], z_T[:],
                                  start=True, stop=True)
                    last.then_inc(h_done, 1)
                if part == 1:
                    wait(pe, h_ready, j + 1)
                    wait(pe, row_ready[1], j)
                    for m in range(HM):
                        last = mm(ps_node[:, 1, 0:F], h_T[:, m, :], W2_sb[:, m, :],
                                  start=(m == 0), stop=(m == HM - 1))
                    last.then_inc(y_done, 1)
                    for m in range(HM):
                        last = mm(ps_node[:, 0, 0:P], W2_sb[:, m, :], h_T[:, m, :],
                                  start=(m == 0), stop=(m == HM - 1))
                    last.then_inc(y_T_done, 1)

            def node_2(j, part):
                if part == 0:
                    wait(pe, z_ready[2], j + 1)
                    wait(pe, row_ready[2], j)
                    turn(ps_node[:, 0, 0:P], z_T[:], ident[:]).then_inc(turned, 1)
                if part == 1:
                    wait(pe, z_row_ready, j + 1)
                    turn(ps_node[:, 1, 0:P], z_row[:], ident[:]).then_inc(z_turned, 1)
                if part == 2:
                    wait(pe, h2_ready, j + 1)
                    mm(ps_node[:, 0, 0:F], h2_T[:], lin1_sb[:], start=True, stop=True).then_inc(xf_done, 1)

            def node_3(j, part):
                if part == 0:
                    wait(pe, z_ready[3], j + 1)
                    mm(ps_node[:, 0, 0:P], lin2_sb[:], z_T[:], start=True, stop=True).then_inc(u_done, 1)
                if part == 1:
                    wait(pe, u_ready, j + 1)
                    wait(pe, row_ready[3], j)
                    mm(ps_node[:, 1, 0:F], z_row[:], lin_sb[:], start=True, stop=True).then_inc(v_done, 1)

            def count_chunk(q, slot):
                wait(pe, chunk_onehot, q + 1)
                wait(pe, chunk_added, 2 * q)
                hold(pe)
                n = HI_SPLIT * SPAN
                mm(ps_filter[:, 0, 0:n], lo_onehot[:, slot, :], code_onehot[:, slot, 0:n],
                   start=True, stop=True)
                mm(ps_filter[:, 1, 0:NB * SPAN - n], lo_onehot[:, slot, :], code_onehot[:, slot, n:],
                   start=True, stop=True).then_inc(chunk_summed, 1)

            def dense_product(c, k, slot):
                if isinstance(k, int) and k == 0:
                    pe.wait_ge(chunk_added, 2 * DENSE)
                wait(pe, parts_ready[c], 4 * (k + 1))
                first, last = (isinstance(k, int) and k == at for at in (0, NB - 1))
                for part in range(3):
                    for h, ps in ((0, ps_edge_T), (1, ps_hidden)):
                        done = mm(ps[:, 0:COLS // 2], table_parts[:, slot, part, :],
                                  adjacency[:, bass.ds(k, 1), h * COLS // 2:(h + 1) * COLS // 2]
                                  .rearrange("p a n -> p (a n)"),
                                  start=(first and part == 0), stop=(last and part == 2),
                                  skip_group_check=True)
                done.then_inc(block_used[c], 1)

            def fast_path():
                for c in (1, 2):
                    def update(n):
                        if c == 1:
                            scales(1, n)
                        for part in range(c + 1):
                            (node_1, node_2)[c - 1](n, part)

                    def body(i, j, stage):
                        for s in range(SLOTS):
                            g = SLOTS * i + s
                            if j is not None and s == 3 and c == 1:
                                node_1(j, 1)
                            wait(pe, gathered[c][s], 16 * CHUNKS * (i + 1))
                            wait(pe, flushed[c], g - 1)
                            sum_window(c, g, s)
                            if j is not None and s == 0 and c == 1:
                                scales(c, j)
                            if j is not None and s == 1:
                                (node_1, node_2)[c - 1](j, 0)
                            if j is not None and s == 3 and c == 2:
                                node_2(j, 1)
                                node_2(j, 2)
                            if counts_chunk(c, g, stage):
                                count_chunk(g - 1, (s - 1) % 2)
                            for slot, k in products_at(i, stage):
                                if slot == s:
                                    dense_product(c, k, s)
                        if has_extra(stage):
                            update(j + 1)
                    gcn_sweep(pe, body)
                    for n, j in GCN_TAIL:
                        update(n)

                edge_turn(0, 0, 0)
                edge_turn(1, 1, 0)
                edge_hidden(0, 0)

                def body(i, j):
                    for s in range(SLOTS):
                        g = SLOTS * i + s
                        if not (isinstance(g, int) and g + 2 >= NG):
                            edge_turn(g + 2, (s + 2) % SLOTS, i + (s + 2) // SLOTS)
                        if not (isinstance(g, int) and g + 1 >= NG):
                            edge_hidden(g + 1, (s + 1) % 2)
                        edge_filter(g, s % 2)
                        if not (isinstance(g, int) and g == 0):
                            wait(pe, message_ready, g)
                            wait(pe, flushed[3], g - 2)
                            sum_window(3, g - 1, (s - 1) % SLOTS)
                        if j is not None and s == 0:
                            scales(3, j)
                        if j is not None and s in (1, 2):
                            node_3(j, s - 1)
                sweep(pe, body)
                wait(pe, message_ready, NG)
                wait(pe, flushed[3], NG - 2)
                sum_window(3, NG - 1, SLOTS - 1)
                for j in TAIL_BLOCKS:
                    scales(3, j)
                    node_3(j, 0)
                    node_3(j, 1)

            def general_windows(c, g, s):
                with pe.Fori(0, NW) as w:
                    sum_window(c, g * NW + w, s)

            def general_path():
                for c in (1, 2, 3):
                    def body(i, j):
                        for s in range(SLOTS):
                            g = SLOTS * i + s
                            if c == 3:
                                edge_turn(g, s, i)
                                edge_hidden(g, s % 2)
                                edge_filter(g, s % 2)
                                wait(pe, message_ready, g + 1)
                            else:
                                wait(pe, gathered[c][s], 16 * CHUNKS * (i + 1))
                            hold(pe)
                            general_windows(c, g, s)
                    sweep(pe, body)

                    def body(j):
                        if c != 2:
                            scales(c, j)
                        for part in range((2, 3, 2)[c - 1]):
                            (node_1, node_2, node_3)[c - 1](j, part)
                    all_blocks(pe, body)

            branch(pe, fast_path, general_path)


_INS = ['x', 'src', 'dst', 'edge_attr_64', 'edge_weight', 'L0_gnn_W1', 'L0_gnn_b1', 'L0_gnn_W2', 'L0_gnn_b2',
        'L1_gnn_mlp_w1', 'L1_gnn_mlp_b1', 'L1_gnn_mlp_w2', 'L1_gnn_mlp_b2', 'L1_gnn_lin1_w', 'L1_gnn_lin2_w',
        'L1_gnn_lin2_b', 'L1_gnn_lin_w', 'L1_gnn_lin_b']


def kernel(**inputs):
    import numpy as _np
    import concourse.bacc as _bacc
    from concourse import mybir as _mybir
    from concourse.bass_utils import run_bass_kernel_spmd as _run

    nc = _bacc.Bacc("TRN2", target_bir_lowering=False, num_devices=1)
    arrays, args = {}, []
    for name in _INS:
        a = _np.ascontiguousarray(inputs[name])
        arrays[f"in_{name}_dram"] = a
        args.append(nc.dram_tensor(f"in_{name}_dram", a.shape, _mybir.dt.from_np(a.dtype), kind="ExternalInput").ap())
    shape = tuple(inputs['x'].shape)
    args.append(nc.dram_tensor("out_dram", shape, _mybir.dt.float32, kind="ExternalOutput").ap())
    gnn_kernel(nc, *args)
    r = _run(nc, [arrays], core_ids=[0])
    return r.results[0]["out_dram"]
```

```python
from contextlib import ExitStack

import concourse.bass as bass
from concourse import mybir

F32 = mybir.dt.float32
BF16 = mybir.dt.bfloat16
I32 = mybir.dt.int32
ALU = mybir.AluOpType
ACT = mybir.ActivationFunctionType
AX_X = mybir.AxisListType.X

P = 128
CHUNKS = 4
GROUP = CHUNKS * P
WINDOW = 64
SLOTS = 4
LAG = 5
LN_EPS = 1e-5
CUTOFF = 5.0
NO_NODE = 20000
BATCH = SLOTS * CHUNKS
PARTS = 7
DENSE_ITERS = 11
EXTRA = 10
SPAN = 12
DENSE_BLOCKS = 6
RATE = 8
TABLE_SLOTS = 4
TESTS = 11
WARM_UP = 16
CODE_ONE = 0x3F80
ROUND = 1.5 * 2.0 ** 23


def gnn_kernel(nc, x, src, dst, edge_attr, edge_weight, W1, b1, W2, b2,
               mlp_w1, mlp_b1, mlp_w2, mlp_b2, lin1_w, lin2_w, lin2_b, lin_w, lin_b, out):
    N, F = x.shape
    E, R = edge_attr.shape
    H = W1.shape[1]
    HM = H // P
    NG = -(-E // GROUP)
    HALF = NG // 2
    ITERS = NG // SLOTS
    NB = -(-N // P)
    LAST_ROWS = N - (NB - 1) * P
    NW = NB * P // WINDOW
    ACC = NB * P + WINDOW
    GCN_ITERS = ITERS - DENSE_ITERS
    DENSE = DENSE_ITERS * BATCH // 2
    PER_GROUP = (2, 2, 1)
    PRODUCT = NB // RATE
    DENSE_EDGES = E - GCN_ITERS * SLOTS * GROUP
    DENSE_FULL = DENSE_EDGES // P - DENSE
    DENSE_REST = DENSE_EDGES % P
    COLS = DENSE_BLOCKS * P
    ORIGIN = ((E - DENSE_EDGES + DENSE * P // 2) * N // E - COLS // 2 + SPAN // 2, NB * P - COLS)
    CLEARED_HERE = 22
    HI_SPLIT = -(-NB // 2)
    TAIL = E - (NG - 1) * GROUP
    assert F == P and NG == 2 * HALF == SLOTS * ITERS and NB % PARTS == 0 and ITERS % 2 == 0
    PART = (0, 1, 0)
    SETS = 3
    TAIL_SETS = 2
    assert GCN_ITERS - LAG == NB - EXTRA - TAIL_SETS - 1
    assert DENSE_REST and DENSE_FULL + 1 < DENSE <= HALF and N - 1 + SPAN <= NB * P
    assert NB == PRODUCT * RATE + 1 and DENSE % RATE == 0 and RATE == 2 * SLOTS
    assert RATE % TABLE_SLOTS == 0 and ORIGIN[0] + COLS > ORIGIN[1]
    assert HALF <= P and H == HM * P and N < NO_NODE - ACC and N % P

    with ExitStack() as ctx:
        def sb(name, shape, dt=F32):
            return ctx.enter_context(nc.sbuf_tensor(name, shape, dt))

        def psum(name, shape):
            return ctx.enter_context(nc.psum_tensor(name, shape, F32))

        def sem(name):
            return ctx.enter_context(nc.semaphore(name))

        table = [None] + [nc.dram_tensor(f"node_table_{c}", [NB * P, F], F32, kind="Internal").ap()
                          for c in (1, 2, 3)]

        early = ExitStack()

        def sb_early(name, shape, dt=F32):
            return early.enter_context(nc.sbuf_tensor(name, shape, dt))

        z_nodes = sb_early("z_nodes", [P, NB, F])
        turns = sb_early("turns", [P, NG, CHUNKS])
        code_iota_i = sb_early("code_iota_i", [P, NB * SPAN], I32)
        hist_lo = sb_early("hist_lo", [P, 2, P, BATCH], BF16)
        hist_hi = sb_early("hist_hi", [P, 2, NB, BATCH], BF16)
        iota_lo = sb_early("iota_lo", [P, P, BATCH], BF16)
        iota_lo_i = sb_early("iota_lo_i", [P, P, BATCH], I32)
        dst_lo = sb_early("dst_lo", [P, NG * CHUNKS], BF16)
        dst_hi = sb_early("dst_hi", [P, NG * CHUNKS], BF16)
        dst_T = sb_early("dst_T", [P, NG * CHUNKS], I32)
        part_i = sb_early("part_i", [P, NG * CHUNKS], I32)
        mean = sb_early("mean", [P, NB])
        minus_mean = sb_early("minus_mean", [P, NB])
        var = sb_early("var", [P, NB])
        row_scale = sb_early("row_scale", [P, NB])
        std = sb_early("std", [P, NB])
        weight_raw = sb_early("weight_raw", [HALF, 2, GROUP])
        rel_f = sb_early("rel_f", [HALF, 2, GROUP])
        src_f = sb_early("src_f", [HALF, 2, GROUP])
        dst_f = sb_early("dst_f", [HALF, 2, GROUP])
        src_raw = sb_early("src_raw", [HALF, 2, GROUP], I32)
        dst_raw = sb_early("dst_raw", [HALF, 2, GROUP], I32)
        dense_dst = sb_early("dense_dst", [DENSE, 2, P], I32)
        dense_src = sb_early("dense_src", [DENSE, 2, P], I32)
        dense_part = sb_early("dense_part", [DENSE, 2, P], I32)
        dense_dst_f = sb_early("dense_dst_f", [DENSE, 2, P])
        dense_rel = sb_early("dense_rel", [DENSE, 2, P])
        dense_lo = sb_early("dense_lo", [DENSE, 2, P])
        dense_hi = sb_early("dense_hi", [DENSE, 2, P])
        dense_code = sb_early("dense_code", [DENSE, 2, P])
        early.close()
        adjacency = sb("adjacency", [P, NB, COLS], BF16)
        edge_in = sb("edge_in", [P, SLOTS, CHUNKS, R])
        edge_T = sb("edge_T", [R, 2, GROUP])
        hidden_T = sb("hidden_T", [P, 2, CHUNKS, P])
        W1_T = sb("W1_T", [P, HM, P])
        table_in = sb("table_in", [P, TABLE_SLOTS, F])
        table_rest = sb("table_rest", [P, F])
        table_parts = sb("table_parts", [P, TABLE_SLOTS, 3, F], BF16)
        lo_onehot = sb("lo_onehot", [P, 4, P], BF16)
        code_onehot = sb("code_onehot", [P, 4, NB * SPAN], BF16)
        nodes = sb("nodes", [P, NB, F])
        acc = sb("acc", [P, ACC])
        degree = sb("degree", [P, NB])
        dinv = sb("dinv", [P, NB])
        inv_count = sb("inv_count", [P, NB])
        largest = sb("largest", [HALF, 2])
        base = sb("base", [HALF, 2])
        tests = sb("tests", [HALF, TESTS])
        group_id = sb("group_id", [HALF, 2], I32)
        earliest = sb("earliest", [HALF, 2])
        early_block = sb("early_block", [HALF, 2])
        totals = sb("totals", [P, 1])
        fast = sb("fast", [P, 1])
        fast_i = sb("fast_i", [1, 1], I32)
        base_i = sb("base_i", [1, NG], I32)
        rel = sb("rel", [P, NG, CHUNKS])
        src_idx = sb("src_idx", [P, NG, CHUNKS], I32)
        cutoff = sb("cutoff", [P, NG, CHUNKS])
        angle = sb("angle", [P, NG, CHUNKS])
        chunk_base = sb("chunk_base", [DENSE, 2])
        chunk_at = sb("chunk_at", [1, 2 * DENSE], I32)
        lo_T = sb("lo_T", [P, 2 * DENSE])
        code_T = sb("code_T", [P, 2 * DENSE], I32)
        lo_iota = sb("lo_iota", [P, P], BF16)
        code_iota = sb("code_iota", [P, NB * SPAN], BF16)
        idx_stage = sb("idx_stage", [P, SLOTS, CHUNKS], I32)
        ring = sb("ring", [P, SLOTS, CHUNKS, F])
        onehot = sb("onehot", [P, 2, CHUNKS, WINDOW])
        iota_i = sb("iota_i", [P, CHUNKS, WINDOW], I32)
        iota_f = sb("iota_f", [P, CHUNKS, WINDOW])
        iota_w = sb("iota_w", [P, CHUNKS, WINDOW])
        z_T = sb("z_T", [P, SETS, P])
        z_row = sb("z_row", [P, SETS, P])
        h2_T = sb("h2_T", [P, SETS, P])
        row_out = sb("row_out", [P, SETS, F])
        scale_diag = sb("scale_diag", [P, P])
        scale_all = sb("scale_all", [P, P])
        stats2 = sb("stats2", [P, SETS, 6])
        mv2 = sb("mv2", [P, SETS, 2])
        std2 = sb("std2", [P, SETS])
        rstd2 = sb("rstd2", [P, SETS])
        ident = sb("ident", [P, P])
        ones = sb("ones", [P, P])
        zeros = sb("zeros", [P, P])
        eps_col = sb("eps_col", [P, 1])
        half_pi = sb("half_pi", [P, 1])
        W1_sb = sb("W1_sb", [P, H])
        W12 = sb("W12", [P, F])
        b1_cols = sb("b1_cols", [P, HM, P])
        b12_all = sb("b12_all", [P, F])
        W2_sb = sb("W2_sb", [P, HM, F])
        b1_col = sb("b1_col", [P, HM])
        b2_all = sb("b2_all", [P, F])
        mlp_w1_sb = sb("mlp_w1_sb", [R, P])
        mlp_w2_sb = sb("mlp_w2_sb", [P, F])
        mlp_b1_col = sb("mlp_b1_col", [P, 1])
        mlp_b2_row = sb("mlp_b2_row", [1, CHUNKS, F])
        lin1_sb = sb("lin1_sb", [P, F])
        lin2_sb = sb("lin2_sb", [P, F])
        lin2_b_col = sb("lin2_b_col", [P, 1])
        lin_sb = sb("lin_sb", [P, F])
        lin_b_all = sb("lin_b_all", [P, F])

        ps_agg = psum("ps_agg", [P, 2, 512])
        ps_filter = psum("ps_filter", [P, 2, 512])
        ps_node = psum("ps_node", [P, 2, 512])
        ps_edge_T = psum("ps_edge_T", [P, 512])
        ps_hidden = psum("ps_hidden", [P, 512])

        padded = sem("padded")
        dst_loaded = sem("dst_loaded")
        dense_loaded = sem("dense_loaded")
        dense_ready = sem("dense_ready")
        dense_T_ready = sem("dense_T_ready")
        src_loaded = sem("src_loaded")
        weight_loaded = sem("weight_loaded")
        x_loaded = sem("x_loaded")
        params_loaded = sem("params_loaded")
        pool_consts = sem("pool_consts")
        consts_ready = sem("consts_ready")
        tests_ready = sem("tests_ready")
        totals_ready = sem("totals_ready")
        rel_ready = sem("rel_ready")
        src_f_ready = sem("src_f_ready")
        flag_ready = sem("flag_ready")
        base_rows_ready = sem("base_rows_ready")
        rel_T_ready = sem("rel_T_ready")
        src_T_ready = sem("src_T_ready")
        weight_T_ready = sem("weight_T_ready")
        indices_ready = sem("indices_ready")
        angle_ready = sem("angle_ready")
        sin_ready = sem("sin_ready")
        std_ready = sem("std_ready")
        minus_mean_ready = sem("minus_mean_ready")
        z_nodes_ready = sem("z_nodes_ready")
        dst_f_ready = sem("dst_f_ready")
        dst_T_ready = sem("dst_T_ready")
        dst_T_copied = sem("dst_T_copied")
        hist_iota = sem("hist_iota")
        hist_onehot = sem("hist_onehot")
        hist_summed = sem("hist_summed")
        degree_ready = sem("degree_ready")
        root_ready = sem("root_ready")
        table_ready = sem("table_ready")
        table_turned = sem("table_turned")
        start_ready = sem("start_ready")
        dve_chain = sem("dve_chain")
        act_chain = sem("act_chain")
        cutoff_ready = sem("cutoff_ready")
        cleared = sem("cleared")
        cleared_here = sem("cleared_here")
        chunk_onehot = sem("chunk_onehot")
        chunk_summed = sem("chunk_summed")
        chunk_added = sem("chunk_added")
        block_loaded = [None] + [[sem(f"block_loaded_{c}_{s}") for s in range(TABLE_SLOTS)] for c in (1, 2)]
        parts_ready = [None] + [sem(f"parts_ready_{c}") for c in (1, 2)]
        block_used = [None] + [sem(f"block_used_{c}") for c in (1, 2)]
        dense_added = [None] + [sem(f"dense_added_{c}") for c in (1, 2)]
        onehot_ready = [None] + [sem(f"onehot_ready_{c}") for c in (1, 2, 3)]
        summed = [None] + [sem(f"summed_{c}") for c in (1, 2, 3)]
        flushed = [None] + [sem(f"flushed_{c}") for c in (1, 2, 3)]
        staged = [None] + [sem(f"staged_{c}") for c in (1, 2, 3)]
        gathered = [None] + [[sem(f"gathered_{c}_{s}") for s in range(SLOTS)] for c in (1, 2, 3)]
        stored = [None] + [sem(f"stored_{c}") for c in (1, 2, 3)]
        edge_loaded = [sem(f"edge_loaded_{s}") for s in range(SLOTS)]
        edge_turned = sem("edge_turned")
        edge_T_ready = sem("edge_T_ready")
        hidden_done = sem("hidden_done")
        hidden_ready = sem("hidden_ready")
        filter_ready = sem("filter_ready")
        message_ready = sem("message_ready")
        z_ready = [None] + [sem(f"z_ready_{c}") for c in (1, 2, 3)]
        diag_ready = sem("diag_ready")
        scale_done = sem("scale_done")
        scale_ready = sem("scale_ready")
        W1_turned = sem("W1_turned")
        W1_T_ready = sem("W1_T_ready")
        b1_ready = sem("b1_ready")
        W12_done = sem("W12_done")
        W12_ready = sem("W12_ready")
        y_done = sem("y_done")
        y_T_done = sem("y_T_done")
        acc_reset = [None] + [sem(f"acc_reset_{c}") for c in (1, 2)]
        row_ready = [None] + [sem(f"row_ready_{c}") for c in (1, 2, 3)]
        turned = sem("turned")
        var2_ready = sem("var2_ready")
        std2_ready = sem("std2_ready")
        rstd2_ready = sem("rstd2_ready")
        z_row_ready = sem("z_row_ready")
        z_turned = sem("z_turned")
        h2_ready = sem("h2_ready")
        xf_done = sem("xf_done")
        u_done = sem("u_done")
        u_ready = sem("u_ready")
        v_done = sem("v_done")
        v_added = sem("v_added")
        out_stored = sem("out_stored")
        z_summed = sem("z_summed")
        z_scaled = sem("z_scaled")
        stats2_ready = sem("stats2_ready")
        held = sem("held")
        window_moved = [None] + [sem(f"window_moved_{c}") for c in (1, 2, 3)]

        def wait(eng, semaphore, count):
            if not (isinstance(count, int) and count <= 0):
                eng.wait_ge(semaphore, count)

        def hold(eng):
            eng.sem_inc(held, 1)

        def sweep(eng, body):
            body(0, None)
            with eng.Fori(1, LAG) as i:
                body(i, None)
            body(LAG, 0)
            with eng.Fori(LAG + 1, ITERS - 1) as i:
                body(i, i - LAG)
            body(ITERS - 1, ITERS - 1 - LAG)

        TAIL_BLOCKS = range(ITERS - LAG, NB)

        def gcn_plan(c):
            tasks = [[] for _ in range(GCN_ITERS)]
            others = [()] * GCN_ITERS

            def build(start, matrix, product):
                end = start + DENSE // (PER_GROUP[matrix] * SLOTS)
                tasks[start].append(("build first", start, matrix, product))
                for i in range(start + 1, end):
                    tasks[i].append(("build", start, matrix, product))
                tasks[end].append(("build last", start, matrix, product))
                multiply(end, matrix, product)
                return end

            def multiply(start, matrix, product):
                tasks[start].append(("multiply first", start, matrix, product))
                for i in range(start + 1, start + 1 + PRODUCT):
                    tasks[i].append(("multiply", start + 1, matrix, product))
                tasks[start + PRODUCT].append(("add", start, matrix, product))

            def other_blocks(start, blocks, each=1):
                for i in range(-(-len(blocks) // each)):
                    others[start + i] = tuple(b - start - i for b in blocks[i * each:(i + 1) * each])

            if c == 1:
                again = build(0, 0, 0) + PRODUCT + 1
                tasks[again].append(("clear", again, 1, 0))
                end = build(again + 1, 1, 1)
                before = ORIGIN[1] // P
                other_blocks(end + 1, range(NB - EXTRA, before))
                other_blocks(end + PRODUCT + 1, range(before, NB), each=2)
                assert before - NB + EXTRA <= PRODUCT
            else:
                multiply(0, 1, 0)
                again = PRODUCT + 1
                tasks[again].append(("clear", again, 2, 0))
                end = build(again + 1, 2, 1)
                beyond = -(-(ORIGIN[0] + COLS) // P)
                other_blocks(again + 1, range(beyond, NB))
                other_blocks(end + PRODUCT + 1, range(NB - EXTRA, beyond), each=2)
            assert not others[GCN_ITERS - 1]
            other_blocks(GCN_ITERS - 1, [NB - EXTRA - TAIL_SETS - 1])
            plan = []
            for i in range(GCN_ITERS):
                peeled = {0, 1, LAG, LAG + 1} | {step for name, start, *_ in tasks[i] if name == "multiply"
                                                 for step in (start, start + 1)}
                if plan and plan[-1][2:] == (tasks[i], others[i]) and i not in peeled:
                    plan[-1] = (plan[-1][0], i + 1, tasks[i], others[i])
                else:
                    plan.append((i, i + 1, tasks[i], others[i]))
            return plan

        def gcn_sweep(c, eng, body):
            n = 0
            for start, stop, tasks, others in gcn_plan(c):
                each = (start >= LAG) + len(others)

                def step(i):
                    k = n + each * (i - start)
                    body(i, ([(k, i - LAG, 0)] if start >= LAG else [])
                         + [(k + 1 + b, i + other, 1 + b) for b, other in enumerate(others)], tasks)
                if stop == start + 1:
                    step(start)
                else:
                    with eng.Fori(start, stop) as i:
                        step(i)
                n += each * (stop - start)

        def made_chunks(tasks, i, s, behind=0):
            chunks = []
            for name, start, matrix, product in tasks:
                if (name == "build" or name == "build first" and s >= behind
                        or name == "build last" and s < behind):
                    each = PER_GROUP[matrix]
                    for u in range(each):
                        q = each * (s - behind) + u - each * SLOTS * start
                        chunks.append((each * SLOTS * i + (matrix * DENSE + q),
                                       each * SLOTS * i + (PART[matrix] * DENSE + q),
                                       (each * (s - behind) + u) % 4, each))
            return chunks

        def multiplied_blocks(tasks, i, s):
            blocks = []
            for name, start, matrix, product in tasks:
                before = product * NB
                if name == "multiply first" and s == SLOTS - 1:
                    blocks.append((0, before, TABLE_SLOTS - 1, product * (1 + NB // TABLE_SLOTS)))
                if name == "multiply":
                    for u in (2 * s, 2 * s + 1):
                        k = RATE * i + (1 - RATE * start + u)
                        slot = u % TABLE_SLOTS
                        loads = RATE // TABLE_SLOTS * i + (u // TABLE_SLOTS - RATE // TABLE_SLOTS * start)
                        last = slot == TABLE_SLOTS - 1
                        blocks.append((k, k + before, slot, loads + (last + product * (last + NB // TABLE_SLOTS))))
            return blocks

        def find(tasks, name):
            return [task for task in tasks if task[0] == name]

        def count_banks(slot, each):
            return ((ps_filter[:, 0, :], ps_filter[:, 1, :]), (ps_edge_T[:], ps_hidden[:]))[slot % 2 if each == 2 else 1]

        def node_banks(b):
            return ((ps_node[:, 0, :], ps_node[:, 1, :]), (ps_filter[:, 0, :], ps_filter[:, 1, :]),
                    (ps_edge_T[:], ps_hidden[:]))[b]

        GCN_TAIL = [(NB - TAIL_SETS + b, NB - EXTRA - TAIL_SETS + b, b) for b in range(TAIL_SETS)]

        def all_blocks(eng, body):
            body(0)
            with eng.Fori(1, NB - 1) as j:
                body(j)
            body(NB - 1)

        def start_bank(q):
            return (ps_filter[:, 0, :], ps_filter[:, 1, :], ps_node[:, 0, :], ps_node[:, 1, :])[q % 4]

        def branch(eng, fast_path, general_path):
            eng.wait_ge(flag_ready, 1)
            flag = eng.value_load(fast_i[0:1, 0:1], min_val=0, max_val=1)
            with eng.If(flag > 0):
                fast_path()
            with eng.Else():
                general_path()

        block = ctx.enter_context(nc.Block())

        @block.sync
        def _(sp):
            def rows(v, lo, n):
                return v[lo * GROUP:(lo + n) * GROUP].rearrange("(g e) -> g e", e=GROUP)

            def one_row(v, lo, hi):
                return v[lo:hi].rearrange("(a e) -> a e", a=1)

            sp.dma_start(dst_raw[:, 0, :], rows(dst, 0, HALF)).then_inc(dst_loaded, 16)
            sp.wait_ge(padded, 1)
            sp.dma_start(dst_raw[0:HALF - 1, 1, :], rows(dst, HALF, HALF - 1)).then_inc(dst_loaded, 16)
            sp.dma_start(dst_raw[HALF - 1:HALF, 1, GROUP - TAIL:GROUP],
                         one_row(dst, E - TAIL, E)).then_inc(dst_loaded, 16)

            def chunks(v, part, n):
                first = E - DENSE_EDGES + part * DENSE * P
                return v[first:first + n * P].rearrange("(c e) -> c e", e=P)

            sp.wait_ge(padded, 3)
            for to, of in ((dense_dst, dst), (dense_src, src)):
                sp.dma_start(to[:, 0, :], chunks(of, 0, DENSE)).then_inc(dense_loaded, 16)
                sp.dma_start(to[0:DENSE_FULL, 1, :], chunks(of, 1, DENSE_FULL)).then_inc(dense_loaded, 16)
            sp.dma_start(dense_dst[DENSE_FULL:DENSE_FULL + 1, 1, P - DENSE_REST:P],
                         one_row(dst, E - DENSE_REST, E)).then_inc(dense_loaded, 16)
            sp.dma_start(dense_src[DENSE_FULL:DENSE_FULL + 1, 1, :],
                         one_row(src, E - P, E)).then_inc(dense_loaded, 16)
            sp.dma_start(src_raw[:, 0, :], rows(src, 0, HALF)).then_inc(src_loaded, 16)
            sp.dma_start(src_raw[0:HALF - 1, 1, :], rows(src, HALF, HALF - 1)).then_inc(src_loaded, 16)
            sp.dma_start(src_raw[HALF - 1:HALF, 1, :], one_row(src, E - GROUP, E)).then_inc(src_loaded, 16)
            sp.dma_start(weight_raw[:, 0, :], rows(edge_weight, 0, HALF)).then_inc(weight_loaded, 16)
            sp.dma_start(weight_raw[0:HALF - 1, 1, :],
                         rows(edge_weight, HALF, HALF - 1)).then_inc(weight_loaded, 16)
            sp.dma_start(weight_raw[HALF - 1:HALF, 1, :],
                         one_row(edge_weight, E - GROUP, E)).then_inc(weight_loaded, 16)

            n = NB // PARTS
            for i in range(PARTS):
                sp.wait_ge(table_ready, i + 1)
                sp.dma_start(table[1][i * n * P:(i + 1) * n * P, :].rearrange("(b p) f -> p b f", p=P),
                             z_nodes[:, i * n:(i + 1) * n, :]).then_inc(stored[1], 16)

            def store_rows(c, n, j, b=0):
                wait(sp, row_ready[c], n + 1)
                sp.dma_start(table[c + 1][bass.ds(j * P, P), :], row_out[:, b, :]).then_inc(stored[c + 1], 16)

            def store_out(j):
                wait(sp, row_ready[3], j + 1)
                n = LAST_ROWS if isinstance(j, int) and j == NB - 1 else P
                sp.dma_start(out[bass.ds(j * P, n), :], row_out[0:n, 0, :]).then_inc(out_stored, 16)

            def load_edges(i, s):
                g = SLOTS * i + s
                wait(sp, edge_turned, g - SLOTS + 1)
                first = min(g * GROUP, E - GROUP) if isinstance(g, int) else g * GROUP
                sp.dma_start(edge_in[:, s, :, :],
                             edge_attr[bass.ds(first, GROUP), :].rearrange("(p j) r -> p j r", j=CHUNKS)
                             ).then_inc(edge_loaded[s], 16)

            def fast_path():
                for c in (1, 2):
                    sp.wait_ge(stored[c], 16 * (PARTS if c == 1 else NB))

                    def body(i, updates, tasks):
                        for s in range(SLOTS):
                            for k, done, slot, loads in multiplied_blocks(tasks, i, s):
                                wait(sp, parts_ready[c], 4 * (done - TABLE_SLOTS + 1))
                                sp.dma_start(table_in[:, slot, :], table[c][bass.ds(k * P, P), :]
                                             ).then_inc(block_loaded[c][slot], 16)
                        for update in updates:
                            store_rows(c, *update)
                    gcn_sweep(c, sp, body)
                    for update in GCN_TAIL:
                        store_rows(c, *update)

                def body(i, j):
                    for s in range(SLOTS):
                        if s == 3 and j is not None and not (isinstance(j, int) and j == 0):
                            store_out(j - 1)
                        load_edges(i, s)
                sweep(sp, body)
                for j in range(ITERS - LAG - 1, NB):
                    store_out(j)

            def general_path():
                for c in (1, 2):
                    all_blocks(sp, lambda j: store_rows(c, j, j))

                def body(i, j):
                    for s in range(SLOTS):
                        load_edges(i, s)
                sweep(sp, body)
                all_blocks(sp, store_out)

            branch(sp, fast_path, general_path)
            sp.wait_ge(out_stored, 16 * NB)

        @block.gpsimd
        def _(pool):
            nc.gpsimd.iota(group_id[:], pattern=[[HALF, 2]], base=0, channel_multiplier=1)
            nc.gpsimd.iota(iota_i[:], pattern=[[0, CHUNKS], [1, WINDOW]], base=0,
                           channel_multiplier=0).then_inc(pool_consts, 1)
            nc.gpsimd.memset(ident[:], 0.0).then_inc(pool_consts, 1)
            pool.wait_ge(pool_consts, 2)
            nc.gpsimd.affine_select(out=ident[:], in_=ident[:], compare_op=ALU.not_equal, fill=1.0,
                                    base=0, pattern=[[-1, P]], channel_multiplier=1).then_inc(pool_consts, 1)

            nc.gpsimd.iota(iota_lo_i[:], pattern=[[1, P], [0, BATCH]], base=0,
                           channel_multiplier=0).then_inc(hist_iota, 1)
            nc.gpsimd.iota(code_iota_i[:], pattern=[[1, NB * SPAN]], base=CODE_ONE,
                           channel_multiplier=0).then_inc(hist_iota, 1)
            pool.wait_ge(minus_mean_ready, 1)
            nc.gpsimd.tensor_tensor(z_nodes[:], nodes[:], minus_mean[:].unsqueeze(2).to_broadcast([P, NB, F]), ALU.add
                                    ).then_inc(z_nodes_ready, 1)

            bound = pool.to_reg(NB * P - 1)

            def gather(c, i, s):
                wait(pool, staged[c], SLOTS * i + s + 1)
                hold(pool)
                for k in range(CHUNKS):
                    nc.gpsimd.indirect_dma_start(
                        ring[:, s, k, :], None, table[c],
                        bass.IndirectOffsetOnAxis(idx_stage[:, s, k:k + 1], 0),
                        bounds_check=bound, oob_is_err=False).then_inc(gathered[c][s], 16)

            def gathers(c, iterations):
                pool.wait_ge(stored[c], 16 * (PARTS if c == 1 else NB))
                with pool.Fori(0, iterations) as i:
                    for s in range(SLOTS):
                        gather(c, i, s)

            def fast_path():
                for c, iterations in ((1, GCN_ITERS), (2, GCN_ITERS), (3, ITERS)):
                    gathers(c, iterations)

            def general_path():
                for c in (1, 2, 3):
                    gathers(c, ITERS)

            branch(pool, fast_path, general_path)

        @block.scalar
        def _(act):
            def params(o, i, **kw):
                act.dma_start(o, i, **kw).then_inc(params_loaded, 16)

            def column(v, cols=1):
                return v.rearrange("(m p) -> p m", p=P)

            def row(v):
                return v.rearrange("(a f) -> a f", a=1)

            act.dma_start(nodes[:, 0:NB - 1, :],
                          x[0:(NB - 1) * P, :].rearrange("(b p) f -> p b f", p=P)).then_inc(x_loaded, 16)
            act.wait_ge(consts_ready, 1)
            act.dma_start(nodes[0:LAST_ROWS, NB - 1, :], x[(NB - 1) * P:N, :]).then_inc(x_loaded, 16)
            params(W1_sb[:], W1)
            params(W2_sb[:], W2.rearrange("(m p) f -> p m f", p=P))
            params(b1_col[:], column(b1), allow_slow_non_contiguous=True)
            params(b2_all[:], b2.partition_broadcast(P))
            params(mlp_w1_sb[:], mlp_w1)
            params(mlp_w2_sb[:], mlp_w2)
            params(mlp_b1_col[:], column(mlp_b1), allow_slow_non_contiguous=True)
            for k in range(CHUNKS):
                params(mlp_b2_row[:, k, :], row(mlp_b2))
            params(lin1_sb[:], lin1_w)
            params(lin2_sb[:], lin2_w)
            params(lin2_b_col[:], column(lin2_b), allow_slow_non_contiguous=True)
            params(lin_sb[:], lin_w)
            params(lin_b_all[:], lin_b.partition_broadcast(P))

            def halves(semaphore, ps, to):
                for t in range(2):
                    act.wait_ge(semaphore, t + 1)
                    last = nc.scalar.copy(
                        to[:, t * HALF:(t + 1) * HALF, :].rearrange("p g k -> p k g"),
                        ps[:, t, 0:CHUNKS * HALF].rearrange("p (k g) -> p k g", k=CHUNKS))
                return last

            halves(dst_T_ready, ps_agg, dst_T[:].rearrange("p (g k) -> p g k", k=CHUNKS)
                   ).then_inc(dst_T_copied, 1)
            act.wait_ge(hist_iota, 2)
            nc.scalar.copy(iota_lo[:], iota_lo_i[:]).then_inc(hist_iota, 1)
            halves(rel_T_ready, ps_filter, rel).then_inc(indices_ready, 1)
            halves(src_T_ready, ps_node, src_idx).then_inc(indices_ready, 1)
            halves(weight_T_ready, ps_agg, angle).then_inc(angle_ready, 1)
            scratch = acc[:, 0:NB * P].rearrange("p (b f) -> p b f", f=F)
            act.wait_ge(x_loaded, 32)
            for b in range(NB):
                last = nc.scalar.activation(scratch[:, b, :], nodes[:, b, :], ACT.Identity,
                                            accum_out=mean[:, b:b + 1])
            last.then_inc(act_chain, 1)
            act.wait_ge(act_chain, 1)
            nc.scalar.mul(minus_mean[:], mean[:], -1.0 / F).then_inc(minus_mean_ready, 1)
            act.wait_ge(minus_mean_ready, 1)
            for b in range(NB):
                last = nc.scalar.activation(scratch[:, b, :], nodes[:, b, :], ACT.Square,
                                            bias=minus_mean[:, b:b + 1], accum_out=var[:, b:b + 1])
            last.then_inc(act_chain, 1)
            act.wait_ge(act_chain, 2)
            nc.scalar.activation(std[:], var[:], ACT.Sqrt, bias=eps_col[:, 0:1], scale=1.0 / F
                                 ).then_inc(std_ready, 1)

            def node_2(n, part, b=0):
                bank0, bank1 = node_banks(b)
                if part == 0:
                    wait(act, var2_ready, n + 1)
                    nc.scalar.activation(std2[:, b:b + 1], mv2[:, b, 1:2], ACT.Sqrt, bias=eps_col[:, 0:1]
                                         ).then_inc(std2_ready, 1)
                if part == 1:
                    wait(act, z_turned, n + 1)
                    nc.scalar.activation(h2_T[:, b, :], bank1[:, 0:P], ACT.Relu).then_inc(h2_ready, 1)
                if part == 2:
                    wait(act, xf_done, n + 1)
                    wait(act, stored[3], 16 * (n - b))
                    nc.scalar.copy(row_out[:, b, :], bank0[:, 0:F]).then_inc(row_ready[2], 1)

            def node_3(j):
                wait(act, scale_done, j + 1)
                nc.scalar.copy(scale_all[:], ps_node[:, 1, P:2 * P]).then_inc(scale_ready, 1)
                wait(act, u_done, j + 1)
                nc.scalar.activation(z_row[:, 0, :], ps_node[:, 0, 0:P], ACT.Silu, bias=lin2_b_col[:, 0:1]
                                     ).then_inc(u_ready, 1)

            def edge_copy(g, slot):
                wait(act, edge_turned, g + 1)
                nc.scalar.copy(edge_T[:, slot, :], ps_edge_T[0:R, :]).then_inc(edge_T_ready, 1)

            def edge_silu(g, slot):
                wait(act, filter_ready, g - 1)
                wait(act, hidden_done, g + 1)
                nc.scalar.activation(hidden_T[:, slot, :, :],
                                     ps_hidden[:, :].rearrange("p (k e) -> p k e", k=CHUNKS),
                                     ACT.Silu, bias=mlp_b1_col[:, 0:1]).then_inc(hidden_ready, 1)

            act.wait_ge(degree_ready, 1)
            nc.scalar.activation(dinv[:], degree[:], ACT.Sqrt).then_inc(root_ready, 1)
            for q in range(-(-NB // 4)):
                act.wait_ge(table_turned, q + 1)
                n = min(4, NB - 4 * q) * P
                nc.scalar.copy(acc[:, 4 * q * P:4 * q * P + n], start_bank(q)[:, 0:n]
                               ).then_inc(start_ready, 1)

            act.wait_ge(angle_ready, 2)
            nc.scalar.activation(angle[:], angle[:], ACT.Sin, bias=half_pi[:, 0:1],
                                 scale=-6.283185307179586).then_inc(sin_ready, 1)
            act.wait_ge(params_loaded, 16 * 16)

            act.wait_ge(W1_turned, 1)
            nc.scalar.copy(W1_T[:], ps_agg[:, 0, 0:H].rearrange("p (m i) -> p m i", m=HM)).then_inc(W1_T_ready, 1)
            act.wait_ge(W12_done, 1)
            nc.scalar.copy(W12[:], ps_agg[:, 1, 0:F])
            nc.scalar.copy(b12_all[:], ps_agg[:, 1, F:2 * F]).then_inc(W12_ready, 1)

            def fast_path():
                def clear():
                    nc.scalar.copy(adjacency[:, CLEARED_HERE:, :].rearrange("p b n -> p (b n)"),
                                   zeros[:, 0:1].to_broadcast([P, (NB - CLEARED_HERE) * COLS])).then_inc(cleared, 1)

                act.wait_ge(stored[1], 16 * PARTS)
                act.wait_ge(cutoff_ready, 1)
                clear()

                for c in (1, 2):
                    def body(i, updates, tasks):
                        if find(tasks, "clear"):
                            act.wait_ge(dense_added[c], 2)
                            clear()
                        if c == 2:
                            for part in range(3):
                                for n, j, b in updates:
                                    node_2(n, part, b)
                    gcn_sweep(c, act, body)
                for part in range(3):
                    for n, j, b in GCN_TAIL:
                        node_2(n, part, b)

                edge_copy(0, 0)
                edge_copy(1, 1)
                edge_silu(0, 0)

                def body(i, j):
                    for s in range(SLOTS):
                        g = SLOTS * i + s
                        if not (isinstance(g, int) and g + 2 >= NG):
                            edge_copy(g + 2, s % 2)
                        if not (isinstance(g, int) and g + 1 >= NG):
                            edge_silu(g + 1, (s + 1) % 2)
                        if s == 1 and j is not None:
                            node_3(j)
                sweep(act, body)
                for j in TAIL_BLOCKS:
                    node_3(j)

            def general_path():
                def body(j):
                    for part in range(3):
                        node_2(j, part)
                all_blocks(act, body)

                def body(i, j):
                    for s in range(SLOTS):
                        g = SLOTS * i + s
                        edge_copy(g, s % 2)
                        edge_silu(g, s % 2)
                sweep(act, body)
                all_blocks(act, node_3)

            branch(act, fast_path, general_path)

        @block.vector
        def _(dve):
            chain = [0]

            def link(ins):
                chain[0] += 1
                ins.then_inc(dve_chain, 1)
                dve.wait_ge(dve_chain, chain[0])

            vec = nc.vector
            vec.memset(dst_raw[:, 1, :], NO_NODE).then_inc(padded, 1)
            vec.memset(dense_dst[:], NO_NODE).then_inc(padded, 1)
            vec.memset(dense_src[:], 0).then_inc(padded, 1)
            vec.memset(nodes[:, NB - 1, :], 0.0).then_inc(consts_ready, 1)
            vec.memset(tests[:], 0.0)
            vec.memset(ones[:], 1.0)
            vec.memset(zeros[:], 0.0)
            vec.memset(eps_col[:], LN_EPS)
            vec.memset(half_pi[:], 1.5707963267948966)
            vec.memset(acc[:, NB * P:], 0.0)
            dve.wait_ge(pool_consts, 1)
            vec.tensor_copy(iota_f[:], iota_i[:]).then_inc(consts_ready, 1)
            link(vec.tensor_scalar(group_id[:], group_id[:], SLOTS.bit_length() - 1, P.bit_length() - 1,
                                   ALU.arith_shift_right, ALU.logical_shift_left))
            link(vec.tensor_scalar(earliest[:], group_id[:], float(-P * (LAG - 1)), None, ALU.add))
            link(vec.tensor_scalar(early_block[:], group_id[:], P * (GCN_ITERS - 1), float(P), ALU.is_equal, ALU.mult))
            link(vec.tensor_tensor(earliest[:], earliest[:], early_block[:], ALU.add))

            dve.wait_ge(dst_loaded, 48)
            vec.tensor_copy(dst_f[:], dst_raw[:]).then_inc(dst_f_ready, 1)
            dve.wait_ge(dst_f_ready, 1)
            link(vec.tensor_reduce(base[:], dst_f[:], AX_X, ALU.min))
            for t in range(2):
                link(vec.tensor_scalar(rel_f[:, t, :], dst_f[:, t, :], base[:, t:t + 1], None, ALU.subtract))
                vec.tensor_scalar(rel_f[:, t, :], rel_f[:, t, :], float(WINDOW), 0.0, ALU.is_lt, ALU.add,
                                  accum_out=tests[:, t:t + 1])
            vec.tensor_tensor(tests[:, 2:4], base[:], earliest[:], ALU.is_ge)
            link(vec.tensor_reduce(largest[:], dst_f[:], AX_X, ALU.max))
            for t, n in ((0, HALF), (1, GCN_ITERS * SLOTS - HALF)):
                vec.tensor_scalar(tests[0:n, 4 + t:5 + t], largest[0:n, t:t + 1],
                                  float((NB - EXTRA) * P), None, ALU.is_lt)
            dve.wait_ge(dense_loaded, 96)
            link(vec.tensor_copy(dense_dst_f[:], dense_dst[:]))
            link(vec.tensor_reduce(chunk_base[:], dense_dst_f[:], AX_X, ALU.min))
            link(vec.tensor_scalar(chunk_base[:], chunk_base[:], float(N - 1), None, ALU.min))
            for t in range(2):
                link(vec.tensor_scalar(dense_rel[:, t, :], dense_dst_f[:, t, :], chunk_base[:, t:t + 1], None,
                                       ALU.subtract))
                vec.tensor_scalar(dense_code[:, t, :], dense_rel[:, t, :], float(SPAN), 0.0, ALU.is_lt, ALU.add,
                                  accum_out=tests[0:DENSE, 6 + t:7 + t])
                vec.tensor_scalar(tests[0:DENSE, 8 + t:9 + t], chunk_base[:, t:t + 1], float(ORIGIN[t]), None,
                                  ALU.is_ge)
            vec.tensor_scalar(tests[0:DENSE, 10:11], chunk_base[:, 0:1], float(ORIGIN[0] + COLS - SPAN), None,
                              ALU.is_le).then_inc(tests_ready, 1)
            link(vec.tensor_scalar(dense_part[:], dense_src[:], P - 1, None, ALU.bitwise_and))
            link(vec.tensor_copy(dense_lo[:], dense_part[:]))
            link(vec.tensor_scalar(dense_part[:], dense_src[:], P.bit_length() - 1, None, ALU.arith_shift_right))
            link(vec.tensor_copy(dense_hi[:], dense_part[:]))
            vec.scalar_tensor_tensor(out=dense_code[:], in0=dense_hi[:], scalar=float(SPAN), in1=dense_rel[:],
                                     op0=ALU.mult, op1=ALU.add).then_inc(dense_ready, 1)
            dve.wait_ge(src_loaded, 48)
            vec.tensor_copy(src_f[:], src_raw[:]).then_inc(src_f_ready, 1)
            dve.wait_ge(totals_ready, 1)
            link(vec.tensor_reduce(totals[:], ps_edge_T[:, 0:TESTS], AX_X, ALU.add))
            link(vec.tensor_scalar(fast[:], totals[:], float(E + NG + GCN_ITERS * SLOTS + DENSE_EDGES + 3 * DENSE),
                                   None, ALU.is_equal))
            vec.tensor_copy(fast_i[:], fast[0:1, :])
            link(vec.tensor_scalar(base[:], base[:], fast[0:HALF, 0:1], None, ALU.mult))
            for t in range(2):
                last = vec.tensor_scalar(rel_f[:, t, :], dst_f[:, t, :], base[:, t:t + 1], None, ALU.subtract)
            last.then_inc(rel_ready, 1)
            dve.wait_ge(base_rows_ready, 1)
            for t in range(2):
                link(vec.tensor_scalar(chunk_at[:, t * DENSE:(t + 1) * DENSE],
                                       ps_hidden[0:1, NG + t * DENSE:NG + (t + 1) * DENSE],
                                       float(ORIGIN[t]), None, ALU.subtract))
            vec.tensor_copy(base_i[:], ps_hidden[0:1, 0:NG]).then_inc(flag_ready, 1)

            dve.wait_ge(dense_T_ready, 1)
            n = 2 * DENSE
            vec.tensor_copy(lo_T[:], ps_edge_T[:, 512 - 2 * n:512 - n])
            link(vec.tensor_scalar(code_T[:], ps_edge_T[:, 512 - n:512], float(CODE_ONE), None, ALU.add))
            link(vec.tensor_scalar(code_T[:], code_T[:], 16, None, ALU.logical_shift_left))

            dve.wait_ge(dst_T_copied, 1)
            link(vec.tensor_scalar(part_i[:], dst_T[:], P - 1, None, ALU.bitwise_and))
            link(vec.tensor_copy(dst_lo[:], part_i[:]))
            link(vec.tensor_scalar(part_i[:], dst_T[:], P.bit_length() - 1, None, ALU.arith_shift_right))
            link(vec.tensor_copy(dst_hi[:], part_i[:]))

            dve.wait_ge(hist_iota, 3)
            vec.tensor_copy(lo_iota[:], iota_lo[:, :, 0])
            link(vec.tensor_scalar(code_iota_i[:], code_iota_i[:], 16, None, ALU.logical_shift_left))
            link(vec.tensor_copy(code_iota[:], code_iota_i[:].bitcast(F32)))

            def hist_batch(b, slot):
                wait(dve, hist_summed, b - 1)
                for to, of, rows in ((hist_lo, dst_lo, P), (hist_hi, dst_hi, NB)):
                    last = vec.tensor_tensor(
                        to[:, slot, :, :], iota_lo[:, 0:rows, :],
                        of[:, bass.ds(b * BATCH, BATCH)].unsqueeze(1).to_broadcast([P, rows, BATCH]),
                        ALU.is_equal)
                last.then_inc(hist_onehot, 1)

            for slot in range(2):
                hist_batch(slot, slot)
            with dve.Fori(1, ITERS // 2) as i:
                for slot in range(2):
                    hist_batch(2 * i + slot, slot)

            dve.wait_ge(hist_summed, ITERS)
            link(vec.tensor_copy(inv_count[:], ps_hidden[:, 0:NB]))
            vec.tensor_scalar(degree[:], inv_count[:], 1.0, None, ALU.add).then_inc(degree_ready, 1)
            dve.wait_ge(root_ready, 1)
            link(vec.reciprocal(dinv[:], dinv[:]))
            dve.wait_ge(std_ready, 1)
            link(vec.reciprocal(row_scale[:], std[:]))
            link(vec.tensor_tensor(row_scale[:], row_scale[:], dinv[:], ALU.mult))
            dve.wait_ge(z_nodes_ready, 1)
            n = NB // PARTS
            for i in range(PARTS):
                zi = z_nodes[:, i * n:(i + 1) * n, :]
                vec.scalar_tensor_tensor(
                    out=zi, in0=zi, scalar=0.0,
                    in1=row_scale[:, i * n:(i + 1) * n].unsqueeze(2).to_broadcast([P, n, F]),
                    op0=ALU.max, op1=ALU.mult).then_inc(table_ready, 1)
            link(vec.tensor_scalar(inv_count[:], inv_count[:], 1.0, None, ALU.max))
            link(vec.reciprocal(inv_count[:], inv_count[:]))
            dve.wait_ge(indices_ready, 2)

            def make_onehot(c, g, slot, iota):
                vec.tensor_tensor(onehot[:, slot, :, :], iota[:],
                                  rel[:, bass.ds(g, 1), :].rearrange("p a k -> p (a k)").unsqueeze(2)
                                  .to_broadcast([P, CHUNKS, WINDOW]),
                                  ALU.is_equal).then_inc(onehot_ready[c], 1)

            def flush(c, g, slot, at, before):
                wait(dve, flushed[c], before)
                wait(dve, summed[c], before + 1)
                to = acc[:, bass.ds(at, WINDOW)]
                vec.tensor_tensor(to, to, ps_agg[:, slot, 0:WINDOW], ALU.add).then_inc(flushed[c], 1)

            def stage_indices(c, g, s):
                vec.tensor_copy(idx_stage[:, s, :].unsqueeze(1), src_idx[:, bass.ds(g, 1), :]
                                ).then_inc(staged[c], 1)

            def message(i, s):
                g = SLOTS * i + s
                wait(dve, gathered[3][s], 16 * CHUNKS * (i + 1))
                wait(dve, filter_ready, g + 1)
                for k in range(CHUNKS):
                    last = vec.scalar_tensor_tensor(
                        out=ring[:, s, k, :], in0=ps_filter[:, s % 2, k * P:(k + 1) * P],
                        scalar=cutoff[:].rearrange("p g k -> p (g k)")[:, bass.ds(g * CHUNKS + k, 1)],
                        in1=ring[:, s, k, :], op0=ALU.mult, op1=ALU.mult)
                last.then_inc(message_ready, 1)

            def fast_flush(c, g, s):
                at = nc.values_load(base_i[0:1, bass.ds(g, 1)], engines=[mybir.EngineType.DVE],
                                    min_val=0, max_val=N - 1,
                                    skip_runtime_bounds_check_because="a group's smallest dst is a node")
                flush(c, g, s % 2, at, g)

            def general_windows(c, g, s):
                wait(dve, window_moved[c], g * (NW + 1))
                vec.tensor_copy(iota_w[:], iota_f[:]).then_inc(window_moved[c], 1)
                with dve.Fori(0, NW) as w:
                    n = g * NW + w
                    dve.wait_ge(window_moved[c], n + g + 1)
                    make_onehot(c, g, s % 2, iota_w)
                    dve.wait_ge(summed[c], n + 1)
                    to = acc[:, bass.ds(w * WINDOW, WINDOW)]
                    vec.tensor_tensor(to, to, ps_agg[:, s % 2, 0:WINDOW], ALU.add).then_inc(flushed[c], 1)
                    vec.tensor_scalar(iota_w[:], iota_w[:], float(WINDOW), None, ALU.add
                                      ).then_inc(window_moved[c], 1)

            def chunk_matrices(done, q, slot, each):
                wait(dve, chunk_summed, done - 3)
                vec.tensor_scalar(lo_onehot[:, slot, :], lo_iota[:], lo_T[:, bass.ds(q, 1)], None, ALU.is_equal)
                vec.tensor_scalar(code_onehot[:, slot, :], code_iota[:],
                                  code_T[:].bitcast(F32)[:, bass.ds(q, 1)], None, ALU.is_equal
                                  ).then_inc(chunk_onehot, 1)

            def chunk_columns(chunks):
                if not chunks:
                    return []
                _, at = nc.values_load_multi_w_load_instructions(
                    chunk_at[0:1, bass.ds(chunks[0][1], len(chunks))], engines=[mybir.EngineType.DVE],
                    min_val=0, max_val=COLS - SPAN,
                    skip_runtime_bounds_check_because="the fast path has been tested for it")
                return at

            def add_chunk(done, q, slot, each, at):
                wait(dve, chunk_summed, done + 1)
                wait(dve, chunk_added, 2 * done)
                for (lo, hi), ps in zip(((0, HI_SPLIT), (HI_SPLIT, NB)), count_banks(slot, each)):
                    to = adjacency[:, lo:hi, bass.ds(at, SPAN)]
                    vec.tensor_tensor(to, to, ps[:, 0:(hi - lo) * SPAN]
                                      .rearrange("p (b n) -> p b n", n=SPAN), ALU.add).then_inc(chunk_added, 1)

            def split_block(c, k, done, slot, loads):
                high, middle, low = (table_parts[:, slot, part, :] for part in range(3))
                wait(dve, block_loaded[c][slot], 16 * (loads + 1))
                wait(dve, block_used[c], done - TABLE_SLOTS + 1)
                vec.tensor_copy(high, table_in[:, slot, :]).then_inc(parts_ready[c], 1)
                wait(dve, parts_ready[c], 4 * done + 1)
                vec.tensor_tensor(table_rest[:], table_in[:, slot, :], high, ALU.subtract
                                  ).then_inc(parts_ready[c], 1)
                wait(dve, parts_ready[c], 4 * done + 2)
                vec.tensor_copy(middle, table_rest[:]).then_inc(parts_ready[c], 1)
                wait(dve, parts_ready[c], 4 * done + 3)
                vec.tensor_tensor(low, table_rest[:], middle, ALU.subtract).then_inc(parts_ready[c], 1)

            def add_dense(c, matrix, product):
                dve.wait_ge(block_used[c], NB * (product + 1))
                for h, ps in ((0, ps_edge_T), (1, ps_hidden)):
                    first = ORIGIN[PART[matrix]] + h * COLS // 2
                    to = acc[:, first:first + COLS // 2]
                    vec.tensor_tensor(to, to, ps[:, 0:COLS // 2], ALU.add).then_inc(dense_added[c], 1)
                dve.wait_ge(dense_added[c], 2 * (product + 1))

            def clear():
                vec.memset(adjacency[:, 0:CLEARED_HERE, :], 0.0).then_inc(cleared_here, 1)

            def columns(tile, j):
                return tile[:, bass.ds(j * P, P)]

            def node_1(n, j, part, b=0):
                bank0, bank1 = node_banks(b)
                if part == 0:
                    vec.tensor_scalar(z_T[:, b, :], columns(acc, j), 1.0, None, ALU.mult
                                      ).then_inc(z_ready[1], 1)
                if part == 1:
                    wait(dve, y_done, n + 1)
                    wait(dve, stored[2], 16 * (n - b))
                    vec.scalar_tensor_tensor(out=z_row[:, b, :], in0=bank0[:, 0:F],
                                             scalar=dinv[:, bass.ds(j, 1)], in1=b12_all[:],
                                             op0=ALU.mult, op1=ALU.add).then_inc(z_scaled, 1)
                    wait(dve, z_scaled, n + 1)
                    hold(dve)
                    vec.tensor_scalar(row_out[:, b, :], z_row[:, b, :], dinv[:, bass.ds(j, 1)], None, ALU.mult
                                      ).then_inc(row_ready[1], 1)
                if part == 2:
                    wait(dve, y_T_done, n + 1)
                    vec.tensor_scalar(columns(acc, j), bank1[:, 0:P], 1.0, None, ALU.mult
                                      ).then_inc(acc_reset[1], 1)

            def node_2(n, j, part, b=0):
                bank0, bank1 = node_banks(b)
                zb, mean_b, var_b = z_row[:, b, :], mv2[:, b, 0:1], mv2[:, b, :]
                if part == 0:
                    vec.tensor_scalar(z_T[:, b, :], columns(acc, j), 1.0, None, ALU.mult
                                      ).then_inc(z_ready[2], 1)
                    wait(dve, z_ready[2], n + 1)
                    vec.tensor_scalar(columns(acc, j), zeros[:], 1.0, None, ALU.mult).then_inc(acc_reset[2], 1)
                if part == 1:
                    wait(dve, turned, n + 1)
                    xj = nodes[:, bass.ds(j, 1), :].rearrange("p a f -> p (a f)")
                    vec.scalar_tensor_tensor(out=zb, in0=bank0[:, 0:F],
                                             scalar=dinv[:, bass.ds(j, 1)], in1=b2_all[:],
                                             op0=ALU.mult, op1=ALU.add).then_inc(z_summed, 1)
                    wait(dve, z_summed, 2 * n + 1)
                    vec.tensor_tensor(zb, zb, xj, ALU.add).then_inc(z_summed, 1)
                    wait(dve, z_summed, 2 * n + 2)
                    vec.tensor_scalar(xj, zb, 1.0, None, ALU.mult)
                    vec.bn_stats(stats2[:, b, :], zb).then_inc(stats2_ready, 1)
                    wait(dve, stats2_ready, n + 1)
                    hold(dve)
                    vec.bn_aggr(var_b, stats2[:, b, :]).then_inc(var2_ready, 1)
                if part == 2:
                    wait(dve, std2_ready, n + 1)
                    vec.reciprocal(rstd2[:, b:b + 1], std2[:, b:b + 1]).then_inc(rstd2_ready, 1)
                    wait(dve, rstd2_ready, n + 1)
                    vec.tensor_scalar(zb, zb, mean_b, rstd2[:, b:b + 1],
                                      ALU.subtract, ALU.mult).then_inc(z_row_ready, 1)

            def diagonal(j):
                vec.tensor_scalar(scale_diag[:], ident[:], inv_count[:, bass.ds(j, 1)], None, ALU.mult
                                  ).then_inc(diag_ready, 1)

            def node_3(j, part):
                if part == 0:
                    wait(dve, scale_ready, j + 1)
                    vec.tensor_tensor(z_T[:, 0, :], columns(acc, j), scale_all[:], ALU.mult
                                      ).then_inc(z_ready[3], 1)
                if part == 1:
                    wait(dve, v_done, j + 1)
                    wait(dve, out_stored, 16 * j)
                    xj = nodes[:, bass.ds(j, 1), :].rearrange("p a f -> p (a f)")
                    vec.tensor_tensor(row_out[:, 0, :], ps_node[:, 1, 0:F], lin_b_all[:], ALU.add
                                      ).then_inc(v_added, 1)
                    wait(dve, v_added, j + 1)
                    vec.tensor_tensor(row_out[:, 0, :], row_out[:, 0, :], xj, ALU.add).then_inc(row_ready[3], 1)

            def fast_path():
                dve.wait_ge(stored[1], 16 * PARTS)
                clear()
                for c in (1, 2):
                    node = (node_1, node_2)[c - 1]

                    def body(i, updates, tasks):
                        def update(part):
                            for n, j, b in updates:
                                node(n, j, part, b)

                        for s in range(SLOTS):
                            g = SLOTS * i + s
                            if s == 2:
                                update(1)
                            if s == 3 and c == 2:
                                update(2)
                            chunks = made_chunks(tasks, i, s, behind=2)
                            if s == 2:
                                for name, start, matrix, product in find(tasks, "build first"):
                                    dve.wait_ge(cleared, matrix + 1)
                                    dve.wait_ge(cleared_here, matrix + 1)
                            for chunk, at in zip(chunks, chunk_columns(chunks)):
                                add_chunk(*chunk, at)
                            for table_block in multiplied_blocks(tasks, i, s):
                                split_block(c, *table_block)
                            fast_flush(c, g, s)
                            if not (isinstance(i, int) and i == GCN_ITERS - 1):
                                stage_indices(c, g + SLOTS, s)
                            if not (isinstance(g, int) and g == SLOTS * GCN_ITERS - 1):
                                make_onehot(c, g + 1, (s + 1) % 2, iota_f)
                            if updates and s == 0:
                                wait(dve, flushed[c], g + 1)
                                update(0)
                            if s == 3 and c == 1:
                                update(2)
                            for chunk in made_chunks(tasks, i, s):
                                chunk_matrices(*chunk)
                        for name, start, matrix, product in find(tasks, "add"):
                            add_dense(c, matrix, product)
                        if find(tasks, "clear"):
                            clear()
                    make_onehot(c, 0, 0, iota_f)
                    gcn_sweep(c, dve, body)
                    dve.wait_ge(flushed[c], GCN_ITERS * SLOTS)
                    for part in range(3):
                        for n, j, b in GCN_TAIL:
                            node(n, j, part, b)
                        if part == 0:
                            for s in range(SLOTS - (c == 2)):
                                stage_indices(c + 1, s, s)
                    dve.wait_ge(acc_reset[c], NB)

                def body(i, j):
                    for s in range(SLOTS):
                        g = SLOTS * i + s
                        if j is not None and s == 0:
                            diagonal(j)
                        if j is not None and s == 3:
                            node_3(j, 1)
                        make_onehot(3, g, s % 2, iota_f)
                        message(i, s)
                        if not (isinstance(g, int) and g == 0):
                            fast_flush(3, g - 1, s - 1)
                        if not (isinstance(g, int) and g + SLOTS - 1 >= NG):
                            stage_indices(3, g + SLOTS - 1, (s + SLOTS - 1) % SLOTS)
                        if j is not None and s == 0:
                            wait(dve, flushed[3], g)
                            node_3(j, 0)
                sweep(dve, body)
                fast_flush(3, NG - 1, SLOTS - 1)
                for j in TAIL_BLOCKS:
                    wait(dve, flushed[3], NG)
                    diagonal(j)
                    node_3(j, 0)
                    node_3(j, 1)

            def general_path():
                for c in (1, 2, 3):
                    if c != 1:
                        for s in range(SLOTS):
                            stage_indices(c, s, s)

                    def body(i, j):
                        for s in range(SLOTS):
                            g = SLOTS * i + s
                            if c == 3:
                                message(i, s)
                            general_windows(c, g, s)
                            if not (isinstance(i, int) and i == ITERS - 1):
                                stage_indices(c, g + SLOTS, s)
                    sweep(dve, body)
                    dve.wait_ge(flushed[c], NG * NW)

                    def body(j):
                        if c == 3:
                            diagonal(j)
                        for part in range(2 if c == 3 else 3):
                            if c == 3:
                                node_3(j, part)
                            else:
                                (node_1, node_2)[c - 1](j, j, part)
                    all_blocks(dve, body)
                    if c < 3:
                        dve.wait_ge(acc_reset[c], NB)

            for s in range(SLOTS):
                stage_indices(1, s, s)
            dve.wait_ge(angle_ready, 1)
            vec.tensor_scalar(cutoff[:], angle[:], CUTOFF, 0.5, ALU.is_lt, ALU.mult)
            link(vec.tensor_scalar(angle[:], angle[:], 0.5 / CUTOFF, None, ALU.mult))
            link(vec.tensor_scalar(turns[:], angle[:], ROUND, ROUND, ALU.add, ALU.subtract))
            link(vec.tensor_tensor(angle[:], angle[:], turns[:], ALU.subtract))
            vec.scalar_tensor_tensor(out=angle[:], in0=angle[:], scalar=-1.0, in1=angle[:],
                                     op0=ALU.mult, op1=ALU.max).then_inc(angle_ready, 1)
            dve.wait_ge(sin_ready, 1)
            link(vec.scalar_tensor_tensor(out=cutoff[:], in0=angle[:], scalar=1.0, in1=cutoff[:],
                                          op0=ALU.add, op1=ALU.mult))
            dve.sem_inc(cutoff_ready, 1)
            dve.wait_ge(params_loaded, 16 * 16)
            for m in range(HM):
                last = vec.tensor_scalar(b1_cols[:, m, :], ones[:], b1_col[:, m:m + 1], None, ALU.mult)
            last.then_inc(b1_ready, 1)
            dve.wait_ge(W12_ready, 1)
            dve.wait_ge(start_ready, -(-NB // 4))
            branch(dve, fast_path, general_path)

        @block.tensor
        def _(pe):
            mm, turn = nc.tensor.matmul, nc.tensor.transpose

            pe.wait_ge(consts_ready, 2)
            pe.wait_ge(pool_consts, 3)

            def turn_indices(tile, ps, semaphore):
                for t in range(2):
                    for k in range(CHUNKS):
                        last = turn(ps[:, t, k * HALF:(k + 1) * HALF],
                                    tile[:, t, :].rearrange("g (p k) -> g k p", k=CHUNKS)[:, k, :],
                                    ident[0:HALF, 0:HALF])
                    last.then_inc(semaphore, 1)

            pe.wait_ge(dst_f_ready, 1)
            turn_indices(dst_f, ps_agg, dst_T_ready)
            pe.wait_ge(tests_ready, 1)
            mm(ps_edge_T[:, 0:TESTS], ones[0:HALF, :], tests[:], start=True, stop=True).then_inc(totals_ready, 1)
            pe.wait_ge(rel_ready, 1)
            for t in range(2):
                last = mm(ps_hidden[0:1, t * HALF:(t + 1) * HALF], base[:, t:t + 1],
                          ident[0:HALF, 0:HALF], start=True, stop=True)
            for t in range(2):
                last = mm(ps_hidden[0:1, NG + t * DENSE:NG + (t + 1) * DENSE], chunk_base[:, t:t + 1],
                          ident[0:DENSE, 0:DENSE], start=True, stop=True)
            last.then_inc(base_rows_ready, 1)
            pe.wait_ge(dense_ready, 1)
            n = 2 * DENSE
            for t in range(2):
                for tile, at in ((dense_lo, 512 - 2 * n), (dense_code, 512 - n)):
                    last = turn(ps_edge_T[:, at + t * DENSE:at + (t + 1) * DENSE], tile[:, t, :],
                                ident[0:DENSE, 0:DENSE])
            last.then_inc(dense_T_ready, 1)
            turn_indices(rel_f, ps_filter, rel_T_ready)
            pe.wait_ge(src_f_ready, 1)
            turn_indices(src_f, ps_node, src_T_ready)
            pe.wait_ge(weight_loaded, 48)
            pe.wait_ge(dst_T_copied, 1)
            turn_indices(weight_raw, ps_agg, weight_T_ready)

            pe.wait_ge(flag_ready, 1)

            def hist_batch(b, slot, first, final):
                wait(pe, hist_onehot, b + 1)
                for k in range(BATCH):
                    last = mm(ps_hidden[:, 0:NB], hist_lo[:, slot, :, k], hist_hi[:, slot, :, k],
                              start=(first and k == 0), stop=(final and k == BATCH - 1),
                              skip_group_check=True)
                last.then_inc(hist_summed, 1)

            for slot in range(2):
                hist_batch(slot, slot, slot == 0, False)
            with pe.Fori(1, ITERS // 2 - 1) as i:
                for slot in range(2):
                    hist_batch(2 * i + slot, slot, False, False)
            for slot in range(2):
                hist_batch(ITERS - 2 + slot, slot, False, slot == 1)

            pe.wait_ge(indices_ready, 2)
            n = NB // PARTS
            for b in range(NB):
                if b % n == 0:
                    pe.wait_ge(table_ready, b // n + 1)
                q = b // 4
                if b % 4 == 0 and q >= 4:
                    pe.wait_ge(start_ready, q - 3)
                last = turn(start_bank(q)[:, b % 4 * P:(b % 4 + 1) * P], z_nodes[:, b, :], ident[:])
                if b % 4 == 3 or b == NB - 1:
                    last.then_inc(table_turned, 1)
            pe.wait_ge(start_ready, -(-NB // 4))
            pe.wait_ge(angle_ready, 1)
            pe.wait_ge(params_loaded, 16 * 16)
            for m in range(HM):
                last = turn(ps_agg[:, 0, m * P:(m + 1) * P], W1_sb[:, m * P:(m + 1) * P], ident[:])
            last.then_inc(W1_turned, 1)
            pe.wait_ge(W1_T_ready, 1)
            pe.wait_ge(b1_ready, 1)
            for ps, left in ((ps_agg[:, 1, 0:F], W1_T), (ps_agg[:, 1, F:2 * F], b1_cols)):
                for m in range(HM):
                    last = mm(ps, left[:, m, :], W2_sb[:, m, :], start=(m == 0), stop=(m == HM - 1))
            last.then_inc(W12_done, 1)
            pe.wait_ge(W12_ready, 1)

            def sum_window(c, n, s):
                wait(pe, onehot_ready[c], n + 1)
                for k in range(CHUNKS):
                    last = mm(ps_agg[:, s % 2, 0:WINDOW], ring[:, s, k, :],
                              onehot[:, s % 2, k, :], start=(k == 0), stop=(k == CHUNKS - 1))
                last.then_inc(summed[c], 1)

            def edge_turn(g, s, i):
                wait(pe, edge_loaded[s], 16 * (i + 1))
                wait(pe, edge_T_ready, g)
                hold(pe)
                for k in range(CHUNKS):
                    last = turn(ps_edge_T[0:R, k * P:(k + 1) * P], edge_in[:, s, k, :], ident[:])
                last.then_inc(edge_turned, 1)

            def edge_hidden(g, slot):
                wait(pe, hidden_ready, g)
                wait(pe, edge_T_ready, g + 1)
                mm(ps_hidden[:, :], mlp_w1_sb[:], edge_T[:, slot, :], start=True, stop=True
                   ).then_inc(hidden_done, 1)

            def edge_filter(g, slot):
                wait(pe, message_ready, g - 1)
                mm(ps_filter[:, slot, :], ones[0:1, :], mlp_b2_row[:].rearrange("a k f -> a (k f)"),
                   start=True, stop=False)
                wait(pe, hidden_ready, g + 1)
                for k in range(CHUNKS):
                    last = mm(ps_filter[:, slot, k * P:(k + 1) * P], hidden_T[:, slot, k, :],
                              mlp_w2_sb[:], start=False, stop=(k == CHUNKS - 1))
                last.then_inc(filter_ready, 1)

            def node_1(n, part, b=0):
                bank0, bank1 = node_banks(b)
                if part == 0:
                    wait(pe, z_ready[1], n + 1)
                    mm(bank0[:, 0:F], z_T[:, b, :], W12[:], start=True, stop=True).then_inc(y_done, 1)
                if part == 1:
                    wait(pe, row_ready[1], n + 1)
                    turn(bank1[:, 0:P], row_out[:, b, :], ident[:]).then_inc(y_T_done, 1)

            def node_2(n, part, b=0):
                bank0, bank1 = node_banks(b)
                if part == 0:
                    wait(pe, z_ready[2], n + 1)
                    wait(pe, row_ready[2], n - b)
                    turn(bank0[:, 0:P], z_T[:, b, :], ident[:]).then_inc(turned, 1)
                if part == 1:
                    wait(pe, z_row_ready, n + 1)
                    turn(bank1[:, 0:P], z_row[:, b, :], ident[:]).then_inc(z_turned, 1)
                if part == 2:
                    wait(pe, h2_ready, n + 1)
                    mm(bank0[:, 0:F], h2_T[:, b, :], lin1_sb[:], start=True, stop=True).then_inc(xf_done, 1)

            def scales(j):
                wait(pe, diag_ready, j + 1)
                wait(pe, row_ready[3], j)
                mm(ps_node[:, 1, P:2 * P], ones[:], scale_diag[:], start=True, stop=True
                   ).then_inc(scale_done, 1)

            def node_3(j, part):
                if part == 0:
                    wait(pe, z_ready[3], j + 1)
                    mm(ps_node[:, 0, 0:P], lin2_sb[:], z_T[:, 0, :], start=True, stop=True).then_inc(u_done, 1)
                if part == 1:
                    wait(pe, u_ready, j + 1)
                    wait(pe, row_ready[3], j)
                    mm(ps_node[:, 1, 0:F], z_row[:, 0, :], lin_sb[:], start=True, stop=True).then_inc(v_done, 1)

            def count_chunk(done, q, slot, each):
                wait(pe, chunk_onehot, done + 1)
                wait(pe, chunk_added, 2 * (done - (each - 1)))
                n = HI_SPLIT * SPAN
                bank0, bank1 = count_banks(slot, each)
                mm(bank0[:, 0:n], lo_onehot[:, slot, :], code_onehot[:, slot, 0:n],
                   start=True, stop=True)
                mm(bank1[:, 0:NB * SPAN - n], lo_onehot[:, slot, :], code_onehot[:, slot, n:],
                   start=True, stop=True).then_inc(chunk_summed, 1)

            def dense_product(c, k, done, slot, loads):
                wait(pe, parts_ready[c], 4 * (done + 1))
                first, last = (isinstance(k, int) and k == 0), final_block(k)
                for part in range(3):
                    for h, ps in ((0, ps_edge_T), (1, ps_hidden)):
                        product = mm(ps[:, 0:COLS // 2], table_parts[:, slot, part, :],
                                     adjacency[:, bass.ds(k, 1), h * COLS // 2:(h + 1) * COLS // 2]
                                     .rearrange("p a n -> p (a n)"),
                                     start=(first and part == 0), stop=(last and part == 2),
                                     skip_group_check=True)
                product.then_inc(block_used[c], 1)

            def final_block(k):
                return isinstance(k, int) and k == NB - 1

            def fast_path():
                for c in (1, 2):
                    def body(i, updates, tasks):
                        def update(part):
                            for n, j, b in updates:
                                (node_1, node_2)[c - 1](n, part, b)

                        for s in range(SLOTS):
                            g = SLOTS * i + s
                            if s == 3 and c == 1:
                                update(1)
                            wait(pe, gathered[c][s], 16 * CHUNKS * (i + 1))
                            wait(pe, flushed[c], g - 1)
                            sum_window(c, g, s)
                            if s == 1:
                                update(0)
                            if s == 3 and c == 2:
                                update(1)
                                update(2)
                            for chunk in made_chunks(tasks, i, s, behind=1):
                                count_chunk(*chunk)
                            for name, start, matrix, product in find(tasks, "multiply first"):
                                if s == SLOTS - 1:
                                    pe.wait_ge(chunk_added, 2 * DENSE * (matrix + 1))
                            for table_block in multiplied_blocks(tasks, i, s):
                                dense_product(c, *table_block)
                    gcn_sweep(c, pe, body)
                    for part in range(c + 1):
                        for n, j, b in GCN_TAIL:
                            (node_1, node_2)[c - 1](n, part, b)

                edge_turn(0, 0, 0)
                edge_turn(1, 1, 0)
                edge_hidden(0, 0)
                pe.wait_ge(flushed[2], SLOTS * GCN_ITERS)
                for _ in range(WARM_UP):
                    mm(ps_agg[:, 1, 0:COLS // 2], table_parts[:, 0, 0, :], adjacency[:, 0, 0:COLS // 2],
                       start=True, stop=True)

                def body(i, j):
                    for s in range(SLOTS):
                        g = SLOTS * i + s
                        if not (isinstance(g, int) and g + 2 >= NG):
                            edge_turn(g + 2, (s + 2) % SLOTS, i + (s + 2) // SLOTS)
                        if not (isinstance(g, int) and g + 1 >= NG):
                            edge_hidden(g + 1, (s + 1) % 2)
                        edge_filter(g, s % 2)
                        if not (isinstance(g, int) and g == 0):
                            wait(pe, message_ready, g)
                            wait(pe, flushed[3], g - 2)
                            sum_window(3, g - 1, (s - 1) % SLOTS)
                        if j is not None and s == 0:
                            scales(j)
                        if j is not None and s in (1, 2):
                            node_3(j, s - 1)
                sweep(pe, body)
                wait(pe, message_ready, NG)
                wait(pe, flushed[3], NG - 2)
                sum_window(3, NG - 1, SLOTS - 1)
                for j in TAIL_BLOCKS:
                    scales(j)
                    node_3(j, 0)
                    node_3(j, 1)

            def general_windows(c, g, s):
                with pe.Fori(0, NW) as w:
                    sum_window(c, g * NW + w, s)

            def general_path():
                for c in (1, 2, 3):
                    def body(i, j):
                        for s in range(SLOTS):
                            g = SLOTS * i + s
                            if c == 3:
                                edge_turn(g, s, i)
                                edge_hidden(g, s % 2)
                                edge_filter(g, s % 2)
                                wait(pe, message_ready, g + 1)
                            else:
                                wait(pe, gathered[c][s], 16 * CHUNKS * (i + 1))
                            hold(pe)
                            general_windows(c, g, s)
                    sweep(pe, body)

                    def body(j):
                        if c == 3:
                            scales(j)
                        for part in range((2, 3, 2)[c - 1]):
                            (node_1, node_2, node_3)[c - 1](j, part)
                    all_blocks(pe, body)

            branch(pe, fast_path, general_path)


_INS = ['x', 'src', 'dst', 'edge_attr_64', 'edge_weight', 'L0_gnn_W1', 'L0_gnn_b1', 'L0_gnn_W2', 'L0_gnn_b2',
        'L1_gnn_mlp_w1', 'L1_gnn_mlp_b1', 'L1_gnn_mlp_w2', 'L1_gnn_mlp_b2', 'L1_gnn_lin1_w', 'L1_gnn_lin2_w',
        'L1_gnn_lin2_b', 'L1_gnn_lin_w', 'L1_gnn_lin_b']


def kernel(**inputs):
    import numpy as _np
    import concourse.bacc as _bacc
    from concourse import mybir as _mybir
    from concourse.bass_utils import run_bass_kernel_spmd as _run

    nc = _bacc.Bacc("TRN2", target_bir_lowering=False, num_devices=1)
    arrays, args = {}, []
    for name in _INS:
        a = _np.ascontiguousarray(inputs[name])
        arrays[f"in_{name}_dram"] = a
        args.append(nc.dram_tensor(f"in_{name}_dram", a.shape, _mybir.dt.from_np(a.dtype), kind="ExternalInput").ap())
    shape = tuple(inputs['x'].shape)
    args.append(nc.dram_tensor("out_dram", shape, _mybir.dt.float32, kind="ExternalOutput").ap())
    gnn_kernel(nc, *args)
    r = _run(nc, [arrays], core_ids=[0])
    return r.results[0]["out_dram"]
```
